# Optimizing a Trainium2 kernel written in Bass

```python
import numpy as np
import jax
import jax.numpy as jnp

def _softmax(x, axis=-1):
    return jax.nn.softmax(x, axis=axis)

def _gelu(x):
    return jax.nn.gelu(x, approximate=True)

def _silu(x):
    return jax.nn.silu(x)

def _sigmoid(x):
    return jax.nn.sigmoid(x)

def _layernorm(x, axis=-1, eps=1e-05):
    m = jnp.mean(x, axis=axis, keepdims=True)
    v = jnp.var(x, axis=axis, keepdims=True)
    return (x - m) / jnp.sqrt(v + eps)

def _scatter_add(tgt, idx, src, axis=0):
    return tgt.at[idx].add(src)

def _segment_sum(src, seg, n):
    return jax.ops.segment_sum(src, seg, n)
kernel_name = 'mk_flamingo_gated_d2_seqx_r4_48b796'

def setup_inputs(seed: int=0):
    np.random.seed(seed)
    _w = jnp.asarray

    def _rec_inputs():
        import jax
        import jax.numpy as jnp
        _rk = jax.random.key(seed)
        x = -0.000125 + 0.9999 * jax.random.normal(jax.random.fold_in(_rk, 1), (32, 128, 256), jnp.float32)
        _lenS = 128 - jax.random.randint(jax.random.fold_in(_rk, 7), (32,), 0, max(1, 128 // 4) + 1, jnp.int32)
        _lenS2 = 128 - jax.random.randint(jax.random.fold_in(_rk, 8), (32,), 0, max(1, 128 // 4) + 1, jnp.int32)
        _ctx_1024P = jax.random.normal(jax.random.fold_in(_rk, 11), (32, 16, 256), jnp.float32)
        _ctx_1024c = jax.random.dirichlet(jax.random.fold_in(_rk, 511), 0.3 * jnp.ones((16,), jnp.float32), (32, 128))
        _ctx_1024t = jnp.einsum('bsk,bkd->bsd', _ctx_1024c, _ctx_1024P)
        _ctx_1024t = _ctx_1024t * jax.lax.rsqrt(jnp.mean(jnp.square(_ctx_1024t)) + 1e-12) * 0.953939
        ctx_1024 = -1.52775e-05 + 0.999936 * (_ctx_1024t + 0.3 * jax.random.normal(jax.random.fold_in(_rk, 611), (32, 128, 256), jnp.float32))
        _validS = jnp.arange(128)[None, :] < _lenS[:, None]
        _validS2 = jnp.arange(128)[None, :] < _lenS2[:, None]
        _causal = jnp.tril(jnp.ones((128, 128), dtype=bool))
        mask_1x1xSxS2_bk0 = jnp.logical_not(jnp.broadcast_to(_validS2[0:1, None, None, :], (1, 1, 128, 128)))
        _g = jax.random.normal(jax.random.fold_in(_rk, 9001), (2, 2), jnp.float32)
        _g = jnp.sign(_g) * jnp.maximum(jnp.abs(_g), 1.0) + (_g == 0) * 1.0
        g_xattn = _g[0]
        g_ffn = _g[1]
        return (x, ctx_1024, mask_1x1xSxS2_bk0, g_xattn, g_ffn)
    x, ctx_1024, mask_1x1xSxS2_bk0, g_xattn, g_ffn = _rec_inputs()

    def _L0_xattn_setup():
        import jax, jax.numpy as jnp
        import numpy as np
        G = 8
        SCALE = 0.125
        RESID = 1.0
        EPS = 1e-05
        key = jax.random.key(seed)
        ks = jax.random.split(key, 9)
        B, C, D = (64, 128, 256)
        s = 0.02
        return {'inp_q': jax.random.normal(ks[0], (B, C, D), jnp.float32), 'inp_k': jax.random.normal(ks[1], (B, C, D), jnp.float32), 'inp_v': jax.random.normal(ks[2], (B, C, D), jnp.float32), 'Wt': jax.random.normal(ks[3], (C, C), jnp.float32) * s, 'Wp': jax.random.normal(ks[4], (C, C), jnp.float32) * s, 'Wg': jax.random.normal(ks[5], (C, C), jnp.float32) * s, 'Wz': jax.random.normal(ks[6], (G, C // G, C // G), jnp.float32) * s, 'gamma': jax.random.normal(ks[7], (C,), jnp.float32), 'beta': jax.random.normal(ks[8], (C,), jnp.float32)}
    _L0_xattn_all = _L0_xattn_setup()
    _L0_xattn_in = {k: v for k, v in _L0_xattn_all.items() if k in ('Wt', 'Wp', 'Wg', 'Wz', 'gamma', 'beta')}
    del _L0_xattn_all

    def _L0_ffn_setup():
        import jax, jax.numpy as jnp
        import numpy as np
        NUM_GROUPS = 2
        EXPERT_CAPACITY = 160
        NUM_SELECTED = 2
        key = jax.random.key(seed)
        k1, k2, k3, k4 = jax.random.split(key, 4)
        B, S, H, E, F = (4, 512, 256, 8, 1024)
        return {'input_emb': jax.random.normal(k1, (B, S, H), dtype=jnp.float32), 'w_router': jax.random.normal(k2, (H, E), dtype=jnp.float32) * 0.02, 'wi': jax.random.normal(k3, (E, H, F), dtype=jnp.float32) * 0.02, 'wo': jax.random.normal(k4, (E, F, H), dtype=jnp.float32) * 0.02}
    _L0_ffn_all = _L0_ffn_setup()
    _L0_ffn_in = {k: v for k, v in _L0_ffn_all.items() if k in ('w_router', 'wi', 'wo')}
    del _L0_ffn_all

    def _L1_xattn_setup():
        import jax, jax.numpy as jnp
        import numpy as np
        B, S, E, H, D = (4, 512, 256, 16, 64)
        NUM_BUCKETS, MAX_DISTANCE = (32, 128)

        def _relative_position_bucket(relative_position, num_buckets, max_distance):
            max_exact = num_buckets // 2
            max_distance = max(max_distance, max_exact + 1)
            distance = jnp.maximum(-relative_position, 0)
            is_small = distance < max_exact
            safe_distance = jnp.maximum(distance, 1)
            log_scale = jnp.log(safe_distance / max_exact) / jnp.log(max_distance / max_exact)
            large_bucket = max_exact + (log_scale * (num_buckets - max_exact)).astype(jnp.int32)
            large_bucket = jnp.minimum(large_bucket, num_buckets - 1)
            return jnp.where(is_small, distance, large_bucket)
        key = jax.random.key(seed)
        ks = jax.random.split(key, 7)
        w_scale = 1.0 / np.sqrt(E)
        inputs_q = jax.random.normal(ks[0], (B, S, E), jnp.float32)
        inputs_kv = jax.random.normal(ks[1], (B, S, E), jnp.float32)
        Wq = jax.random.normal(ks[2], (E, H * D), jnp.float32) * w_scale
        Wk = jax.random.normal(ks[3], (E, H * D), jnp.float32) * w_scale
        Wv = jax.random.normal(ks[4], (E, H * D), jnp.float32) * w_scale
        Wo = jax.random.normal(ks[5], (H * D, E), jnp.float32) * (1.0 / np.sqrt(H * D))
        rel_bias = jax.random.normal(ks[6], (H, NUM_BUCKETS), jnp.float32) * 0.02
        mask = jnp.tril(jnp.ones((S, S), dtype=bool))[None, None]
        return {'inputs_q': inputs_q, 'inputs_kv': inputs_kv, 'mask': mask, 'Wq': Wq, 'Wk': Wk, 'Wv': Wv, 'Wo': Wo, 'rel_bias': rel_bias}
    _L1_xattn_all = _L1_xattn_setup()
    _L1_xattn_in = {k: v for k, v in _L1_xattn_all.items() if k in ('Wq', 'Wk', 'Wv', 'Wo', 'rel_bias')}
    del _L1_xattn_all

    def _L1_ffn_setup():
        import jax, jax.numpy as jnp
        import numpy as np
        HIDDEN = 256
        INTER = 128
        N_EXPERTS = 16
        N_GROUP = 4
        TOPK_GROUP = 2
        TOP_K = 4
        SCALING = 2.5

        def _gate(x_flat, gate_w, e_bias):
            logits = x_flat @ gate_w.T
            scores = jax.nn.sigmoid(logits)
            scores_for_choice = scores + e_bias[None, :]
            T = x_flat.shape[0]
            per_group = N_EXPERTS // N_GROUP
            grouped = scores_for_choice.reshape(T, N_GROUP, per_group)
            top2, _ = jax.lax.top_k(grouped, 2)
            group_scores = top2.sum(-1)
            _, group_idx = jax.lax.top_k(group_scores, TOPK_GROUP)
            group_mask = jax.nn.one_hot(group_idx, N_GROUP, dtype=jnp.float32).sum(1) > 0
            score_mask = jnp.repeat(group_mask, per_group, axis=-1)
            tmp_scores = jnp.where(score_mask, scores_for_choice, 0.0)
            _, topk_idx = jax.lax.top_k(tmp_scores, TOP_K)
            topk_weight = jnp.take_along_axis(scores, topk_idx, axis=1)
            topk_weight = topk_weight / (topk_weight.sum(-1, keepdims=True) + 1e-20)
            topk_weight = topk_weight * SCALING
            return (topk_idx, topk_weight)
        key = jax.random.key(seed)
        ks = jax.random.split(key, 8)
        B, S = (2, 512)
        hidden_states = jax.random.normal(ks[0], (B, S, HIDDEN), dtype=jnp.float32)
        gate_w = jax.random.normal(ks[1], (N_EXPERTS, HIDDEN), dtype=jnp.float32) * 0.02
        e_bias = jnp.zeros((N_EXPERTS,), dtype=jnp.float32)
        gate_proj = jax.random.normal(ks[2], (N_EXPERTS, INTER, HIDDEN), dtype=jnp.float32) * 0.02
        up_proj = jax.random.normal(ks[3], (N_EXPERTS, INTER, HIDDEN), dtype=jnp.float32) * 0.02
        down_proj = jax.random.normal(ks[4], (N_EXPERTS, HIDDEN, INTER), dtype=jnp.float32) * 0.02
        shared_gate_w = jax.random.normal(ks[5], (INTER, HIDDEN), dtype=jnp.float32) * 0.02
        shared_up_w = jax.random.normal(ks[6], (INTER, HIDDEN), dtype=jnp.float32) * 0.02
        shared_down_w = jax.random.normal(ks[7], (HIDDEN, INTER), dtype=jnp.float32) * 0.02
        return {'hidden_states': hidden_states, 'gate_w': gate_w, 'e_bias': e_bias, 'gate_proj': gate_proj, 'up_proj': up_proj, 'down_proj': down_proj, 'shared_gate_w': shared_gate_w, 'shared_up_w': shared_up_w, 'shared_down_w': shared_down_w}
    _L1_ffn_all = _L1_ffn_setup()
    _L1_ffn_in = {k: v for k, v in _L1_ffn_all.items() if k in ('gate_w', 'e_bias', 'gate_proj', 'up_proj', 'down_proj', 'shared_gate_w', 'shared_up_w', 'shared_down_w')}
    del _L1_ffn_all
    return {'x': x, 'ctx_1024': ctx_1024, 'mask_1x1xSxS2_bk0': mask_1x1xSxS2_bk0, 'g_xattn': g_xattn, 'g_ffn': g_ffn, 'L0_xattn_Wt': _L0_xattn_in['Wt'], 'L0_xattn_Wp': _L0_xattn_in['Wp'], 'L0_xattn_Wg': _L0_xattn_in['Wg'], 'L0_xattn_Wz': _L0_xattn_in['Wz'], 'L0_xattn_gamma': _L0_xattn_in['gamma'], 'L0_xattn_beta': _L0_xattn_in['beta'], 'L0_ffn_w_router': _L0_ffn_in['w_router'], 'L0_ffn_wi': _L0_ffn_in['wi'], 'L0_ffn_wo': _L0_ffn_in['wo'], 'L1_xattn_Wq': _L1_xattn_in['Wq'], 'L1_xattn_Wk': _L1_xattn_in['Wk'], 'L1_xattn_Wv': _L1_xattn_in['Wv'], 'L1_xattn_Wo': _L1_xattn_in['Wo'], 'L1_xattn_rel_bias': _L1_xattn_in['rel_bias'], 'L1_ffn_gate_w': _L1_ffn_in['gate_w'], 'L1_ffn_e_bias': _L1_ffn_in['e_bias'], 'L1_ffn_gate_proj': _L1_ffn_in['gate_proj'], 'L1_ffn_up_proj': _L1_ffn_in['up_proj'], 'L1_ffn_down_proj': _L1_ffn_in['down_proj'], 'L1_ffn_shared_gate_w': _L1_ffn_in['shared_gate_w'], 'L1_ffn_shared_up_w': _L1_ffn_in['shared_up_w'], 'L1_ffn_shared_down_w': _L1_ffn_in['shared_down_w']}

def reference(x, ctx_1024, mask_1x1xSxS2_bk0, g_xattn, g_ffn, L0_xattn_Wt, L0_xattn_Wp, L0_xattn_Wg, L0_xattn_Wz, L0_xattn_gamma, L0_xattn_beta, L0_ffn_w_router, L0_ffn_wi, L0_ffn_wo, L1_xattn_Wq, L1_xattn_Wk, L1_xattn_Wv, L1_xattn_Wo, L1_xattn_rel_bias, L1_ffn_gate_w, L1_ffn_e_bias, L1_ffn_gate_proj, L1_ffn_up_proj, L1_ffn_down_proj, L1_ffn_shared_gate_w, L1_ffn_shared_up_w, L1_ffn_shared_down_w):
    import jax
    import jax.numpy as jnp

    def _L0_xattn_ref(inp_q, inp_k, inp_v, Wt, Wp, Wg, Wz, gamma, beta):
        import jax, jax.numpy as jnp
        import numpy as np
        G = 8
        SCALE = 0.125
        RESID = 1.0
        EPS = 1e-05
        b, C, d = inp_v.shape
        cg = C // G
        t = jnp.einsum('oc,bcd->bod', Wt, inp_v)
        p = jnp.einsum('oc,bcd->bod', Wp, inp_q)
        g = jnp.einsum('oc,bcd->bod', Wg, inp_k)
        tg = t.reshape(b, G, cg, d)
        pg = p.reshape(b, G, cg, d)
        gg = g.reshape(b, G, cg, d)
        att = jnp.einsum('bgcd,bgcd->bg', pg, gg) * SCALE
        x = att[:, :, None, None] * tg
        x = jnp.einsum('goc,bgcd->bgod', Wz, x)
        mean = x.mean(axis=(2, 3), keepdims=True)
        var = x.var(axis=(2, 3), keepdims=True)
        xn = (x - mean) / jnp.sqrt(var + EPS)
        xn = xn.reshape(b, C, d) * gamma[None, :, None] + beta[None, :, None]
        return xn + inp_v * RESID

    def _L0_ffn_ref(input_emb, w_router, wi, wo):
        import jax, jax.numpy as jnp
        import numpy as np
        NUM_GROUPS = 2
        EXPERT_CAPACITY = 160
        NUM_SELECTED = 2
        B, S, H = input_emb.shape
        E = w_router.shape[1]
        G = NUM_GROUPS
        T = B * S // G
        C = EXPERT_CAPACITY
        K = NUM_SELECTED
        x = input_emb.reshape(G, T, H)
        router_logits = jnp.einsum('gth,he->gte', x.astype(jnp.float32), w_router.astype(jnp.float32))
        router_probs = jax.nn.softmax(router_logits, axis=-1)
        gate, idx = jax.lax.top_k(router_probs, K)
        mask = jax.nn.one_hot(idx, E, dtype=jnp.float32)
        mask_kt = jnp.swapaxes(mask, 1, 2).reshape(G, K * T, E)
        pos = jnp.cumsum(mask_kt, axis=1) * mask_kt - 1.0
        pos = jnp.swapaxes(pos.reshape(G, K, T, E), 1, 2)
        disp_k = jax.nn.one_hot(pos, C, dtype=jnp.float32) * mask[..., None]
        dispatch = disp_k.sum(axis=2)
        combine = jnp.einsum('gtk,gtkec->gtec', gate, disp_k)
        expert_in = jnp.einsum('gtec,gth->egch', dispatch, x)
        h = jax.nn.relu(jnp.einsum('egch,ehf->egcf', expert_in, wi))
        expert_out = jnp.einsum('egcf,efh->egch', h, wo)
        y = jnp.einsum('gtec,egch->gth', combine, expert_out)
        return y.reshape(B, S, H)

    def _L1_xattn_ref(inputs_q, inputs_kv, mask, Wq, Wk, Wv, Wo, rel_bias):
        import jax, jax.numpy as jnp
        import numpy as np
        B, S, E, H, D = (4, 512, 256, 16, 64)
        NUM_BUCKETS, MAX_DISTANCE = (32, 128)

        def _relative_position_bucket(relative_position, num_buckets, max_distance):
            max_exact = num_buckets // 2
            max_distance = max(max_distance, max_exact + 1)
            distance = jnp.maximum(-relative_position, 0)
            is_small = distance < max_exact
            safe_distance = jnp.maximum(distance, 1)
            log_scale = jnp.log(safe_distance / max_exact) / jnp.log(max_distance / max_exact)
            large_bucket = max_exact + (log_scale * (num_buckets - max_exact)).astype(jnp.int32)
            large_bucket = jnp.minimum(large_bucket, num_buckets - 1)
            return jnp.where(is_small, distance, large_bucket)
        batch, q_len, embed = inputs_q.shape
        k_len = inputs_kv.shape[1]
        q = (inputs_q @ Wq).reshape(batch, q_len, H, D)
        k = (inputs_kv @ Wk).reshape(batch, k_len, H, D)
        v = (inputs_kv @ Wv).reshape(batch, k_len, H, D)
        attention = jnp.einsum('bqhd,bkhd->bhqk', q, k) * (1.0 / jnp.sqrt(D))
        rel_pos = jnp.arange(k_len, dtype=jnp.int32)[None, :] - jnp.arange(q_len, dtype=jnp.int32)[:, None]
        bucket = _relative_position_bucket(rel_pos, NUM_BUCKETS, MAX_DISTANCE)
        attention = attention + jnp.take(rel_bias, bucket, axis=1)[None]
        attention = jnp.where(mask, attention, jnp.finfo(jnp.float32).min)
        normalized = jax.nn.softmax(attention, axis=-1)
        output = jnp.einsum('bhqk,bkhd->bqhd', normalized, v).reshape(batch, q_len, H * D)
        return output @ Wo

    def _L1_ffn_ref(hidden_states, gate_w, e_bias, gate_proj, up_proj, down_proj, shared_gate_w, shared_up_w, shared_down_w):
        import jax, jax.numpy as jnp
        import numpy as np
        HIDDEN = 256
        INTER = 128
        N_EXPERTS = 16
        N_GROUP = 4
        TOPK_GROUP = 2
        TOP_K = 4
        SCALING = 2.5

        def _gate(x_flat, gate_w, e_bias):
            logits = x_flat @ gate_w.T
            scores = jax.nn.sigmoid(logits)
            scores_for_choice = scores + e_bias[None, :]
            T = x_flat.shape[0]
            per_group = N_EXPERTS // N_GROUP
            grouped = scores_for_choice.reshape(T, N_GROUP, per_group)
            top2, _ = jax.lax.top_k(grouped, 2)
            group_scores = top2.sum(-1)
            _, group_idx = jax.lax.top_k(group_scores, TOPK_GROUP)
            group_mask = jax.nn.one_hot(group_idx, N_GROUP, dtype=jnp.float32).sum(1) > 0
            score_mask = jnp.repeat(group_mask, per_group, axis=-1)
            tmp_scores = jnp.where(score_mask, scores_for_choice, 0.0)
            _, topk_idx = jax.lax.top_k(tmp_scores, TOP_K)
            topk_weight = jnp.take_along_axis(scores, topk_idx, axis=1)
            topk_weight = topk_weight / (topk_weight.sum(-1, keepdims=True) + 1e-20)
            topk_weight = topk_weight * SCALING
            return (topk_idx, topk_weight)
        B, S, H = hidden_states.shape
        x = hidden_states.reshape(-1, H)
        T = x.shape[0]
        topk_idx, topk_weight = _gate(x, gate_w, e_bias)
        g = jnp.einsum('th,eih->eti', x, gate_proj)
        u = jnp.einsum('th,eih->eti', x, up_proj)
        inter = jax.nn.silu(g) * u
        expert_out = jnp.einsum('eti,ehi->eth', inter, down_proj)
        sel = expert_out[topk_idx, jnp.arange(T)[:, None]]
        y = jnp.einsum('tkh,tk->th', sel, topk_weight)
        y = y.reshape(B, S, H)
        sg = hidden_states @ shared_gate_w.T
        su = hidden_states @ shared_up_w.T
        shared_out = jax.nn.silu(sg) * su @ shared_down_w.T
        return y + shared_out
    x = x + jnp.tanh(g_xattn[0]) * _L0_xattn_ref(_layernorm(x, axis=-1), ctx_1024, ctx_1024, L0_xattn_Wt, L0_xattn_Wp, L0_xattn_Wg, L0_xattn_Wz, L0_xattn_gamma, L0_xattn_beta)
    x = x + jnp.tanh(g_ffn[0]) * _L0_ffn_ref(_layernorm(x, axis=-1), L0_ffn_w_router, L0_ffn_wi, L0_ffn_wo)
    x = x + jnp.tanh(g_xattn[1]) * _L1_xattn_ref(_layernorm(x, axis=-1), ctx_1024, mask_1x1xSxS2_bk0, L1_xattn_Wq, L1_xattn_Wk, L1_xattn_Wv, L1_xattn_Wo, L1_xattn_rel_bias)
    x = x + jnp.tanh(g_ffn[1]) * _L1_ffn_ref(_layernorm(x, axis=-1), L1_ffn_gate_w, L1_ffn_e_bias, L1_ffn_gate_proj, L1_ffn_up_proj, L1_ffn_down_proj, L1_ffn_shared_gate_w, L1_ffn_shared_up_w, L1_ffn_shared_down_w)
    return x

_drawn_inputs = setup_inputs


def setup_inputs(seed=0):
    import zlib

    import numpy as np

    out = dict(_drawn_inputs(seed))
    spreads = {'g_ffn': (-1.0, 0.6), 'L1_ffn_e_bias': (0.0, 0.8)}
    factors = {'L0_ffn_w_router': 5.976,
     'L0_ffn_wi': 6.722,
     'L0_ffn_wo': 5.588,
     'L1_ffn_gate_w': 8.0,
     'L1_ffn_gate_proj': 7.633,
     'L1_ffn_up_proj': 7.54,
     'L1_ffn_down_proj': 7.549,
     'L1_ffn_shared_gate_w': 8.0,
     'L1_ffn_shared_up_w': 8.0,
     'L1_ffn_shared_down_w': 8.0}
    for name, (base, spread) in spreads.items():
        noise = np.random.default_rng([zlib.crc32(name.encode()), seed]).standard_normal(out[name].shape)
        drawn = base * np.exp(spread * noise) if base else spread * noise
        out[name] = jnp.asarray(drawn.astype(out[name].dtype))
    for name, factor in factors.items():
        out[name] = (out[name] * factor).astype(out[name].dtype)
    return out
```

```python
from contextlib import ExitStack

import numpy as np
import concourse.bass as bass
from concourse import mybir

F32 = mybir.dt.float32
F32R = mybir.dt.float32r
BF16 = mybir.dt.bfloat16
I32 = mybir.dt.int32
ALU = mybir.AluOpType
ACT = mybir.ActivationFunctionType
AX = mybir.AxisListType

P = 128
B, S, D = 32, 128, 256
KD = D // P
EPS = 1e-5
LOWEST = -3.4028234663852886e38

GROUPS, GROUP = 8, 16
E0, F0, CAP = 8, 1024, 160
HALVES = 2
TILES = B // HALVES
SLOTS = 80
PARTS = HALVES * (CAP // SLOTS)
DUMMY = B * S
ROWS = B * S + P
HEADS, DH = 16, 64
PAIRS = HEADS // 2
E1, I1, TOP = 16, 128, 4


class Chain:

    def __init__(self, eng, sem, length):
        self.eng, self.sem, self.length, self.count, self.base = eng, sem, length, 0, 0

    def start(self, step):
        self.base, self.count = step * self.length, 0

    def __call__(self, ins):
        self.count += 1
        ins.then_inc(self.sem, 1)
        self.eng.wait_ge(self.sem, self.base + self.count)

    def end(self):
        assert self.count == self.length, (self.count, self.length)


def rows(t):
    return t.rearrange("p a b -> p (a b)")


def stand(eng, sem):
    eng.sem_inc(sem, 1)


def product(pe, out, weights, moving, first, last):
    (wh, wl), (mh, ml) = weights, moving
    pe.matmul(out, wl, mh, start=first, stop=False)
    pe.matmul(out, wh, ml, start=False, stop=False)
    return pe.matmul(out, wh, mh, start=False, stop=last)


class Space:

    def __init__(self, nc, ctx, tag):
        self.nc, self.ctx, self.tag = nc, ctx, tag

    def sb(self, name, shape, dt=F32):
        return self.ctx.enter_context(self.nc.sbuf_tensor(f"{self.tag}_{name}", shape, dt))

    def ps(self, name, shape, dt=F32):
        return self.ctx.enter_context(self.nc.psum_tensor(f"{self.tag}_{name}", shape, dt))

    def sem(self, name):
        return self.ctx.enter_context(self.nc.semaphore(f"{self.tag}_{name}"))


def setup(nc, A, C):
    with ExitStack() as ctx:
        m = Space(nc, ctx, "setup")
        made, gates_in, gates_up, zeroed = (m.sem(n) for n in ("made", "gates_in", "gates_up", "zeroed"))
        graw = m.sb("graw", [P, 4])
        block = ctx.enter_context(nc.Block())

        @block.sync
        def _(sp):
            sp.dma_start(graw[:, 0:2], A["g_xattn"].rearrange("(a n) -> a n", a=1).to_broadcast((P, 2))).then_inc(gates_in, 16)
            sp.dma_start(graw[:, 2:4], A["g_ffn"].rearrange("(a n) -> a n", a=1).to_broadcast((P, 2))).then_inc(gates_in, 16)
            sp.wait_ge(gates_in, 32)

        @block.scalar
        def _(act):
            act.wait_ge(gates_in, 32)
            nc.scalar.activation(C["gate"][:], graw[:], ACT.Tanh).then_inc(gates_up, 1)
            act.wait_ge(gates_up, 1)

        @block.vector
        def _(dve):
            nc.vector.memset(C["eps"][:], EPS).then_inc(zeroed, 1)
            dve.wait_ge(zeroed, 1)

        @block.gpsimd
        def _(pool):
            nc.gpsimd.memset(C["ident"][:], 0.0)
            nc.gpsimd.memset(C["ones"][:], 1.0)
            nc.gpsimd.memset(C["tri"][:], 1.0)
            nc.gpsimd.memset(C["gsum"][:], 1.0 / GROUP).then_inc(made, 1)
            pool.wait_ge(made, 1)
            nc.gpsimd.affine_select(out=C["ident"][:], in_=C["ident"][:], compare_op=ALU.not_equal, fill=1.0,
                                    base=0, pattern=[[-1, P]], channel_multiplier=1)
            nc.gpsimd.affine_select(out=C["tri"][:], in_=C["tri"][:], compare_op=ALU.is_ge, fill=0.0,
                                    base=0, pattern=[[1, P]], channel_multiplier=-1)
            g = C["gsum"].rearrange("p (a b) -> p a b", b=GROUP)
            nc.gpsimd.affine_select(out=g, in_=g, compare_op=ALU.is_ge, fill=0.0,
                                    base=0, pattern=[[-GROUP, GROUPS], [0, GROUP]], channel_multiplier=1).then_inc(made, 1)
            pool.wait_ge(made, 2)
            nc.gpsimd.affine_select(out=g, in_=g, compare_op=ALU.is_ge, fill=0.0,
                                    base=GROUP - 1, pattern=[[GROUP, GROUPS], [0, GROUP]], channel_multiplier=-1).then_inc(made, 1)
            pool.wait_ge(made, 3)


def mix(nc, A, C, X2, XN):
    STEPS, NB = B // 4, 4
    W = NB * D
    with ExitStack() as ctx:
        m = Space(nc, ctx, "mix")
        sb, ps, sem = m.sb, m.ps, m.sem
        bdz = sb("bdz", [P, P])
        wt = sb("wt", [P, P])
        wraw = sb("wraw", [P, 3, P])
        wh = sb("wh", [P, 3, P], F32R)
        wl = sb("wl", [P, 3, P], F32R)
        wr = sb("wr", [P, KD, E0])
        gb = sb("gb", [P, 2])
        gbt = sb("gbt", [P, 2])
        xin = sb("xin", [P, 2, NB, D])
        cin = sb("cin", [P, 2, NB, D])
        xnf = sb("xnf", [P, 2, W])
        xh = sb("xh", [P, 2, W], F32R)
        xl = sb("xl", [P, 2, W], F32R)
        ch = sb("ch", [P, 2, W], F32R)
        cl = sb("cl", [P, 2, W], F32R)
        stat = sb("stat", [P, NB, 6])
        mv = sb("mv", [P, 2, NB, 2])
        sd = sb("sd", [P, 2, NB])
        rs = sb("rs", [P, NB])
        gs = sb("gs", [P, W])
        junk = sb("junk", [P, W])
        ustat = sb("ustat", [P, NB, 6])
        umv = sb("umv", [P, NB, 2])
        q = sb("q", [P, 3, NB])
        s3 = sb("s3", [P, 3, NB])
        t1 = sb("t1", [P, NB])
        t2 = sb("t2", [P, NB])
        va = sb("va", [P, NB])
        sdu = sb("sdu", [P, NB])
        ab = sb("ab", [P, 2, NB])
        w = sb("w", [P, W])
        z = sb("z", [P, W])
        x1 = sb("x1", [P, 2, W])
        stat2 = sb("stat2", [P, NB, 6])
        mv2 = sb("mv2", [P, NB, 2])
        sd2 = sb("sd2", [P, NB])
        rs2 = sb("rs2", [P, NB])
        xn = sb("xn", [P, 2, W])
        xt = sb("xt", [P, NB * KD, P])
        zero = sb("zero", [P, D])
        psP, psG, psU = (ps(n, [P, W]) for n in ("psP", "psG", "psU"))
        psS = ps("psS", [P, 512])
        psT = ps("psT", [P, 512])

        w_in, bd_zero, w_up, w2_made, w_split, gbt_up = (sem(n) for n in ("w_in", "bd_zero", "w_up", "w2_made", "w_split", "gbt_up"))
        in_ready = [sem(f"in_ready{p}") for p in range(2)]
        in_free, var1, sd1_ready, xn_ready, hi_ready, lo_ready = (sem(n) for n in ("in_free", "var1", "sd1_ready", "xn_ready", "hi_ready", "lo_ready"))
        g_done, p_done, u_done, gs_ready, p_used, u_used = (sem(n) for n in ("g_done", "p_done", "u_done", "gs_ready", "p_used", "u_used"))
        q_ready, s_ready, va_ready, sdu_ready, ab_ready, w_ready = (sem(n) for n in ("q_ready", "s_ready", "va_ready", "sdu_ready", "ab_ready", "w_ready"))
        x1_ready, var2, sd2_ready, xn2_ready = (sem(n) for n in ("x1_ready", "var2", "sd2_ready", "xn2_ready"))
        lg_copied = sem("lg_copied")
        t_done, t_used, l_done = (sem(n) for n in ("t_done", "t_used", "l_done"))
        stored = [sem(f"stored{p}") for p in range(2)]
        zeros_up, dummies = sem("zeros_up"), sem("dummies")
        s_front, s_back, stood = (sem(n) for n in ("s_front", "s_back", "stood"))
        block = ctx.enter_context(nc.Block())

        x_d = A["x"].rearrange("b p d -> p b d")
        c_d = A["ctx_1024"].rearrange("b p d -> p b d")
        x2_d = X2[0:B * S, :].rearrange("(b p) d -> p b d", p=P)
        xn_d = XN[0:B * S, :].rearrange("(b p) d -> p b d", p=P)

        def over_steps(eng, front, back):
            front(0, 0, 0)
            front(1, 1, 0)
            back(0, 0, 0)
            with eng.Fori(1, STEPS // 2) as h:
                front(h * 2, 0, h)
                back(h * 2 - 1, 1, h - 1)
                front(h * 2 + 1, 1, h)
                back(h * 2, 0, h)
            back(STEPS - 1, 1, STEPS // 2 - 1)

        @block.sync
        def _(sp):
            sp.dma_start(wt[:], A["Wt"]).then_inc(w_in, 16)
            sp.dma_start(wraw[:, 0, :], A["WpT"]).then_inc(w_in, 16)
            sp.dma_start(wraw[:, 1, :], A["WgT"]).then_inc(w_in, 16)
            sp.dma_start(wr[:], A["wr"].rearrange("(k p) e -> p k e", p=P)).then_inc(w_in, 16)
            sp.dma_start(gb[:, 0:1], A["gamma"].rearrange("(p a) -> p a", a=1)).then_inc(w_in, 16)
            sp.dma_start(gb[:, 1:2], A["beta"].rearrange("(p a) -> p a", a=1)).then_inc(w_in, 16)
            sp.wait_ge(bd_zero, 1)
            for g in range(GROUPS):
                r = slice(g * GROUP, (g + 1) * GROUP)
                sp.dma_start(bdz[r, r], A["WzT"][r, :]).then_inc(w_in, 16)

            def front(n, p, h):
                sp.wait_ge(in_free, n + 1)
                sp.dma_start(xin[:, p], x_d[:, bass.ds(n * NB, NB), :]).then_inc(in_ready[p], 16)
                sp.dma_start(cin[:, p], c_d[:, bass.ds(n * NB, NB), :]).then_inc(in_ready[p], 16)

            with sp.Fori(0, STEPS // 2) as h:
                front(h * 2, 0, h)
                front(h * 2 + 1, 1, h)
            sp.wait_ge(zeros_up, 1)
            sp.dma_start(X2[DUMMY:ROWS, :], zero[:]).then_inc(dummies, 16)
            sp.dma_start(XN[DUMMY:ROWS, :], zero[:]).then_inc(dummies, 16)
            sp.wait_ge(dummies, 32)

        @block.gpsimd
        def _(pool):
            nc.gpsimd.memset(zero[:], 0.0).then_inc(zeros_up, 1)
            pool.wait_ge(w_up, 1)
            nc.gpsimd.tensor_tensor(wl[:], wraw[:], wh[:], ALU.subtract).then_inc(w_split, 1)

            def split(n, p, h):
                pool.wait_ge(u_done, n + 1)
                pool.wait_ge(hi_ready, n * 2 + 1)
                nc.gpsimd.tensor_tensor(cl[:, p], cin[:, p].rearrange("p a b -> p (a b)"), ch[:, p], ALU.subtract).then_inc(lo_ready, 1)
                pool.wait_ge(hi_ready, n * 2 + 2)
                nc.gpsimd.tensor_tensor(xl[:, p], xnf[:, p], xh[:, p], ALU.subtract).then_inc(lo_ready, 1)

            with pool.Fori(0, STEPS // 2) as h:
                split(h * 2, 0, h)
                split(h * 2 + 1, 1, h)

        @block.scalar
        def _(act):
            act.wait_ge(w2_made, 1)
            act.wait_ge(w_in, 16 * (6 + GROUPS))
            nc.scalar.activation(wraw[:, 2, :], psS[:, 0:P], ACT.Copy).then_inc(gbt_up, 1)
            act.wait_ge(gbt_up, 1)
            nc.scalar.activation(wh[:], wraw[:], ACT.Copy).then_inc(w_up, 1)
            nc.scalar.activation(gbt[:], gb[:], ACT.Copy, scale=C["gate"][:, 0:1]).then_inc(gbt_up, 1)
            act.sem_inc(gs_ready, 1)
            act.sem_inc(w_ready, 1)
            act.sem_inc(t_used, 1)

            def front(n, p, h):
                act.wait_ge(in_ready[p], h * 32 + 32)
                act.wait_ge(u_done, n + 1)
                nc.scalar.activation(ch[:, p], cin[:, p].rearrange("p a b -> p (a b)"), ACT.Copy).then_inc(hi_ready, 1)
                act.wait_ge(var1, n + 1)
                nc.scalar.activation(sd[:, p], mv[:, p, :, 1], ACT.Sqrt, bias=C["eps"][:]).then_inc(sd1_ready, 1)
                act.wait_ge(xn_ready, n + 1)
                nc.scalar.activation(xh[:, p], xnf[:, p], ACT.Copy).then_inc(hi_ready, 1)

            def back(n, p, h):
                act.wait_ge(g_done, n + 1)
                act.wait_ge(p_used, n + 1)
                nc.scalar.activation(gs[:], psG[:], ACT.Copy).then_inc(gs_ready, 1)
                act.wait_ge(va_ready, n + 1)
                nc.scalar.activation(sdu[:], va[:], ACT.Sqrt, bias=C["eps"][:]).then_inc(sdu_ready, 1)
                act.wait_ge(ab_ready, n + 1)
                for j in range(NB):
                    last = nc.scalar.activation(w[:, j * D:(j + 1) * D], psU[:, j * D:(j + 1) * D], ACT.Identity,
                                                bias=ab[:, 1, j:j + 1], scale=ab[:, 0, j:j + 1])
                last.then_inc(w_ready, 1)
                act.wait_ge(var2, n + 1)
                nc.scalar.activation(sd2[:], mv2[:, :, 1], ACT.Sqrt, bias=C["eps"][:]).then_inc(sd2_ready, 1)
                act.wait_ge(x1_ready, n + 1)
                act.dma_start(x2_d[:, bass.ds(n * NB, NB), :], x1[:, p].rearrange("p (a b) -> p a b", b=D)).then_inc(stored[p], 16)
                for r in range(KD):
                    act.wait_ge(t_done, n * 2 + (r + 1))
                    if r == 0:
                        act.wait_ge(l_done, n + 1)
                    nc.scalar.activation(xt[:, r * NB:(r + 1) * NB, :].rearrange("p a b -> p (a b)"), psT[:], ACT.Copy).then_inc(t_used, 1)
                act.wait_ge(xn2_ready, n + 1)
                act.dma_start(xn_d[:, bass.ds(n * NB, NB), :], xn[:, p].rearrange("p (a b) -> p a b", b=D)).then_inc(stored[p], 16)

            over_steps(act, front, back)
            for p in range(2):
                act.wait_ge(stored[p], 32 * (STEPS // 2) + 16)

        @block.vector
        def _(dve):
            nc.vector.memset(bdz[:], 0.0).then_inc(bd_zero, 1)
            dve.sem_inc(in_free, 2)
            dve.sem_inc(p_used, 1)
            for p in range(2):
                dve.sem_inc(stored[p], 16)
            dve.wait_ge(gbt_up, 2)
            fchain, bchain = Chain(dve, s_front, 2), Chain(dve, s_back, 12)

            def front(n, p, h):
                fchain.start(n)
                dve.wait_ge(in_ready[p], h * 32 + 32)
                for j in range(NB):
                    last = nc.vector.bn_stats(stat[:, j, :], xin[:, p, j, :])
                fchain(last)
                stand(dve, stood)
                for j in range(NB):
                    last = nc.vector.bn_aggr(mv[:, p, j, :], stat[:, j, :])
                last.then_inc(var1, 1)
                dve.wait_ge(sd1_ready, n + 1)
                fchain(nc.vector.reciprocal(rs[:], sd[:, p]))
                for j in range(NB):
                    last = nc.vector.tensor_scalar(xnf[:, p, j * D:(j + 1) * D], xin[:, p, j, :], mv[:, p, j, 0:1],
                                                   rs[:, j:j + 1], ALU.subtract, ALU.mult)
                last.then_inc(xn_ready, 1)
                fchain.end()
                if not isinstance(n, int):
                    logits(n - 2)

            def logits(n):
                dve.wait_ge(l_done, n + 2)
                nc.vector.tensor_copy(C["logits0"][:, bass.ds(n * NB, NB), :],
                                      psS[:, 64:64 + NB * E0].rearrange("p (a b) -> p a b", b=E0)).then_inc(lg_copied, 1)

            def back(n, p, h):
                c = bchain
                c.start(n)
                dve.wait_ge(p_done, n + 1)
                dve.wait_ge(gs_ready, n + 2)
                for j in range(NB):
                    last = nc.vector.tensor_tensor_reduce(junk[:, j * D:(j + 1) * D], psP[:, j * D:(j + 1) * D], gs[:, j * D:(j + 1) * D], 1.0, 0.0,
                                                          ALU.mult, ALU.add, q[:, 0, j:j + 1])
                last.then_inc(p_used, 1)
                dve.wait_ge(u_done, n + 3)
                for j in range(NB):
                    last = nc.vector.bn_stats(ustat[:, j, :], psU[:, j * D:(j + 1) * D])
                c(last)
                stand(dve, stood)
                for j in range(NB):
                    last = nc.vector.bn_aggr(umv[:, j, :], ustat[:, j, :])
                c(last)
                nc.vector.tensor_copy(q[:, 1, :], umv[:, :, 0])
                c(nc.vector.tensor_tensor(t1[:], umv[:, :, 0], umv[:, :, 0], ALU.mult))
                nc.vector.tensor_tensor(q[:, 2, :], umv[:, :, 1], t1[:], ALU.add).then_inc(q_ready, 1)
                dve.wait_ge(s_ready, n + 1)
                c(nc.vector.tensor_copy(s3[:], psS[:, 0:3 * NB].rearrange("p (a b) -> p a b", b=NB)))
                nc.vector.scalar_tensor_tensor(t1[:], s3[:, 0, :], 4.0, s3[:, 0, :], ALU.mult, ALU.mult)
                c(nc.vector.tensor_tensor(t2[:], s3[:, 1, :], s3[:, 1, :], ALU.mult))
                c(nc.vector.tensor_tensor(t2[:], s3[:, 2, :], t2[:], ALU.subtract))
                nc.vector.tensor_tensor(va[:], t1[:], t2[:], ALU.mult).then_inc(va_ready, 1)
                nc.vector.scalar_tensor_tensor(z[:], cin[:, p].rearrange("p a b -> p (a b)"), C["gate"][:, 0:1],
                                               xin[:, p].rearrange("p a b -> p (a b)"), ALU.mult, ALU.add).then_inc(in_free, 1)
                dve.wait_ge(sdu_ready, n + 1)
                c(nc.vector.reciprocal(t1[:], sdu[:]))
                c(nc.vector.scalar_tensor_tensor(t2[:], s3[:, 0, :], 2.0, t1[:], ALU.mult, ALU.mult))
                c(nc.vector.tensor_scalar(ab[:, 0, :], t2[:], gbt[:, 0:1], None, ALU.mult))
                c(nc.vector.tensor_tensor(t1[:], ab[:, 0, :], s3[:, 1, :], ALU.mult))
                nc.vector.tensor_scalar(ab[:, 1, :], t1[:], -1.0, gbt[:, 1:2], ALU.mult, ALU.add).then_inc(ab_ready, 1)
                dve.wait_ge(w_ready, n + 2)
                dve.wait_ge(in_free, n + 3)
                dve.wait_ge(stored[p], h * 32 + 16)
                nc.vector.tensor_tensor(x1[:, p], z[:], w[:], ALU.add).then_inc(x1_ready, 1)
                dve.wait_ge(x1_ready, n + 1)
                for j in range(NB):
                    last = nc.vector.bn_stats(stat2[:, j, :], x1[:, p, j * D:(j + 1) * D])
                c(last)
                stand(dve, stood)
                for j in range(NB):
                    last = nc.vector.bn_aggr(mv2[:, j, :], stat2[:, j, :])
                last.then_inc(var2, 1)
                dve.wait_ge(sd2_ready, n + 1)
                c(nc.vector.reciprocal(rs2[:], sd2[:]))
                for j in range(NB):
                    last = nc.vector.tensor_scalar(xn[:, p, j * D:(j + 1) * D], x1[:, p, j * D:(j + 1) * D], mv2[:, j, 0:1],
                                                   rs2[:, j:j + 1], ALU.subtract, ALU.mult)
                last.then_inc(xn2_ready, 1)
                c.end()

            over_steps(dve, front, back)
            logits(STEPS - 2)
            logits(STEPS - 1)
            dve.wait_ge(lg_copied, STEPS)

        @block.tensor
        def _(pe):
            pe.sem_inc(u_done, 2)
            pe.sem_inc(l_done, 1)
            pe.wait_ge(w_in, 16 * (6 + GROUPS))
            nc.tensor.matmul(psS[:, 0:P], wt[:], bdz[:], start=True, stop=True).then_inc(w2_made, 1)
            pe.wait_ge(w_split, 1)

            def products(n, p, h):
                def into(out, k, high, low, done):
                    for half in range(W // 512):
                        r = slice(half * 512, half * 512 + 512)
                        last = product(pe, out[:, r], (wh[:, k, :], wl[:, k, :]), (high[:, p, r], low[:, p, r]), True, True)
                    last.then_inc(done, 1)

                pe.wait_ge(lo_ready, n * 2 + 1)
                pe.wait_ge(gs_ready, n + 1)
                into(psG, 1, ch, cl, g_done)
                pe.wait_ge(lo_ready, n * 2 + 2)
                pe.wait_ge(p_used, n + 1)
                into(psP, 0, xh, xl, p_done)
                pe.wait_ge(w_ready, n + 1)
                into(psU, 2, ch, cl, u_done)

            def group_sums(n):
                pe.wait_ge(q_ready, n + 1)
                nc.tensor.matmul(psS[:, 0:3 * NB], C["gsum"][:], q[:].rearrange("p a b -> p (a b)"), start=True, stop=True).then_inc(s_ready, 1)

            def front(n, p, h):
                if not (isinstance(n, int) and n == 0):
                    group_sums(n - 1)
                products(n, p, h)

            def back(n, p, h):
                pe.wait_ge(xn2_ready, n + 1)
                for r in range(KD):
                    pe.wait_ge(t_used, n * 2 + (r + 1))
                    for j in range(NB):
                        last = nc.tensor.transpose(psT[:, j * P:(j + 1) * P], xn[:, p, j * D + r * P:j * D + (r + 1) * P], C["ident"][:])
                    last.then_inc(t_done, 1)
                pe.wait_ge(t_used, n * 2 + 3)
                for j in range(NB):
                    for r in range(KD):
                        last = nc.tensor.matmul(psS[:, 64 + j * E0:64 + (j + 1) * E0], xt[:, r * NB + j, :], wr[:, r, :],
                                                start=(r == 0), stop=(r == KD - 1))
                last.then_inc(l_done, 1)

            front(0, 0, 0)
            front(1, 1, 0)
            back(0, 0, 0)
            with pe.Fori(1, STEPS // 2) as h:
                front(h * 2, 0, h)
                back(h * 2 - 1, 1, h - 1)
                front(h * 2 + 1, 1, h)
                back(h * 2, 0, h)
            group_sums(STEPS - 1)
            pe.wait_ge(lg_copied, STEPS - 1)
            back(STEPS - 1, 1, STEPS // 2 - 1)


def first_of(nc, link, values, best, rank, work, top, mask):
    n = values.shape[-1]
    link(nc.vector.tensor_tensor(work, values, best.unsqueeze(2).to_broadcast(values.shape), ALU.is_equal))
    link(nc.vector.tensor_tensor(work, work, rank.unsqueeze(1).to_broadcast(values.shape), ALU.mult))
    link(nc.vector.tensor_reduce(top, work, AX.X, ALU.max))
    return nc.vector.tensor_tensor(mask, work, top.unsqueeze(2).to_broadcast(values.shape), ALU.is_equal)


def route(nc, C):
    NI = HALVES * 2 * TILES
    MK = HALVES * E0 * 2 * TILES
    V = 5
    with ExitStack() as ctx:
        m = Space(nc, ctx, "route")
        sb, ps, sem = m.sb, m.ps, m.sem
        lg = C["logits0"]
        mx = sb("mx", [P, B])
        pr = sb("pr", [P, B, E0])
        sm = sb("sm", [P, B])
        best = sb("best", [P, 2, B])
        work = sb("work", [P, B, E0])
        top = sb("top", [P, B])
        mask = sb("mask", [P, 2, B, E0])
        p2 = sb("p2", [P, B, E0])
        rank = sb("rank", [P, E0])
        mk = sb("mk", [P, HALVES, E0, 2, TILES])
        reset = sb("reset", [P, HALVES * E0, 2 * TILES])
        tot = sb("tot", [P, MK])
        upto = sb("upto", [P, MK])
        pos = sb("pos", [P, HALVES, E0, 2, TILES])
        posk = sb("posk", [P, HALVES, 2, TILES])
        parts = sb("parts", [P, 3, NI], BF16)
        rest = sb("rest", [P, 2, NI])
        gk = sb("gk", [P, HALVES, 2, TILES])
        tileno = sb("tileno", [P, HALVES, 2, TILES])
        rowno = sb("rowno", [P, 1])
        val = sb("val", [P, V, NI], BF16)
        rhs = sb("rhs", [P, NI, E0, V], BF16)
        place = sb("place", [P, CAP])
        onehot = sb("onehot", [P, NI, CAP], BF16)
        tab = sb("tab", [SLOTS, PARTS, E0, V])
        free = sb("free", [SLOTS, 1])
        nfree = sb("nfree", [SLOTS, 1])
        f = sb("f", [SLOTS, PARTS, E0])
        ix = sb("ix", [SLOTS, PARTS, E0])
        psC, psN = ps("psC", [P, MK]), ps("psN", [P, MK])
        psTab = ps("psTab", [SLOTS, PARTS, E0 * V])
        iotas, l_sub, e_up, mk_up, counted, hot, tabled, step = (sem(n) for n in ("iotas", "l_sub", "e_up", "mk_up", "counted", "hot", "tabled", "step"))
        block = ctx.enter_context(nc.Block())

        @block.gpsimd
        def _(pool):
            small = dict(allow_small_or_imprecise_dtypes=True)
            nc.gpsimd.iota(rank[:], [[-1, E0]], base=E0, channel_multiplier=0, **small)
            nc.gpsimd.iota(place[:], [[1, CAP]], base=0, channel_multiplier=0, **small)
            nc.gpsimd.iota(tileno[:], [[TILES, HALVES], [0, 2], [1, TILES]], base=1, channel_multiplier=0, **small)
            nc.gpsimd.iota(rowno[:], [[0, 1]], base=0, channel_multiplier=1, **small)
            nc.gpsimd.iota(free[:], [[0, 1]], base=DUMMY, channel_multiplier=1, **small)
            nc.gpsimd.iota(nfree[:], [[0, 1]], base=-DUMMY - P, channel_multiplier=-1, **small)
            nc.gpsimd.memset(reset[:], 1.0).then_inc(iotas, 1)
            pool.wait_ge(iotas, 1)
            nc.gpsimd.memset(reset[:, :, 0:1], 0.0).then_inc(iotas, 1)
            pool.wait_ge(iotas, 2)

        @block.scalar
        def _(act):
            act.wait_ge(l_sub, 1)
            nc.scalar.activation(pr[:], pr[:], ACT.Exp).then_inc(e_up, 1)

        @block.tensor
        def _(pe):
            pe.wait_ge(mk_up, 1)
            flat = mk[:].rearrange("p h e k t -> p (h e k t)")
            nc.tensor.matmul(psC[:], C["tri"][:], flat, start=True, stop=True)
            nc.tensor.matmul(psN[:], C["ones"][:], flat, start=True, stop=True).then_inc(counted, 1)
            pe.wait_ge(hot, 4)
            for h in range(HALVES):
                for part in range(CAP // SLOTS):
                    for i in range(2 * TILES):
                        n = h * 2 * TILES + i
                        last = nc.tensor.matmul(psTab[:, h * (CAP // SLOTS) + part, :], onehot[:, n, part * SLOTS:(part + 1) * SLOTS],
                                                rhs[:, n].rearrange("p e v -> p (e v)"), start=(i == 0), stop=(i == 2 * TILES - 1))
            last.then_inc(tabled, 1)

        @block.vector
        def _(dve):
            link = Chain(dve, step, 0)
            bc = lambda a: a.unsqueeze(2).to_broadcast([P, B, E0])
            v = nc.vector
            dve.wait_ge(iotas, 2)
            link(v.tensor_reduce(mx[:], lg[:], AX.X, ALU.max))
            v.tensor_tensor(pr[:], lg[:], bc(mx[:]), ALU.subtract).then_inc(l_sub, 1)
            dve.wait_ge(e_up, 1)
            link(v.tensor_reduce(sm[:], pr[:], AX.X, ALU.add))
            link(v.reciprocal(sm[:], sm[:]))
            link(v.tensor_tensor(pr[:], pr[:], bc(sm[:]), ALU.mult))
            link(v.tensor_reduce(best[:, 0, :], pr[:], AX.X, ALU.max))
            link(first_of(nc, link, pr[:], best[:, 0, :], rank[:], work[:], top[:], mask[:, 0]))
            link(v.scalar_tensor_tensor(rows(p2), rows(mask[:, 0]), -2.0, rows(pr), ALU.mult, ALU.add))
            link(v.tensor_reduce(best[:, 1, :], p2[:], AX.X, ALU.max))
            link(first_of(nc, link, p2[:], best[:, 1, :], rank[:], work[:], top[:], mask[:, 1]))
            for k in range(2):
                for h in range(HALVES):
                    last = v.tensor_copy(mk[:, h, :, k, :], mask[:, k, h * TILES:(h + 1) * TILES, :].rearrange("p t e -> p e t"))
            last.then_inc(mk_up, 1)
            for k in range(2):
                last = v.tensor_copy(gk[:, :, k, :], best[:, k, :].rearrange("p (h t) -> p h t", h=HALVES))
            link(last)
            g = gk[:].rearrange("p h k t -> p (h k t)")
            link(v.tensor_copy(parts[:, 0], g))
            link(v.tensor_tensor(rest[:, 0], g, parts[:, 0], ALU.subtract))
            link(v.tensor_copy(parts[:, 1], rest[:, 0]))
            link(v.tensor_tensor(rest[:, 1], rest[:, 0], parts[:, 1], ALU.subtract))
            v.tensor_copy(val[:, 0], tileno[:].rearrange("p h k t -> p (h k t)"))
            v.tensor_copy(val[:, 1], rowno[:].to_broadcast([P, NI]))
            v.tensor_copy(val[:, 2:4], parts[:, 0:2])
            link(v.tensor_copy(val[:, 4], rest[:, 1]))
            for h in range(HALVES):
                r = slice(h * 2 * TILES, (h + 1) * 2 * TILES)
                for n in range(V):
                    last = v.tensor_tensor(rhs[:, r, :, n], mk[:, h].rearrange("p e k t -> p (k t) e"),
                                           val[:, n, r].unsqueeze(2).to_broadcast([P, 2 * TILES, E0]), ALU.mult)
            link(last)
            dve.wait_ge(counted, 1)
            link(v.tensor_copy(tot[:], psN[:]))
            link(v.tensor_tensor_scan(upto[:], reset[:].rearrange("p a b -> p (a b)"), tot[:], 0.0, ALU.mult, ALU.add))
            link(v.tensor_tensor(upto[:], upto[:], tot[:], ALU.subtract))
            flat = pos[:].rearrange("p h e k t -> p (h e k t)")
            link(v.scalar_tensor_tensor(flat, psC[:], -1.0, upto[:], ALU.add, ALU.add))
            link(v.tensor_tensor(flat, flat, mk[:].rearrange("p h e k t -> p (h e k t)"), ALU.mult))
            for h in range(HALVES):
                last = v.tensor_reduce(posk[:, h].rearrange("p k t -> p (k t)"), pos[:, h].rearrange("p e k t -> p (k t) e"), AX.X, ALU.add)
            link(last)
            pk = posk[:].rearrange("p h k t -> p (h k t)")
            for c in range(4):
                r = slice(c * NI // 4, (c + 1) * NI // 4)
                v.tensor_tensor(onehot[:, r], place[:].unsqueeze(1).to_broadcast([P, NI // 4, CAP]),
                                pk[:, r].unsqueeze(2).to_broadcast([P, NI // 4, CAP]), ALU.is_equal).then_inc(hot, 1)
            dve.wait_ge(tabled, 1)
            link(v.tensor_copy(tab[:].rearrange("p a e v -> p a (e v)"), psTab[:]))
            v.tensor_scalar(f[:], tab[:, :, :, 0], 0.0, None, ALU.is_gt)
            link(v.scalar_tensor_tensor(ix[:], tab[:, :, :, 0], float(P), tab[:, :, :, 1], ALU.mult, ALU.add))
            link(v.tensor_scalar(f[:], f[:], nfree[:], free[:], ALU.mult, ALU.add))
            link(v.tensor_tensor(ix[:], ix[:], f[:], ALU.add))
            link(v.tensor_copy(C["slot_row"][:].rearrange("p e a -> p a e"), ix[:]))
            link(v.tensor_tensor(f[:], tab[:, :, :, 4], tab[:, :, :, 3], ALU.add))
            link(v.tensor_tensor(f[:], f[:], tab[:, :, :, 2], ALU.add))
            link(v.tensor_scalar(C["slot_weight"][:].rearrange("p e a -> p a e"), f[:], C["gate"][0:SLOTS, 2:3], None, ALU.mult))


def experts(nc, A, C, X2, XN):
    N = PARTS * SLOTS
    NF = F0 // P
    with ExitStack() as ctx:
        m = Space(nc, ctx, "experts")
        sb, ps, sem = m.sb, m.ps, m.sem
        raw = sb("raw", [P, 2, 2048])
        wih = sb("wih", [P, 2, KD, F0], F32R)
        wil = sb("wil", [P, 2, KD, F0], F32R)
        woh = sb("woh", [P, 2, NF, D], F32R)
        wol = sb("wol", [P, 2, NF, D], F32R)
        row = sb("row", [SLOTS, 2, PARTS], I32)
        xg = sb("xg", [SLOTS, 2, PARTS, D])
        xth = sb("xth", [P, KD, N], F32R)
        xtl = sb("xtl", [P, KD, N], F32R)
        hh = sb("hh", [P, NF, N], F32R)
        hl = sb("hl", [P, NF, N], F32R)
        yg = sb("yg", [SLOTS, 2, PARTS, D])
        psX = [ps(f"psX{k}", [P, 512]) for k in range(KD)]
        psH = [ps(f"psH{k}", [P, 512]) for k in range(4)]
        psY = ps("psY", [SLOTS, PARTS, D])
        w_in = [sem("wi_in"), sem("wo_in")]
        w_hi, w_lo, row_up, stood = (sem(n) for n in ("w_hi", "w_lo", "row_up", "stood"))
        gathered = [sem(f"gathered{p}") for p in range(2)]
        added = [sem(f"added{p}") for p in range(2)]
        xt_done, x_hi, x_lo, h_done, h_hi, h_lo, y_done, y_up = (sem(n) for n in ("xt_done", "x_hi", "x_lo", "h_done", "h_hi", "h_lo", "y_done", "y_up"))
        block = ctx.enter_context(nc.Block())
        PAIRS_OF = E0 // 2

        def over(eng, body):
            body(0, 0, 0)
            body(1, 1, 0)
            with eng.Fori(1, PAIRS_OF - 1) as h:
                body(h * 2, 0, h)
                body(h * 2 + 1, 1, h)
            body(E0 - 2, 0, PAIRS_OF - 1)

        def later(e, first):
            return not isinstance(e, int) or e >= first

        @block.sync
        def _(sp):
            def load(e, p, h):
                sp.wait_ge(w_lo, e * 2 + 1)
                sp.dma_start(raw[:, 0].rearrange("p (k f) -> p k f", k=KD), A["wi"][bass.ds(e, 1)].rearrange("a (k p) f -> p (a k) f", p=P)).then_inc(w_in[0], 16)
                sp.wait_ge(w_lo, e * 2 + 2)
                sp.dma_start(raw[:, 1].rearrange("p (k f) -> p k f", k=NF), A["wo"][bass.ds(e, 1)].rearrange("a (k p) f -> p (a k) f", p=P)).then_inc(w_in[1], 16)
            over(sp, load)
            load(E0 - 1, 1, PAIRS_OF - 1)

        @block.gpsimd
        def _(pool):
            def gather(e, p, h):
                if later(e, 2):
                    pool.wait_ge(added[p], h * 16 * PARTS)
                nc.gpsimd.tensor_copy(row[:, p], C["slot_row"][:, bass.ds(e, 1), :].rearrange("p e a -> p (e a)")).then_inc(row_up, 1)
                pool.wait_ge(row_up, e + 1)
                pool.wait_ge(xt_done, e + 1)
                stand(pool, stood)
                for a in range(PARTS):
                    nc.gpsimd.indirect_dma_start(out=xg[:, p, a, :], out_offset=None, in_=XN,
                                                 in_offset=bass.IndirectOffsetOnAxis(ap=row[:, p, a:a + 1], axis=0)).then_inc(gathered[p], 16)

            def add(e, p, h):
                pool.wait_ge(y_up, e + 2)
                q = 1 - p
                if later(e, 1):
                    pool.wait_ge(added[q], (h + p) * 16 * PARTS)
                stand(pool, stood)
                for a in range(PARTS):
                    nc.gpsimd.indirect_dma_start(out=X2, out_offset=bass.IndirectOffsetOnAxis(ap=row[:, p, a:a + 1], axis=0),
                                                 in_=yg[:, p, a, :], in_offset=None, compute_op=ALU.add).then_inc(added[p], 16)

            gather(0, 0, 0)

            def body(e, p, h):
                gather(e + 1, 1 - p, h + p)
                add(e, p, h)

            over(pool, body)
            add(E0 - 1, 1, PAIRS_OF - 1)
            for p in range(2):
                pool.wait_ge(added[p], PAIRS_OF * 16 * PARTS)

        @block.scalar
        def _(act):
            act.sem_inc(y_up, 1)

            def weights(e, p, h):
                act.wait_ge(y_done, e + 1)
                act.wait_ge(w_in[0], e * 16 + 16)
                nc.scalar.activation(wih[:, p].rearrange("p a b -> p (a b)"), raw[:, 0], ACT.Copy).then_inc(w_hi, 1)
                act.wait_ge(w_in[1], e * 16 + 16)
                nc.scalar.activation(woh[:, p].rearrange("p a b -> p (a b)"), raw[:, 1], ACT.Copy).then_inc(w_hi, 1)

            def x_high(e, p, h):
                act.wait_ge(xt_done, e + 3)
                for k in range(KD):
                    last = nc.scalar.activation(xth[:, k, :], psX[k][:, 0:N], ACT.Copy)
                last.then_inc(x_hi, 1)

            def relu(e, p, h):
                for n in range(NF):
                    act.wait_ge(h_done, e * NF + (n + 1))
                    nc.scalar.activation(hh[:, n, :], psH[n % 4][:, 0:N], ACT.Relu).then_inc(h_hi, 1)

            def weigh(e, p, h):
                act.wait_ge(y_done, e + 3)
                if later(e, 2):
                    act.wait_ge(added[p], h * 16 * PARTS)
                for a in range(PARTS):
                    last = nc.scalar.activation(yg[:, p, a, :], psY[:, a, :], ACT.Copy,
                                                scale=C["slot_weight"][:, bass.ds(e, 1), a:a + 1].rearrange("p e a -> p (e a)"))
                last.then_inc(y_up, 1)

            weights(0, 0, 0)
            x_high(0, 0, 0)

            def body(e, p, h):
                weights(e + 1, 1 - p, h + p)
                relu(e, p, h)
                x_high(e + 1, 1 - p, h + p)
                weigh(e, p, h)

            over(act, body)
            relu(E0 - 1, 1, PAIRS_OF - 1)
            weigh(E0 - 1, 1, PAIRS_OF - 1)

        @block.vector
        def _(dve):
            dve.sem_inc(w_lo, 2)
            dve.sem_inc(h_lo, 4)

            def weights(e, p, h):
                dve.wait_ge(w_hi, e * 2 + 1)
                nc.vector.tensor_tensor(wil[:, p].rearrange("p a b -> p (a b)"), raw[:, 0], wih[:, p].rearrange("p a b -> p (a b)"), ALU.subtract).then_inc(w_lo, 1)
                dve.wait_ge(w_hi, e * 2 + 2)
                nc.vector.tensor_tensor(wol[:, p].rearrange("p a b -> p (a b)"), raw[:, 1], woh[:, p].rearrange("p a b -> p (a b)"), ALU.subtract).then_inc(w_lo, 1)

            def x_low(e, p, h):
                dve.wait_ge(x_hi, e + 1)
                for k in range(KD):
                    last = nc.vector.tensor_tensor(xtl[:, k, :], psX[k][:, 0:N], xth[:, k, :], ALU.subtract)
                last.then_inc(x_lo, 1)

            def relu(e, p, h):
                for n in range(NF):
                    dve.wait_ge(h_hi, e * NF + (n + 1))
                    nc.vector.scalar_tensor_tensor(hl[:, n, :], psH[n % 4][:, 0:N], 0.0, hh[:, n, :], ALU.max, ALU.subtract).then_inc(h_lo, 1)

            weights(0, 0, 0)
            x_low(0, 0, 0)

            def body(e, p, h):
                weights(e + 1, 1 - p, h + p)
                relu(e, p, h)
                x_low(e + 1, 1 - p, h + p)

            over(dve, body)
            relu(E0 - 1, 1, PAIRS_OF - 1)

        @block.tensor
        def _(pe):
            pe.sem_inc(y_done, 2)
            pe.sem_inc(xt_done, 2)

            def turn(e, p, h):
                pe.wait_ge(gathered[p], (h + 1) * 16 * PARTS)
                for k in range(KD):
                    for a in range(PARTS):
                        last = nc.tensor.transpose(psX[k][:, a * SLOTS:(a + 1) * SLOTS], xg[:, p, a, k * P:(k + 1) * P], C["ident"][0:SLOTS, 0:SLOTS])
                last.then_inc(xt_done, 1)

            def up(e, p, h):
                pe.wait_ge(w_lo, e * 2 + 4)
                pe.wait_ge(x_lo, e + 1)
                for n in range(NF):
                    f = slice(n * P, (n + 1) * P)
                    pe.wait_ge(h_lo, e * NF + (n + 1))
                    for k in range(KD):
                        last = product(pe, psH[n % 4][:, 0:N], (wih[:, p, k, f], wil[:, p, k, f]), (xth[:, k, :], xtl[:, k, :]), k == 0, k == KD - 1)
                    last.then_inc(h_done, 1)

            def down(e, p, h):
                pe.wait_ge(h_lo, e * NF + (NF + 4))
                pe.wait_ge(y_up, e + 1)
                for a in range(PARTS):
                    s = slice(a * SLOTS, (a + 1) * SLOTS)
                    for n in range(NF):
                        last = product(pe, psY[:, a, :], (hh[:, n, s], hl[:, n, s]), (woh[:, p, n, :], wol[:, p, n, :]), n == 0, n == NF - 1)
                last.then_inc(y_done, 1)

            turn(0, 0, 0)

            def body(e, p, h):
                up(e, p, h)
                turn(e + 1, 1 - p, h + p)
                down(e, p, h)

            over(pe, body)
            up(E0 - 1, 1, PAIRS_OF - 1)
            down(E0 - 1, 1, PAIRS_OF - 1)


BUCKETS, MAX_DISTANCE = 32, 128


def bucket_onehot():
    exact = BUCKETS // 2
    d = np.maximum(S - 1 - np.arange(2 * S), 0)
    large = exact + (np.log(np.maximum(d, 1) / exact) / np.log(MAX_DISTANCE / exact) * (BUCKETS - exact)).astype(np.int32)
    bucket = np.where(d < exact, d, np.minimum(large, BUCKETS - 1))
    return (np.arange(BUCKETS)[:, None] == bucket[None, :]).astype(np.float32)


def attend(nc, A, C, X2, X3, VB):
    STEPS, NB = B // 2, 2
    N = NB * P
    W = HEADS * P
    SCALE = DH ** -0.5
    with ExitStack() as ctx:
        m_ = Space(nc, ctx, "attend")
        sb, ps, sem = m_.sb, m_.ps, m_.sem
        wqh, wkh, wvh = (sb(n, [P, KD, HEADS * DH], F32R) for n in ("wqh", "wkh", "wvh"))
        wql, wkl, wvl = (sb(n, [P, KD, HEADS * DH], F32R) for n in ("wql", "wkl", "wvl"))
        woh, wol = (sb(n, [P, PAIRS, D], F32R) for n in ("woh", "wol"))
        bias = sb("bias", [P, 2, PAIRS, P])
        q_t, k_t = (sb(n, [P, 2, PAIRS, N]) for n in ("q_t", "k_t"))
        v_n = sb("v_n", [P, 2, NB, HEADS * DH])
        s = sb("s", [P, HEADS, P])
        pr = sb("pr", [P, HEADS, P])
        pt = sb("pt", [P, HEADS, P])
        oh, ol = (sb(n, [P, PAIRS, P], F32R) for n in ("oh", "ol"))
        xin, cin = (sb(n, [P, 2, NB, D]) for n in ("xin", "cin"))
        xn = sb("xn", [P, NB, D])
        xh, xl, ch, cl = (sb(n, [P, KD, N], F32R) for n in ("xh", "xl", "ch", "cl"))
        res = sb("res", [P, 2, D])
        x3 = sb("x3", [P, 2, D])
        stat = sb("stat", [P, NB, 6])
        mv = sb("mv", [P, NB, 2])
        sd = sb("sd", [P, NB])
        rs = sb("rs", [P, NB])
        mx = sb("mx", [P, HEADS])
        sm = sb("sm", [P, HEADS])
        rc = sb("rc", [P, HEADS])
        rel = sb("rel", [BUCKETS, HEADS])
        hot = sb("hot", [BUCKETS, 2 * P])
        vb = sb("vb", [HEADS, 2 * P])
        mask8 = sb("mask8", [P, P], mybir.dt.uint8)
        mask = sb("mask", [P, P])
        psS = ps("psS", [P, W])
        psO = ps("psO", [P, PAIRS * P])
        psJ = [ps(f"psJ{k}", [P, 512]) for k in range(2)]

        raw_in = [sem(f"raw_in{k}") for k in range(2)]
        w_hi, w_lo, rel_in, vb_done, vb_up, vb_out, bias_in, mask_in, bias_up, mask_up = (
            sem(n) for n in ("w_hi", "w_lo", "rel_in", "vb_done", "vb_up", "vb_out", "bias_in", "mask_in", "bias_up", "mask_up"))
        x_in = [sem(f"x_in{k}") for k in range(2)]
        c_in = [sem(f"c_in{k}") for k in range(2)]
        res_in = [sem(f"res_in{k}") for k in range(2)]
        stored = [sem(f"stored{k}") for k in range(2)]
        j_done = [sem(f"j_done{k}") for k in range(2)]
        j_free = [sem(f"j_free{k}") for k in range(2)]
        xn_up, var, sd_up = sem("xn_up"), sem("var"), sem("sd_up")
        x_hi, c_hi = sem("x_hi"), sem("c_hi")
        s_done, s_less, e_up, p_up, pt_done, pt_up, o_done, o_hi, o_lo = (
            sem(n) for n in ("s_done", "s_less", "e_up", "p_up", "pt_done", "pt_up", "o_done", "o_hi", "o_lo"))
        s_ln, s_soft, stood = (sem(n) for n in ("s_ln", "s_soft", "stood"))
        block = ctx.enter_context(nc.Block())

        x2_d = X2[0:B * S, :].rearrange("(b p) d -> p b d", p=P)
        x3_d = X3.rearrange("(b p) d -> p b d", p=P)
        c_d = A["ctx_1024"].rearrange("b p d -> p b d")

        Q, WO_OLD, K, V0, WO_NEW, V1, TURN = [0, 1, 2, 3], [4], [5, 6, 7, 8], [9, 10], [11], [12, 13], [14, 15]
        ALL = Q + WO_OLD + K + V0 + WO_NEW + V1 + TURN

        def uses(n):
            if n == -1:
                return [u for u in ALL if u not in WO_OLD + WO_NEW]
            if n == 0:
                return [u for u in ALL if u not in WO_OLD]
            if n == STEPS - 2:
                return [u for u in ALL if u not in TURN]
            if n == STEPS - 1:
                return WO_OLD + WO_NEW
            return WO_OLD if n == STEPS else ALL

        def uses_before(bank, n):
            return 1 + sum(u % 2 == bank for k in range(-1, n) for u in uses(k))

        def turn_of(n, u):
            bank = u % 2
            if isinstance(n, int) and n == -2:
                return 1
            at = sum(v % 2 == bank and v <= u for v in (uses(n) if isinstance(n, int) else ALL))
            if isinstance(n, int):
                return uses_before(bank, n) + at
            return (n - 1) * (len(ALL) // 2) + (uses_before(bank, 1) + at)

        def used(eng, n, u):
            eng.wait_ge(j_done[u % 2], turn_of(n, u))

        def read(eng, n, u):
            eng.wait_ge(j_free[u % 2], turn_of(n, u))

        def over(eng, body, last):
            body(0, 0, 0)
            with eng.Fori(0, (STEPS - 4) // 2) as h:
                body(h * 2 + 1, 1, h)
                body(h * 2 + 2, 0, h + 1)
            for n in range(STEPS - 3, STEPS):
                body(n, n % 2, n // 2)
            last()

        def projects(n):
            return not isinstance(n, int) or n <= STEPS - 2

        def turns(n):
            return not isinstance(n, int) or n <= STEPS - 3

        def later(n):
            return not isinstance(n, int) or n >= 1

        @block.sync
        def _(sp):
            for k, name in enumerate(("Wq", "Wk", "Wv", "Wo")):
                if k >= 2:
                    sp.wait_ge(w_lo, k - 1)
                to = (s, pr)[k % 2][:].rearrange("p a b -> p (a b)").rearrange("p (k n) -> p k n", k=PAIRS if name == "Wo" else KD)
                sp.dma_start(to, A[name].rearrange("(k p) n -> p k n", p=P)).then_inc(raw_in[k % 2], 16)
                if k == 0:
                    sp.dma_start(rel[:], A["relT"]).then_inc(rel_in, 16)
                    sp.dma_start(hot[:], A["hot"]).then_inc(rel_in, 16)
                    sp.dma_start(mask8[:], A["mask"]).then_inc(mask_in, 16)
            sp.wait_ge(vb_up, 1)
            sp.dma_start(VB, vb[:].unsqueeze(1).to_broadcast([HEADS, P, 2 * P])).then_inc(vb_out, 16)
            sp.wait_ge(vb_out, 16)
            for r in range(2):
                sp.dma_start(bias[:, r], bass.AP(VB.tensor, VB.offset + r * P * 2 * P + P - 1, [[2 * P - 1, P], [2 * P * 2 * P, PAIRS], [1, P]])).then_inc(bias_in, 16)

            def load(n, p, h):
                sp.wait_ge(xn_up, n + 1)
                sp.dma_start(xin[:, p], x2_d[:, bass.ds(n * NB, NB), :]).then_inc(x_in[p], 16)
                if not isinstance(n, int) or n >= 2:
                    used(sp, n - 4, TURN[1])
                sp.dma_start(cin[:, p], c_d[:, bass.ds(n * NB, NB), :]).then_inc(c_in[p], 16)

            def residual(n, i):
                if later(n):
                    read(sp, *((n - 1, WO_NEW[0]) if i == 0 else (n, WO_OLD[0])))
                sp.dma_start(res[:, i], x2_d[:, bass.ds(n * NB + i, 1), :].rearrange("p a d -> p (a d)")).then_inc(res_in[i], 16)

            load(0, 0, 0)
            load(1, 1, 0)

            def body(n, p, h):
                residual(n, 0)
                if turns(n):
                    load(n + 2, p, h + 1)
                residual(n, 1)

            over(sp, body, lambda: None)

        @block.scalar
        def _(act):
            for k, high in enumerate((wqh, wkh, wvh, woh)):
                act.wait_ge(raw_in[k % 2], 16 * (k // 2 + 1))
                nc.scalar.activation(high[:].rearrange("p a b -> p (a b)"), (s, pr)[k % 2][:].rearrange("p a b -> p (a b)"), ACT.Copy).then_inc(w_hi, 1)
            act.wait_ge(vb_done, 1)
            nc.scalar.activation(vb[:], psO[0:HEADS, 0:2 * P], ACT.Copy).then_inc(vb_up, 1)
            for p in range(2):
                act.sem_inc(stored[p], 16)

            def x_high(n):
                for u, to, done in ((TURN[0], xh, x_hi), (TURN[1], ch, c_hi)):
                    used(act, n, u)
                    nc.scalar.activation(to[:].rearrange("p a b -> p (a b)"), psJ[u % 2][:], ACT.Copy).then_inc(done, 1)

            def deviation(n):
                act.wait_ge(var, n + 1)
                nc.scalar.activation(sd[:], mv[:, :, 1], ACT.Sqrt, bias=C["eps"][:]).then_inc(sd_up, 1)

            def exps(b):
                act.wait_ge(s_less, b + 1)
                nc.scalar.activation(s[:], s[:], ACT.Exp).then_inc(e_up, 1)

            def evacuate(n, u, to):
                used(act, n, u)
                nc.scalar.activation(to, psJ[u % 2][:].rearrange("p (a b) -> p a b", a=to.shape[1]), ACT.Copy).then_inc(j_free[u % 2], 1)

            def qk(n, us, to, p):
                for k, u in enumerate(us):
                    evacuate(n, u, to[:, p, k * 2:k * 2 + 2, :])

            def vs(n, us, i, p):
                for k, u in enumerate(us):
                    evacuate(n, u, v_n[:, p, i:i + 1, k * 512:(k + 1) * 512])

            def p_out(b):
                act.wait_ge(pt_done, b + 1)
                flat = pt[:].rearrange("p a b -> p (a b)")
                for k in range(2):
                    r = slice(k * W // 2, (k + 1) * W // 2)
                    last = nc.scalar.activation(flat[:, r], psS[:, r], ACT.Copy)
                last.then_inc(pt_up, 1)

            def o_high(b):
                act.wait_ge(o_done, b + 1)
                nc.scalar.activation(oh[:].rearrange("p a b -> p (a b)"), psO[:], ACT.Copy).then_inc(o_hi, 1)

            def store(b, n, u, i):
                read(act, n, u)
                act.dma_start(x3_d[:, bass.ds(b, 1), :].rearrange("p a d -> p (a d)"), x3[:, i]).then_inc(stored[i], 16)

            deviation(0)
            x_high(-2)
            deviation(1)
            qk(-1, Q, q_t, 0)
            qk(-1, K, k_t, 0)
            vs(-1, V0, 0, 0)
            vs(-1, V1, 1, 0)
            x_high(-1)

            def body(n, p, h):
                b = n * 2
                if later(n):
                    o_high(b - 1)
                if projects(n):
                    qk(n, Q[0:2], q_t, 1 - p)
                exps(b)
                if turns(n):
                    deviation(n + 2)
                if projects(n):
                    for k, u in enumerate(Q[2:4]):
                        evacuate(n, u, q_t[:, 1 - p, 4 + k * 2:6 + k * 2, :])
                if later(n):
                    store(b - 1, n, WO_OLD[0], 1)
                if projects(n):
                    qk(n, K, k_t, 1 - p)
                p_out(b)
                o_high(b)
                if projects(n):
                    vs(n, V0, 0, 1 - p)
                exps(b + 1)
                store(b, n, WO_NEW[0], 0)
                if projects(n):
                    vs(n, V1, 1, 1 - p)
                if turns(n):
                    x_high(n)
                p_out(b + 1)

            def last():
                o_high(B - 1)
                store(B - 1, STEPS, WO_OLD[0], 1)
                for p in range(2):
                    act.wait_ge(stored[p], 16 * (B // 2) + 16)

            over(act, body, last)

        @block.vector
        def _(dve):
            dve.sem_inc(xn_up, 2)
            v = nc.vector
            for k, (high, low) in enumerate(((wqh, wql), (wkh, wkl), (wvh, wvl), (woh, wol))):
                dve.wait_ge(w_hi, k + 1)
                v.tensor_tensor(low[:].rearrange("p a b -> p (a b)"), (s, pr)[k % 2][:].rearrange("p a b -> p (a b)"),
                                high[:].rearrange("p a b -> p (a b)"), ALU.subtract).then_inc(w_lo, 1)
            dve.wait_ge(w_lo, 4)
            dve.wait_ge(mask_in, 16)
            v.tensor_copy(mask[:], mask8[:]).then_inc(mask_up, 1)
            dve.wait_ge(mask_up, 1)
            v.tensor_scalar(mask[:], mask[:], -1.0, -LOWEST, ALU.add, ALU.mult).then_inc(mask_up, 1)
            dve.wait_ge(mask_up, 2)
            dve.wait_ge(bias_in, 32)
            flat = bias[:].rearrange("p r m k -> p (r m) k")
            v.tensor_tensor(flat, flat, mask[:].unsqueeze(1).to_broadcast([P, HEADS, P]), ALU.add).then_inc(bias_up, 1)
            dve.wait_ge(bias_up, 1)
            ln, soft = Chain(dve, s_ln, 2), Chain(dve, s_soft, 4)

            def norm(n, p, h):
                ln.start(n)
                dve.wait_ge(x_in[p], h * 16 + 16)
                for i in range(NB):
                    last = v.bn_stats(stat[:, i, :], xin[:, p, i, :])
                ln(last)
                stand(dve, stood)
                for i in range(NB):
                    last = v.bn_aggr(mv[:, i, :], stat[:, i, :])
                last.then_inc(var, 1)
                dve.wait_ge(sd_up, n + 1)
                ln(v.reciprocal(rs[:], sd[:]))
                if not isinstance(n, int) or n >= 1:
                    used(dve, n - 3, TURN[0])
                for i in range(NB):
                    last = v.tensor_scalar(xn[:, i, :], xin[:, p, i, :], mv[:, i, 0:1], rs[:, i:i + 1], ALU.subtract, ALU.mult)
                last.then_inc(xn_up, 1)
                ln.end()

            def x_low(n, m):
                for u, high, low, done in ((TURN[0], xh, xl, x_hi), (TURN[1], ch, cl, c_hi)):
                    dve.wait_ge(done, m + 1)
                    v.tensor_tensor(low[:].rearrange("p a b -> p (a b)"), psJ[u % 2][:], high[:].rearrange("p a b -> p (a b)"), ALU.subtract).then_inc(j_free[u % 2], 1)

            def less_max(b):
                soft.start(b)
                dve.wait_ge(s_done, b + 1)
                soft(v.scalar_tensor_tensor(s[:].rearrange("p a b -> p (a b)"), psS[:], SCALE, bias[:].rearrange("p r m k -> p (r m k)"), ALU.mult, ALU.add))
                soft(v.tensor_reduce(mx[:], s[:], AX.X, ALU.max))
                v.tensor_tensor(s[:], s[:], mx[:].unsqueeze(2).to_broadcast([P, HEADS, P]), ALU.subtract).then_inc(s_less, 1)

            def normed(b):
                dve.wait_ge(e_up, b + 1)
                soft(v.tensor_reduce(sm[:], s[:], AX.X, ALU.add))
                soft(v.reciprocal(rc[:], sm[:]))
                if not isinstance(b, int) or b >= 1:
                    dve.wait_ge(pt_done, b)
                v.tensor_tensor(pr[:], s[:], rc[:].unsqueeze(2).to_broadcast([P, HEADS, P]), ALU.mult).then_inc(p_up, 1)
                soft.end()

            def o_low(b):
                dve.wait_ge(o_hi, b + 1)
                v.tensor_tensor(ol[:].rearrange("p a b -> p (a b)"), psO[:], oh[:].rearrange("p a b -> p (a b)"), ALU.subtract).then_inc(o_lo, 1)

            def add(n, u, i, nb):
                used(dve, n, u)
                dve.wait_ge(res_in[i], nb * 16 + 16)
                dve.wait_ge(stored[i], nb * 16 + 16)
                v.scalar_tensor_tensor(x3[:, i], psJ[u % 2][:, 0:D], C["gate"][:, 1:2], res[:, i], ALU.mult, ALU.add).then_inc(j_free[u % 2], 1)

            norm(0, 0, 0)
            x_low(-2, 0)
            norm(1, 1, 0)
            x_low(-1, 1)

            def body(n, p, h):
                b = n * 2
                less_max(b)
                if later(n):
                    o_low(b - 1)
                if turns(n):
                    norm(n + 2, p, h + 1)
                if later(n):
                    add(n, WO_OLD[0], 1, n - 1)
                normed(b)
                less_max(b + 1)
                o_low(b)
                add(n, WO_NEW[0], 0, n)
                normed(b + 1)
                if turns(n):
                    x_low(n, n + 2)

            def last():
                o_low(B - 1)
                add(STEPS, WO_OLD[0], 1, STEPS - 1)

            over(dve, body, last)

        @block.tensor
        def _(pe):
            pe.wait_ge(rel_in, 32)
            nc.tensor.matmul(psO[0:HEADS, 0:2 * P], rel[:], hot[:], start=True, stop=True).then_inc(vb_done, 1)
            pe.wait_ge(w_lo, 4)
            pe.wait_ge(vb_up, 1)

            def bank(n, u):
                before = turn_of(n, u) - 1
                if not (isinstance(before, int) and before == 0):
                    pe.wait_ge(j_free[u % 2], before)
                return psJ[u % 2]

            def turn(n, m, p, h):
                for u, src, ready in ((TURN[0], xn, lambda: pe.wait_ge(xn_up, m + 3)),
                                      (TURN[1], cin[:, p], lambda: pe.wait_ge(c_in[p], h * 16 + 16))):
                    to = bank(n, u)
                    ready()
                    for k in range(KD):
                        for i in range(NB):
                            last = nc.tensor.transpose(to[:, k * N + i * P:k * N + (i + 1) * P], src[:, i, k * P:(k + 1) * P], C["ident"][:])
                    last.then_inc(j_done[u % 2], 1)

            def qk(n, us, weights, moving, at=0):
                for c, u in enumerate(us):
                    to = bank(n, u)
                    for j in range(2):
                        r = slice((at + c * 2 + j) * P, (at + c * 2 + j + 1) * P)
                        for k in range(KD):
                            last = product(pe, to[:, j * N:(j + 1) * N], [w[:, k, r] for w in weights], [x[:, k, :] for x in moving], k == 0, k == KD - 1)
                    last.then_inc(j_done[u % 2], 1)

            def vs(n, us, i):
                for c, u in enumerate(us):
                    to = bank(n, u)
                    for k in range(KD):
                        last = product(pe, to[:], [x[:, k, i * P:(i + 1) * P] for x in (ch, cl)],
                                       [w[:, k, c * 512:(c + 1) * 512] for w in (wvh, wvl)], k == 0, k == KD - 1)
                    last.then_inc(j_done[u % 2], 1)

            def scores(b, n, p, i):
                if i == 0:
                    for u in V1:
                        read(pe, n - 1, u)
                if not (isinstance(b, int) and b == 0):
                    pe.wait_ge(pt_up, b)
                q = slice(i * P, (i + 1) * P)
                for m in range(PAIRS):
                    for r in range(2):
                        half = slice(r * DH, (r + 1) * DH)
                        last = nc.tensor.matmul(psS[:, (r * PAIRS + m) * P:(r * PAIRS + m + 1) * P], q_t[half, p, m, q], k_t[half, p, m, q],
                                                start=True, stop=True)
                last.then_inc(s_done, 1)

            def turn_p(b):
                pe.wait_ge(p_up, b + 1)
                for j in range(HEADS):
                    last = nc.tensor.transpose(psS[:, j * P:(j + 1) * P], pr[:, j, :], C["ident"][:])
                last.then_inc(pt_done, 1)

            def values(b, p, i):
                pe.wait_ge(pt_up, b + 1)
                if not (isinstance(b, int) and b == 0):
                    pe.wait_ge(o_lo, b)
                for m in range(PAIRS):
                    for r in range(2):
                        last = nc.tensor.matmul(psO[r * DH:(r + 1) * DH, m * P:(m + 1) * P], v_n[:, p, i, (2 * m + r) * DH:(2 * m + r + 1) * DH],
                                                pt[:, r * PAIRS + m, :], start=True, stop=True)
                last.then_inc(o_done, 1)

            def out(b, n, u):
                to = bank(n, u)
                pe.wait_ge(o_lo, b + 1)
                for m in range(PAIRS):
                    last = product(pe, to[:, 0:D], (oh[:, m, :], ol[:, m, :]), (woh[:, m, :], wol[:, m, :]), m == 0, m == PAIRS - 1)
                last.then_inc(j_done[u % 2], 1)

            turn(-2, 0, 0, 0)
            qk(-1, Q, (wqh, wql), (xh, xl))
            qk(-1, K, (wkh, wkl), (ch, cl))
            vs(-1, V0, 0)
            vs(-1, V1, 1)
            turn(-1, 1, 1, 0)

            def body(n, p, h):
                b = n * 2
                scores(b, n, p, 0)
                if later(n):
                    values(b - 1, 1 - p, 1)
                if projects(n):
                    qk(n, Q, (wqh, wql), (xh, xl))
                if later(n):
                    out(b - 1, n, WO_OLD[0])
                if projects(n):
                    qk(n, K, (wkh, wkl), (ch, cl))
                turn_p(b)
                scores(b + 1, n, p, 1)
                values(b, p, 0)
                if projects(n):
                    vs(n, V0, 0)
                out(b, n, WO_NEW[0])
                if projects(n):
                    vs(n, V1, 1)
                if turns(n):
                    turn(n, n + 2, p, h + 1)
                turn_p(b + 1)

            def last():
                values(B - 1, 1, 1)
                out(B - 1, STEPS, WO_OLD[0])

            over(pe, body, last)


def gated_in(nc, A, C, X3, acc, xth, xtl):
    STEPS, NB = B // 4, 4
    N = NB * P
    with ExitStack() as ctx:
        m = Space(nc, ctx, "gin")
        sb, ps, sem = m.sb, m.ps, m.sem
        gw = sb("gw", [P, KD, E1])
        stat = sb("stat", [P, NB, 6])
        mv = sb("mv", [P, 2, NB, 2])
        sd = sb("sd", [P, 2, NB])
        rs = sb("rs", [P, NB])
        xn = sb("xn", [P, 2, NB, D])
        xt = sb("xt", [P, 2, KD, N])
        psT = [ps(f"psT{p}", [P, KD, N]) for p in range(2)]
        psL = [ps(f"psL{p}", [P, 512]) for p in range(2)]
        x_in = [sem(f"x_in{p}") for p in range(2)]
        gw_in, var, sd_up, xn_up, t_done, t_up, hi, lo, l_done, l_up = (sem(n) for n in ("gw_in", "var", "sd_up", "xn_up", "t_done", "t_up", "hi", "lo", "l_done", "l_up"))
        s_ln, stood = sem("s_ln"), sem("stood")
        block = ctx.enter_context(nc.Block())
        x3_d = X3.rearrange("(b p) d -> p b d", p=P)

        def over(eng, body):
            with eng.Fori(0, STEPS // 2) as h:
                body(h * 2, 0, h)
                body(h * 2 + 1, 1, h)

        @block.sync
        def _(sp):
            sp.dma_start(gw[:], A["gwT"].rearrange("(k p) e -> p k e", p=P)).then_inc(gw_in, 16)

            def load(n, p, h):
                sp.wait_ge(var, n + 1)
                sp.dma_start(acc[:, bass.ds(n * NB, NB), :], x3_d[:, bass.ds(n * NB, NB), :]).then_inc(x_in[p], 16)
            over(sp, load)

        @block.scalar
        def _(act):
            act.sem_inc(l_up, 2)
            act.sem_inc(t_up, 2)

            def body(n, p, h):
                act.wait_ge(var, n + 3)
                nc.scalar.activation(sd[:, p], mv[:, p, :, 1], ACT.Sqrt, bias=C["eps"][:]).then_inc(sd_up, 1)
                act.wait_ge(t_done, n + 3)
                act.wait_ge(lo, n + 1)
                nc.scalar.activation(xt[:, p].rearrange("p k t -> p (k t)"), psT[p][:].rearrange("p k t -> p (k t)"), ACT.Copy).then_inc(t_up, 1)
                act.wait_ge(t_up, n + 3)
                nc.scalar.activation(xth[:, :, bass.ds(n * N, N)], xt[:, p], ACT.Copy).then_inc(hi, 1)
                act.wait_ge(l_done, n + 1)
                nc.scalar.activation(C["logits1"][:, bass.ds(n * NB, NB), :], psL[p][:, 0:NB * E1].rearrange("p (i e) -> p i e", e=E1), ACT.Copy).then_inc(l_up, 1)
            over(act, body)

        @block.gpsimd
        def _(pool):
            pool.sem_inc(lo, 2)

            def body(n, p, h):
                pool.wait_ge(hi, n + 1)
                nc.gpsimd.tensor_tensor(xtl[:, :, bass.ds(n * N, N)], xt[:, p], xth[:, :, bass.ds(n * N, N)], ALU.subtract).then_inc(lo, 1)
            over(pool, body)

        @block.tensor
        def _(pe):
            pe.wait_ge(gw_in, 16)
            pe.sem_inc(t_done, 2)

            def body(n, p, h):
                pe.wait_ge(xn_up, n + 3)
                pe.wait_ge(t_up, n + 1)
                for k in range(KD):
                    for i in range(NB):
                        last = nc.tensor.transpose(psT[p][:, k, i * P:(i + 1) * P], xn[:, p, i, k * P:(k + 1) * P], C["ident"][:])
                last.then_inc(t_done, 1)
                pe.wait_ge(t_up, n + 3)
                pe.wait_ge(l_up, n + 1)
                for i in range(NB):
                    for k in range(KD):
                        last = nc.tensor.matmul(psL[p][:, i * E1:(i + 1) * E1], xt[:, p, k, i * P:(i + 1) * P], gw[:, k, :], start=(k == 0), stop=(k == KD - 1))
                last.then_inc(l_done, 1)
            over(pe, body)

        @block.vector
        def _(dve):
            v = nc.vector
            dve.sem_inc(var, 2)
            dve.sem_inc(xn_up, 2)
            ln = Chain(dve, s_ln, 2)

            def body(n, p, h):
                ln.start(n)
                dve.wait_ge(x_in[p], h * 16 + 16)
                for i in range(NB):
                    last = v.bn_stats(stat[:, i, :], acc[:, bass.ds(n * NB + i, 1), :].rearrange("p a d -> p (a d)"))
                ln(last)
                stand(dve, stood)
                for i in range(NB):
                    last = v.bn_aggr(mv[:, p, i, :], stat[:, i, :])
                last.then_inc(var, 1)
                dve.wait_ge(sd_up, n + 1)
                ln(v.reciprocal(rs[:], sd[:, p]))
                dve.wait_ge(t_done, n + 1)
                for i in range(NB):
                    last = v.tensor_scalar(xn[:, p, i, :], acc[:, bass.ds(n * NB + i, 1), :].rearrange("p a d -> p (a d)"), mv[:, p, i, 0:1], rs[:, i:i + 1],
                                           ALU.subtract, ALU.mult)
                last.then_inc(xn_up, 1)
                ln.end()
            over(dve, body)


def gated_route(nc, A, C):
    NG = E1 // 4
    with ExitStack() as ctx:
        m = Space(nc, ctx, "groute")
        sb, sem = m.sb, m.sem
        score, tmp, work, pick, sel = (sb(n, [P, B, E1]) for n in ("score", "tmp", "work", "pick", "sel"))
        eb = sb("eb", [P, E1])
        rank = sb("rank", [P, E1])
        hi2, lo2 = sb("hi2", [P, B, NG, 2]), sb("lo2", [P, B, NG, 2])
        gs, gwork, g1, g2 = (sb(n, [P, B, NG]) for n in ("gs", "gwork", "g1", "g2"))
        top, best = sb("top", [P, B]), sb("best", [P, B])
        eb_in, ranked, s_up, step = sem("eb_in"), sem("ranked"), sem("s_up"), sem("step")
        block = ctx.enter_context(nc.Block())

        @block.sync
        def _(sp):
            sp.dma_start(eb[:], A["ebias"].rearrange("(a n) -> a n", a=1).to_broadcast((P, E1))).then_inc(eb_in, 16)

        @block.gpsimd
        def _(pool):
            nc.gpsimd.iota(rank[:], [[-1, E1]], base=E1, channel_multiplier=0, allow_small_or_imprecise_dtypes=True).then_inc(ranked, 1)

        @block.scalar
        def _(act):
            nc.scalar.activation(score[:], C["logits1"][:], ACT.Sigmoid).then_inc(s_up, 1)

        @block.vector
        def _(dve):
            v = nc.vector
            link = Chain(dve, step, 0)
            dve.wait_ge(eb_in, 16)
            dve.wait_ge(ranked, 1)
            dve.wait_ge(s_up, 1)
            link(v.tensor_tensor(tmp[:], score[:], eb[:].unsqueeze(1).to_broadcast([P, B, E1]), ALU.add))
            four = tmp[:].rearrange("p t (g a b) -> p (t g) a b", g=NG, a=2)
            flat = lambda x: x[:].rearrange("p t g a -> p (t g) a")
            v.tensor_tensor(flat(hi2), four[:, :, :, 0], four[:, :, :, 1], ALU.max)
            link(v.tensor_tensor(flat(lo2), four[:, :, :, 0], four[:, :, :, 1], ALU.min))
            v.tensor_tensor(gs[:], hi2[:, :, :, 0], hi2[:, :, :, 1], ALU.max)
            v.tensor_tensor(g1[:], hi2[:, :, :, 0], hi2[:, :, :, 1], ALU.min)
            link(v.tensor_tensor(g2[:], lo2[:, :, :, 0], lo2[:, :, :, 1], ALU.max))
            link(v.tensor_tensor(g1[:], g1[:], g2[:], ALU.max))
            link(v.tensor_tensor(gs[:], gs[:], g1[:], ALU.add))
            link(v.tensor_reduce(best[:], gs[:], AX.X, ALU.max))
            link(first_of(nc, link, gs[:], best[:], rank[:, 0:NG], gwork[:], top[:], g1[:]))
            link(v.scalar_tensor_tensor(rows(gs), rows(g1), -1e30, rows(gs), ALU.mult, ALU.add))
            link(v.tensor_reduce(best[:], gs[:], AX.X, ALU.max))
            link(first_of(nc, link, gs[:], best[:], rank[:, 0:NG], gwork[:], top[:], g2[:]))
            link(v.tensor_tensor(g1[:], g1[:], g2[:], ALU.add))
            link(v.tensor_tensor(tmp[:].rearrange("p t (g a) -> p (t g) a", g=NG), tmp[:].rearrange("p t (g a) -> p (t g) a", g=NG),
                                 g1[:].rearrange("p t g -> p (t g)").unsqueeze(2).to_broadcast([P, B * NG, E1 // NG]), ALU.mult))
            for k in range(TOP):
                link(v.tensor_reduce(best[:], tmp[:], AX.X, ALU.max))
                link(first_of(nc, link, tmp[:], best[:], rank[:], work[:], top[:], pick[:]))
                if k == 0:
                    link(v.tensor_copy(sel[:], pick[:]))
                else:
                    link(v.tensor_tensor(sel[:], sel[:], pick[:], ALU.add))
                if k < TOP - 1:
                    link(v.scalar_tensor_tensor(rows(tmp), rows(pick), -1e30, rows(tmp), ALU.mult, ALU.add))
            link(v.tensor_tensor(sel[:], sel[:], score[:], ALU.mult))
            link(v.tensor_reduce(top[:], sel[:], AX.X, ALU.add))
            link(v.tensor_scalar(top[:], top[:], 1e-20, None, ALU.add))
            link(v.reciprocal(top[:], top[:]))
            link(v.tensor_tensor(sel[:], sel[:], top[:].unsqueeze(2).to_broadcast([P, B, E1]), ALU.mult))
            link(v.tensor_scalar(C["weight1"][:, :, 0:E1], sel[:], 2.5, C["gate"][:, 3:4], ALU.mult, ALU.mult))
            link(v.tensor_copy(C["weight1"][:, :, E1:E1 + 1].rearrange("p t a -> p (t a)"), C["gate"][:, 3:4].to_broadcast([P, B])))


def gated(nc, A, C, acc, xth, xtl, out):
    EX, NB = E1 + 1, 4
    N = NB * P
    BLOCKS = B // NB
    with ExitStack() as ctx:
        m = Space(nc, ctx, "gated")
        sb, ps, sem = m.sb, m.ps, m.sem
        raw = sb("raw", [P, 2, 3, KD, I1])
        wh = sb("wh", [P, 2, 3, KD, I1], F32R)
        wl = sb("wl", [P, 2, 3, KD, I1], F32R)
        sg = sb("sg", [P, 2, N])
        it = sb("it", [P, 2, N])
        ih = sb("ih", [P, 2, N], F32R)
        il = sb("il", [P, 2, N], F32R)
        psG = [ps(f"psG{p}", [P, N]) for p in range(2)]
        psU = [ps(f"psU{p}", [P, N]) for p in range(2)]
        psY = [ps(f"psY{p}", [P, NB, D]) for p in range(2)]
        w_in = [sem(f"w_in{p}") for p in range(2)]
        w_hi, w_lo, g_done, u_done, s_up, i_up, i_hi, i_lo, y_done, y_up, stored = (
            sem(n) for n in ("w_hi", "w_lo", "g_done", "u_done", "s_up", "i_up", "i_hi", "i_lo", "y_done", "y_up", "stored"))
        block = ctx.enter_context(nc.Block())
        out_d = out.rearrange("b p d -> p b d")

        def over(eng, body):
            with eng.Fori(0, EX // 2) as h:
                body(h * 2, 0, h)
                body(h * 2 + 1, 1, h)
            body(EX - 1, 0, EX // 2)

        @block.sync
        def _(sp):
            def load(e, p, h):
                sp.wait_ge(w_lo, e + 1)
                sp.dma_start(raw[:, p].rearrange("p a k i -> p (a k i)"), A["gex"][bass.ds(e, 1)].rearrange("a p n -> p (a n)")).then_inc(w_in[p], 16)
            over(sp, load)
            sp.wait_ge(y_up, EX * BLOCKS)
            sp.wait_ge(stored, 16 * BLOCKS)

        @block.gpsimd
        def _(pool):
            pool.sem_inc(w_lo, 2)

            def weights(e, p, h):
                pool.wait_ge(w_hi, e + 1)
                nc.gpsimd.tensor_tensor(wl[:, p].rearrange("p a k i -> p (a k i)"), raw[:, p].rearrange("p a k i -> p (a k i)"),
                                        wh[:, p].rearrange("p a k i -> p (a k i)"), ALU.subtract).then_inc(w_lo, 1)

            def low(e, j):
                n = e * BLOCKS + j
                pool.wait_ge(i_hi, n + 1)
                nc.gpsimd.tensor_tensor(il[:, j % 2], it[:, j % 2], ih[:, j % 2], ALU.subtract).then_inc(i_lo, 1)

            weights(0, 0, 0)

            def body(e, p, h):
                for j in range(BLOCKS):
                    low(e, j)
                    if j == 3 and not (isinstance(e, int) and e == EX - 1):
                        weights(e + 1, 1 - p, h + p)
            over(pool, body)

        @block.scalar
        def _(act):
            def weights(e, p, h):
                act.wait_ge(w_in[p], h * 16 + 16)
                if not (isinstance(e, int) and e < 1):
                    act.wait_ge(y_done, e * BLOCKS - BLOCKS + 1)
                nc.scalar.activation(wh[:, p].rearrange("p a k i -> p (a k i)"), raw[:, p].rearrange("p a k i -> p (a k i)"), ACT.Copy).then_inc(w_hi, 1)

            def body(e, p, h):
                for j in range(BLOCKS):
                    n = e * BLOCKS + j
                    act.wait_ge(g_done, n + 1)
                    nc.scalar.activation(sg[:, j % 2], psG[j % 2][:], ACT.Silu).then_inc(s_up, 1)
                    act.wait_ge(i_up, n + 1)
                    nc.scalar.activation(ih[:, j % 2], it[:, j % 2], ACT.Copy).then_inc(i_hi, 1)
                    if j == 3 and not (isinstance(e, int) and e == EX - 1):
                        weights(e + 1, 1 - p, h + p)
                    if isinstance(e, int) and e == EX - 1 and j >= 1:
                        store(j - 1)

            def store(j):
                act.wait_ge(y_up, (EX - 1) * BLOCKS + j + 1)
                act.dma_start(out_d[:, j * NB:(j + 1) * NB, :], acc[:, j * NB:(j + 1) * NB, :]).then_inc(stored, 16)

            weights(0, 0, 0)
            over(act, body)
            store(BLOCKS - 1)

        @block.vector
        def _(dve):
            v = nc.vector

            def mul(e, j):
                n = e * BLOCKS + j
                dve.wait_ge(s_up, n + 1)
                dve.wait_ge(u_done, n + 1)
                v.tensor_tensor(it[:, j % 2], sg[:, j % 2], psU[j % 2][:], ALU.mult).then_inc(i_up, 1)

            def add(e, j):
                n = e * BLOCKS + j
                dve.wait_ge(y_done, n + 2)
                for i in range(NB):
                    a = acc[:, j * NB + i, :]
                    last = v.scalar_tensor_tensor(a, psY[j % 2][:, i, :], C["weight1"][:, j * NB + i, bass.ds(e, 1)], a, ALU.mult, ALU.add)
                last.then_inc(y_up, 1)

            def body(e, p, h):
                for j in range(BLOCKS):
                    mul(e, j)
                    if j:
                        add(e, j - 1)
                    elif not (isinstance(e, int) and e == 0):
                        add(e - 1, BLOCKS - 1)

            mul(0, 0)
            for j in range(1, BLOCKS):
                mul(0, j)
                add(0, j - 1)
            with dve.Fori(0, (EX - 1) // 2) as h:
                body(h * 2 + 1, 1, h)
                body(h * 2 + 2, 0, h + 1)
            add(EX - 1, BLOCKS - 1)

        @block.tensor
        def _(pe):
            def up(e, p, j):
                n = e * BLOCKS + j
                t = slice(j * N, (j + 1) * N)
                if isinstance(n, int) and n < 2:
                    pass
                else:
                    pe.wait_ge(i_up, n - 1)
                if j == 0:
                    pe.wait_ge(w_lo, e + 3)
                for a, to, done in ((0, psG, g_done), (1, psU, u_done)):
                    for k in range(KD):
                        last = product(pe, to[j % 2][:], (wh[:, p, a, k, :], wl[:, p, a, k, :]), (xth[:, k, t], xtl[:, k, t]), k == 0, k == KD - 1)
                    last.then_inc(done, 1)

            def down(e, p, j):
                n = e * BLOCKS + j
                pe.wait_ge(i_lo, n + 1)
                if not (isinstance(n, int) and n < 2):
                    pe.wait_ge(y_up, n - 1)
                w = [x[:, p, 2].rearrange("p k i -> p (k i)") for x in (wh, wl)]
                for i in range(NB):
                    r = slice(i * P, (i + 1) * P)
                    last = product(pe, psY[j % 2][:, i, :], (ih[:, j % 2, r], il[:, j % 2, r]), w, True, True)
                last.then_inc(y_done, 1)

            def body(e, p):
                for j in range(BLOCKS):
                    up(e, p, j)
                    if j:
                        down(e, p, j - 1)
                    elif not (isinstance(e, int) and e == 0):
                        down(e - 1, 1 - p, BLOCKS - 1)

            pe.sem_inc(y_done, 1)
            body(0, 0)
            with pe.Fori(0, (EX - 1) // 2) as h:
                body(h * 2 + 1, 1)
                body(h * 2 + 2, 0)
            down(EX - 1, 0, BLOCKS - 1)


def gated_mix__experts__attend__gated_experts(nc, A, out):
    X2, XN = (nc.dram_tensor(n, (ROWS, D), F32, kind="Internal").ap() for n in ("x2_rows", "xn_rows"))
    X3 = nc.dram_tensor("x3_rows", (B * S, D), F32, kind="Internal").ap()
    VB = nc.dram_tensor("bias_by_distance", (HEADS, P, 2 * P), F32, kind="Internal").ap()
    with ExitStack() as ctx:
        m = Space(nc, ctx, "const")
        C = {n: m.sb(n, [P, P]) for n in ("ident", "ones", "tri", "gsum")}
        C["gate"] = m.sb("gate", [P, 4])
        C["eps"] = m.sb("eps", [P, 1])
        setup(nc, A, C)
        with ExitStack() as first:
            m0 = Space(nc, first, "layer0")
            C["logits0"] = m0.sb("logits0", [P, B, E0])
            C["slot_row"] = m0.sb("slot_row", [SLOTS, E0, PARTS], I32)
            C["slot_weight"] = m0.sb("slot_weight", [SLOTS, E0, PARTS])
            mix(nc, A, C, X2, XN)
            route(nc, C)
            experts(nc, A, C, X2, XN)
        attend(nc, A, C, X2, X3, VB)
        C["logits1"] = m.sb("logits1", [P, B, E1])
        C["weight1"] = m.sb("weight1", [P, B, E1 + 1])
        acc = m.sb("acc", [P, B, D])
        xth, xtl = (m.sb(n, [P, KD, B * P], F32R) for n in ("xth", "xtl"))
        gated_in(nc, A, C, X3, acc, xth, xtl)
        gated_route(nc, A, C)
        gated(nc, A, C, acc, xth, xtl, out)


def layouts(i):
    def blocks(w):
        return w.transpose(0, 2, 1).reshape(E1 + 1, KD, P, I1).transpose(0, 2, 1, 3)

    def with_shared(name, shared):
        return np.concatenate([np.asarray(i[name]), np.asarray(i[shared])[None]])

    gate = with_shared("L1_ffn_gate_proj", "L1_ffn_shared_gate_w")
    up = with_shared("L1_ffn_up_proj", "L1_ffn_shared_up_w")
    down = with_shared("L1_ffn_down_proj", "L1_ffn_shared_down_w")
    down = down.transpose(0, 2, 1).reshape(E1 + 1, I1, KD, P)
    arrays = {
        "x": i["x"], "ctx_1024": i["ctx_1024"], "g_xattn": i["g_xattn"], "g_ffn": i["g_ffn"],
        "Wt": i["L0_xattn_Wt"], "WpT": np.asarray(i["L0_xattn_Wp"]).T, "WgT": np.asarray(i["L0_xattn_Wg"]).T,
        "WzT": np.asarray(i["L0_xattn_Wz"]).transpose(0, 2, 1).reshape(GROUPS * GROUP, GROUP),
        "gamma": i["L0_xattn_gamma"], "beta": i["L0_xattn_beta"],
        "wr": i["L0_ffn_w_router"], "wi": i["L0_ffn_wi"], "wo": i["L0_ffn_wo"],
        "Wq": i["L1_xattn_Wq"], "Wk": i["L1_xattn_Wk"], "Wv": i["L1_xattn_Wv"], "Wo": i["L1_xattn_Wo"],
        "relT": np.asarray(i["L1_xattn_rel_bias"]).T, "hot": bucket_onehot(),
        "mask": np.asarray(i["mask_1x1xSxS2_bk0"]).reshape(S, S),
        "gwT": np.asarray(i["L1_ffn_gate_w"]).T, "ebias": i["L1_ffn_e_bias"],
        "gex": np.stack([blocks(gate), blocks(up), down], 2).reshape(E1 + 1, P, 3 * KD * I1),
    }
    return {n: np.ascontiguousarray(a) for n, a in arrays.items()}


def kernel(**inputs):
    import concourse.bacc as bacc
    from concourse.bass_utils import run_bass_kernel_spmd

    nc = bacc.Bacc("TRN2", target_bir_lowering=False, num_devices=1)
    laid = layouts(inputs)
    A = {n: nc.dram_tensor(f"in_{n}_dram", a.shape, mybir.dt.from_np(a.dtype), kind="ExternalInput").ap() for n, a in laid.items()}
    out = nc.dram_tensor("out_0_dram", (B, S, D), F32, kind="ExternalOutput").ap()
    gated_mix__experts__attend__gated_experts(nc, A, out)
    r = run_bass_kernel_spmd(nc, [{f"in_{n}_dram": a for n, a in laid.items()}], core_ids=[0])
    return r.results[0]["out_0_dram"]
```

```python
from contextlib import ExitStack

import numpy as np
import concourse.bass as bass
from concourse import mybir

F32 = mybir.dt.float32
F32R = mybir.dt.float32r
BF16 = mybir.dt.bfloat16
I32 = mybir.dt.int32
ALU = mybir.AluOpType
ACT = mybir.ActivationFunctionType
AX = mybir.AxisListType

P = 128
B, S, D = 32, 128, 256
KD = D // P
EPS = 1e-5
LOWEST = -3.4028234663852886e38

GROUPS, GROUP = 8, 16
E0, F0, CAP = 8, 1024, 160
HALVES = 2
TILES = B // HALVES
SLOTS = 80
PARTS = HALVES * (CAP // SLOTS)
DUMMY = B * S
ROWS = B * S + P
HEADS, DH = 16, 64
PAIRS = HEADS // 2
E1, I1, TOP = 16, 128, 4


class Chain:

    def __init__(self, eng, sem, length):
        self.eng, self.sem, self.length, self.count, self.base = eng, sem, length, 0, 0

    def start(self, step):
        self.base, self.count = step * self.length, 0

    def __call__(self, ins):
        self.count += 1
        ins.then_inc(self.sem, 1)
        self.eng.wait_ge(self.sem, self.base + self.count)

    def end(self):
        assert self.count == self.length, (self.count, self.length)


def rows(t):
    return t.rearrange("p a b -> p (a b)")


def stand(eng, sem):
    eng.sem_inc(sem, 1)


def product(pe, out, weights, moving, first, last):
    (wh, wl), (mh, ml) = weights, moving
    pe.matmul(out, wl, mh, start=first, stop=False)
    pe.matmul(out, wh, ml, start=False, stop=False)
    return pe.matmul(out, wh, mh, start=False, stop=last)


class Space:

    def __init__(self, nc, ctx, tag):
        self.nc, self.ctx, self.tag = nc, ctx, tag

    def sb(self, name, shape, dt=F32):
        return self.ctx.enter_context(self.nc.sbuf_tensor(f"{self.tag}_{name}", shape, dt))

    def ps(self, name, shape, dt=F32):
        return self.ctx.enter_context(self.nc.psum_tensor(f"{self.tag}_{name}", shape, dt))

    def sem(self, name):
        return self.ctx.enter_context(self.nc.semaphore(f"{self.tag}_{name}"))


def setup(nc, A, C):
    with ExitStack() as ctx:
        m = Space(nc, ctx, "setup")
        made, gates_in, gates_up, zeroed = (m.sem(n) for n in ("made", "gates_in", "gates_up", "zeroed"))
        graw = m.sb("graw", [P, 4])
        block = ctx.enter_context(nc.Block())

        @block.sync
        def _(sp):
            sp.dma_start(graw[:, 0:2], A["g_xattn"].rearrange("(a n) -> a n", a=1).to_broadcast((P, 2))).then_inc(gates_in, 16)
            sp.dma_start(graw[:, 2:4], A["g_ffn"].rearrange("(a n) -> a n", a=1).to_broadcast((P, 2))).then_inc(gates_in, 16)
            sp.wait_ge(gates_in, 32)

        @block.scalar
        def _(act):
            act.wait_ge(gates_in, 32)
            nc.scalar.activation(C["gate"][:], graw[:], ACT.Tanh).then_inc(gates_up, 1)
            act.wait_ge(gates_up, 1)

        @block.vector
        def _(dve):
            nc.vector.memset(C["eps"][:], EPS).then_inc(zeroed, 1)
            dve.wait_ge(zeroed, 1)

        @block.gpsimd
        def _(pool):
            nc.gpsimd.memset(C["ident"][:], 0.0)
            nc.gpsimd.memset(C["ones"][:], 1.0)
            nc.gpsimd.memset(C["tri"][:], 1.0)
            nc.gpsimd.memset(C["gsum"][:], 1.0 / GROUP).then_inc(made, 1)
            pool.wait_ge(made, 1)
            nc.gpsimd.affine_select(out=C["ident"][:], in_=C["ident"][:], compare_op=ALU.not_equal, fill=1.0,
                                    base=0, pattern=[[-1, P]], channel_multiplier=1)
            nc.gpsimd.affine_select(out=C["tri"][:], in_=C["tri"][:], compare_op=ALU.is_ge, fill=0.0,
                                    base=0, pattern=[[1, P]], channel_multiplier=-1)
            g = C["gsum"].rearrange("p (a b) -> p a b", b=GROUP)
            nc.gpsimd.affine_select(out=g, in_=g, compare_op=ALU.is_ge, fill=0.0,
                                    base=0, pattern=[[-GROUP, GROUPS], [0, GROUP]], channel_multiplier=1).then_inc(made, 1)
            pool.wait_ge(made, 2)
            nc.gpsimd.affine_select(out=g, in_=g, compare_op=ALU.is_ge, fill=0.0,
                                    base=GROUP - 1, pattern=[[GROUP, GROUPS], [0, GROUP]], channel_multiplier=-1).then_inc(made, 1)
            pool.wait_ge(made, 3)


def mix(nc, A, C, X2, XN):
    STEPS, NB = B // 4, 4
    W = NB * D
    with ExitStack() as ctx:
        m = Space(nc, ctx, "mix")
        sb, ps, sem = m.sb, m.ps, m.sem
        bdz = sb("bdz", [P, P])
        wt = sb("wt", [P, P])
        wraw = sb("wraw", [P, 3, P])
        wh = sb("wh", [P, 3, P], F32R)
        wl = sb("wl", [P, 3, P], F32R)
        wr = sb("wr", [P, KD, E0])
        gb = sb("gb", [P, 2])
        gbt = sb("gbt", [P, 2])
        xin = sb("xin", [P, 2, NB, D])
        cin = sb("cin", [P, 2, NB, D])
        xnf = sb("xnf", [P, 2, W])
        xh = sb("xh", [P, 2, W], F32R)
        xl = sb("xl", [P, 2, W], F32R)
        ch = sb("ch", [P, 2, W], F32R)
        cl = sb("cl", [P, 2, W], F32R)
        stat = sb("stat", [P, NB, 6])
        mv = sb("mv", [P, 2, NB, 2])
        sd = sb("sd", [P, 2, NB])
        rs = sb("rs", [P, NB])
        gs = sb("gs", [P, W])
        junk = sb("junk", [P, W])
        ustat = sb("ustat", [P, NB, 6])
        umv = sb("umv", [P, NB, 2])
        q = sb("q", [P, 3, NB])
        s3 = sb("s3", [P, 3, NB])
        t1 = sb("t1", [P, NB])
        t2 = sb("t2", [P, NB])
        va = sb("va", [P, NB])
        sdu = sb("sdu", [P, NB])
        ab = sb("ab", [P, 2, NB])
        w = sb("w", [P, W])
        z = sb("z", [P, W])
        x1 = sb("x1", [P, 2, W])
        stat2 = sb("stat2", [P, NB, 6])
        mv2 = sb("mv2", [P, NB, 2])
        sd2 = sb("sd2", [P, NB])
        rs2 = sb("rs2", [P, NB])
        xn = sb("xn", [P, 2, W])
        xt = sb("xt", [P, NB * KD, P])
        zero = sb("zero", [P, D])
        psP, psG, psU = (ps(n, [P, W]) for n in ("psP", "psG", "psU"))
        psS = ps("psS", [P, 512])
        psT = ps("psT", [P, 512])

        w_in, bd_zero, w_up, w2_made, w_split, gbt_up = (sem(n) for n in ("w_in", "bd_zero", "w_up", "w2_made", "w_split", "gbt_up"))
        in_ready = [sem(f"in_ready{p}") for p in range(2)]
        in_free, var1, sd1_ready, xn_ready, hi_ready, lo_ready = (sem(n) for n in ("in_free", "var1", "sd1_ready", "xn_ready", "hi_ready", "lo_ready"))
        g_done, p_done, u_done, gs_ready, p_used, u_used = (sem(n) for n in ("g_done", "p_done", "u_done", "gs_ready", "p_used", "u_used"))
        q_ready, s_ready, va_ready, sdu_ready, ab_ready, w_ready = (sem(n) for n in ("q_ready", "s_ready", "va_ready", "sdu_ready", "ab_ready", "w_ready"))
        x1_ready, var2, sd2_ready, xn2_ready = (sem(n) for n in ("x1_ready", "var2", "sd2_ready", "xn2_ready"))
        lg_copied = sem("lg_copied")
        t_done, t_used, l_done = (sem(n) for n in ("t_done", "t_used", "l_done"))
        stored = [sem(f"stored{p}") for p in range(2)]
        zeros_up, dummies = sem("zeros_up"), sem("dummies")
        s_front, s_back, stood, stood_pool, c_high = (sem(n) for n in ("s_front", "s_back", "stood", "stood_pool", "c_high"))
        block = ctx.enter_context(nc.Block())

        x_d = A["x"].rearrange("b p d -> p b d")
        c_d = A["ctx_1024"].rearrange("b p d -> p b d")
        x2_d = X2[0:B * S, :].rearrange("(b p) d -> p b d", p=P)
        xn_d = XN[0:B * S, :].rearrange("(b p) d -> p b d", p=P)

        def over_steps(front, back):
            front(0, 0, 0)
            back(0, 0, 0, (1, 1, 0))

            def pair(h):
                back(h * 2 - 1, 1, h - 1, (h * 2, 0, h))
                back(h * 2, 0, h, (h * 2 + 1, 1, h))
            return pair, lambda: back(STEPS - 1, 1, STEPS // 2 - 1, None)

        @block.sync
        def _(sp):
            sp.dma_start(wt[:], A["Wt"]).then_inc(w_in, 16)
            sp.dma_start(wraw[:, 0, :], A["WpT"]).then_inc(w_in, 16)
            sp.dma_start(wraw[:, 1, :], A["WgT"]).then_inc(w_in, 16)
            sp.dma_start(wr[:], A["wr"].rearrange("(k p) e -> p k e", p=P)).then_inc(w_in, 16)
            sp.dma_start(gb[:, 0:1], A["gamma"].rearrange("(p a) -> p a", a=1)).then_inc(w_in, 16)
            sp.dma_start(gb[:, 1:2], A["beta"].rearrange("(p a) -> p a", a=1)).then_inc(w_in, 16)
            sp.wait_ge(bd_zero, 1)
            for g in range(GROUPS):
                r = slice(g * GROUP, (g + 1) * GROUP)
                sp.dma_start(bdz[r, r], A["WzT"][r, :]).then_inc(w_in, 16)

            def front(n, p, h):
                sp.wait_ge(in_free, n + 1)
                sp.dma_start(xin[:, p], x_d[:, bass.ds(n * NB, NB), :]).then_inc(in_ready[p], 16)
                sp.dma_start(cin[:, p], c_d[:, bass.ds(n * NB, NB), :]).then_inc(in_ready[p], 16)

            with sp.Fori(0, STEPS // 2) as h:
                front(h * 2, 0, h)
                front(h * 2 + 1, 1, h)
            sp.wait_ge(zeros_up, 1)
            sp.dma_start(X2[DUMMY:ROWS, :], zero[:]).then_inc(dummies, 16)
            sp.dma_start(XN[DUMMY:ROWS, :], zero[:]).then_inc(dummies, 16)
            sp.wait_ge(dummies, 32)

        @block.gpsimd
        def _(pool):
            nc.gpsimd.memset(zero[:], 0.0).then_inc(zeros_up, 1)
            pool.wait_ge(w_up, 1)
            nc.gpsimd.tensor_tensor(wl[:], wraw[:], wh[:], ALU.subtract).then_inc(w_split, 1)

            def split(n, p, h):
                pool.wait_ge(in_ready[p], h * 32 + 32)
                pool.wait_ge(p_done, n + 1)
                stand(pool, stood_pool)
                nc.gpsimd.tensor_copy(ch[:, p], rows(cin[:, p])).then_inc(c_high, 1)
                pool.wait_ge(c_high, n + 1)
                nc.gpsimd.tensor_tensor(cl[:, p], rows(cin[:, p]), ch[:, p], ALU.subtract).then_inc(lo_ready, 1)
                pool.wait_ge(hi_ready, n + 1)
                nc.gpsimd.tensor_tensor(xl[:, p], xnf[:, p], xh[:, p], ALU.subtract).then_inc(lo_ready, 1)

            with pool.Fori(0, STEPS // 2) as h:
                split(h * 2, 0, h)
                split(h * 2 + 1, 1, h)

        @block.scalar
        def _(act):
            act.wait_ge(w2_made, 1)
            act.wait_ge(w_in, 16 * (6 + GROUPS))
            nc.scalar.activation(wraw[:, 2, :], psS[:, 0:P], ACT.Copy).then_inc(gbt_up, 1)
            act.wait_ge(gbt_up, 1)
            nc.scalar.activation(wh[:], wraw[:], ACT.Copy).then_inc(w_up, 1)
            nc.scalar.activation(gbt[:], gb[:], ACT.Copy, scale=C["gate"][:, 0:1]).then_inc(gbt_up, 1)
            act.sem_inc(gs_ready, 1)
            act.sem_inc(w_ready, 1)
            act.sem_inc(t_used, 1)

            def deviation(n, p, h):
                act.wait_ge(var1, n + 1)
                nc.scalar.activation(sd[:, p], mv[:, p, :, 1], ACT.Sqrt, bias=C["eps"][:]).then_inc(sd1_ready, 1)

            def x_high(n, p, h):
                act.wait_ge(xn_ready, n + 1)
                act.wait_ge(p_done, n + 1)
                nc.scalar.activation(xh[:, p], xnf[:, p], ACT.Copy).then_inc(hi_ready, 1)

            def g_out(n, p, h):
                act.wait_ge(g_done, n + 1)
                act.wait_ge(p_used, n + 1)
                nc.scalar.activation(gs[:], psG[:], ACT.Copy).then_inc(gs_ready, 1)

            def front(n, p, h):
                deviation(n, p, h)
                x_high(n, p, h)
                g_out(n, p, h)

            def back(n, p, h, ahead):
                if ahead:
                    deviation(*ahead)
                act.wait_ge(va_ready, n + 1)
                nc.scalar.activation(sdu[:], va[:], ACT.Sqrt, bias=C["eps"][:]).then_inc(sdu_ready, 1)
                act.wait_ge(ab_ready, n + 1)
                for j in range(NB):
                    last = nc.scalar.activation(w[:, j * D:(j + 1) * D], psU[:, j * D:(j + 1) * D], ACT.Identity,
                                                bias=ab[:, 1, j:j + 1], scale=ab[:, 0, j:j + 1])
                last.then_inc(w_ready, 1)
                if ahead:
                    x_high(*ahead)
                act.wait_ge(var2, n + 1)
                nc.scalar.activation(sd2[:], mv2[:, :, 1], ACT.Sqrt, bias=C["eps"][:]).then_inc(sd2_ready, 1)
                act.wait_ge(x1_ready, n + 1)
                act.dma_start(x2_d[:, bass.ds(n * NB, NB), :], x1[:, p].rearrange("p (a b) -> p a b", b=D)).then_inc(stored[p], 16)
                if ahead:
                    g_out(*ahead)
                for r in range(KD):
                    act.wait_ge(t_done, n * 2 + (r + 1))
                    if r == 0:
                        act.wait_ge(l_done, n + 1)
                    nc.scalar.activation(rows(xt[:, r * NB:(r + 1) * NB, :]), psT[:], ACT.Copy).then_inc(t_used, 1)
                act.wait_ge(xn2_ready, n + 1)
                act.dma_start(xn_d[:, bass.ds(n * NB, NB), :], xn[:, p].rearrange("p (a b) -> p a b", b=D)).then_inc(stored[p], 16)

            pair, last_back = over_steps(front, back)
            with act.Fori(1, STEPS // 2) as h:
                pair(h)
            last_back()
            for p in range(2):
                act.wait_ge(stored[p], 32 * (STEPS // 2) + 16)

        @block.vector
        def _(dve):
            nc.vector.memset(bdz[:], 0.0).then_inc(bd_zero, 1)
            dve.sem_inc(in_free, 2)
            dve.sem_inc(p_used, 1)
            for p in range(2):
                dve.sem_inc(stored[p], 16)
            dve.wait_ge(gbt_up, 2)
            fchain, bchain = Chain(dve, s_front, 2), Chain(dve, s_back, 12)

            def x_stats(n, p, h):
                fchain.start(n)
                dve.wait_ge(in_ready[p], h * 32 + 32)
                for j in range(NB):
                    last = nc.vector.bn_stats(stat[:, j, :], xin[:, p, j, :])
                fchain(last)
                stand(dve, stood)
                for j in range(NB):
                    last = nc.vector.bn_aggr(mv[:, p, j, :], stat[:, j, :])
                last.then_inc(var1, 1)

            def x_norm(n, p, h):
                dve.wait_ge(sd1_ready, n + 1)
                fchain(nc.vector.reciprocal(rs[:], sd[:, p]))
                for j in range(NB):
                    last = nc.vector.tensor_scalar(xnf[:, p, j * D:(j + 1) * D], xin[:, p, j, :], mv[:, p, j, 0:1],
                                                   rs[:, j:j + 1], ALU.subtract, ALU.mult)
                last.then_inc(xn_ready, 1)
                fchain.end()

            def front(n, p, h):
                x_stats(n, p, h)
                x_norm(n, p, h)

            def logits(n):
                dve.wait_ge(l_done, n + 2)
                nc.vector.tensor_copy(C["logits0"][:, bass.ds(n * NB, NB), :],
                                      psS[:, 64:64 + NB * E0].rearrange("p (a b) -> p a b", b=E0)).then_inc(lg_copied, 1)

            def back(n, p, h, ahead):
                c = bchain
                c.start(n)
                dve.wait_ge(u_done, n + 1)
                for j in range(NB):
                    last = nc.vector.bn_stats(ustat[:, j, :], psU[:, j * D:(j + 1) * D])
                c(last)
                stand(dve, stood)
                for j in range(NB):
                    last = nc.vector.bn_aggr(umv[:, j, :], ustat[:, j, :])
                c(last)
                dve.wait_ge(p_done, n + 3)
                dve.wait_ge(gs_ready, n + 2)
                for j in range(NB):
                    last = nc.vector.tensor_tensor_reduce(junk[:, j * D:(j + 1) * D], psP[:, j * D:(j + 1) * D], gs[:, j * D:(j + 1) * D], 1.0, 0.0,
                                                          ALU.mult, ALU.add, q[:, 0, j:j + 1])
                last.then_inc(p_used, 1)
                if not isinstance(n, int) or n >= 1:
                    logits(n - 1)
                nc.vector.tensor_copy(q[:, 1, :], umv[:, :, 0])
                c(nc.vector.tensor_tensor(t1[:], umv[:, :, 0], umv[:, :, 0], ALU.mult))
                nc.vector.tensor_tensor(q[:, 2, :], umv[:, :, 1], t1[:], ALU.add).then_inc(q_ready, 1)
                if ahead:
                    x_stats(*ahead)
                dve.wait_ge(s_ready, n + 1)
                c(nc.vector.tensor_copy(s3[:], psS[:, 0:3 * NB].rearrange("p (a b) -> p a b", b=NB)))
                nc.vector.scalar_tensor_tensor(t1[:], s3[:, 0, :], 4.0, s3[:, 0, :], ALU.mult, ALU.mult)
                c(nc.vector.tensor_tensor(t2[:], s3[:, 1, :], s3[:, 1, :], ALU.mult))
                c(nc.vector.tensor_tensor(t2[:], s3[:, 2, :], t2[:], ALU.subtract))
                nc.vector.tensor_tensor(va[:], t1[:], t2[:], ALU.mult).then_inc(va_ready, 1)
                nc.vector.scalar_tensor_tensor(z[:], cin[:, p].rearrange("p a b -> p (a b)"), C["gate"][:, 0:1],
                                               xin[:, p].rearrange("p a b -> p (a b)"), ALU.mult, ALU.add).then_inc(in_free, 1)
                dve.wait_ge(sdu_ready, n + 1)
                c(nc.vector.reciprocal(t1[:], sdu[:]))
                c(nc.vector.scalar_tensor_tensor(t2[:], s3[:, 0, :], 2.0, t1[:], ALU.mult, ALU.mult))
                c(nc.vector.tensor_scalar(ab[:, 0, :], t2[:], gbt[:, 0:1], None, ALU.mult))
                c(nc.vector.tensor_tensor(t1[:], ab[:, 0, :], s3[:, 1, :], ALU.mult))
                nc.vector.tensor_scalar(ab[:, 1, :], t1[:], -1.0, gbt[:, 1:2], ALU.mult, ALU.add).then_inc(ab_ready, 1)
                if ahead:
                    x_norm(*ahead)
                dve.wait_ge(w_ready, n + 2)
                dve.wait_ge(in_free, n + 3)
                dve.wait_ge(stored[p], h * 32 + 16)
                nc.vector.tensor_tensor(x1[:, p], z[:], w[:], ALU.add).then_inc(x1_ready, 1)
                dve.wait_ge(x1_ready, n + 1)
                for j in range(NB):
                    last = nc.vector.bn_stats(stat2[:, j, :], x1[:, p, j * D:(j + 1) * D])
                c(last)
                stand(dve, stood)
                for j in range(NB):
                    last = nc.vector.bn_aggr(mv2[:, j, :], stat2[:, j, :])
                last.then_inc(var2, 1)
                dve.wait_ge(sd2_ready, n + 1)
                c(nc.vector.reciprocal(rs2[:], sd2[:]))
                for j in range(NB):
                    last = nc.vector.tensor_scalar(xn[:, p, j * D:(j + 1) * D], x1[:, p, j * D:(j + 1) * D], mv2[:, j, 0:1],
                                                   rs2[:, j:j + 1], ALU.subtract, ALU.mult)
                last.then_inc(xn2_ready, 1)
                c.end()

            pair, last_back = over_steps(front, back)
            with dve.Fori(1, STEPS // 2) as h:
                pair(h)
            last_back()
            logits(STEPS - 1)
            dve.wait_ge(lg_copied, STEPS)

        @block.tensor
        def _(pe):
            pe.sem_inc(p_done, 2)
            pe.sem_inc(l_done, 1)
            pe.wait_ge(w_in, 16 * (6 + GROUPS))
            nc.tensor.matmul(psS[:, 0:P], wt[:], bdz[:], start=True, stop=True).then_inc(w2_made, 1)
            pe.wait_ge(w_split, 1)

            def products(n, p, h):
                def into(out, k, high, low, done):
                    for half in range(W // 512):
                        r = slice(half * 512, half * 512 + 512)
                        last = product(pe, out[:, r], (wh[:, k, :], wl[:, k, :]), (high[:, p, r], low[:, p, r]), True, True)
                    last.then_inc(done, 1)

                pe.wait_ge(lo_ready, n * 2 + 1)
                pe.wait_ge(gs_ready, n + 1)
                into(psG, 1, ch, cl, g_done)
                pe.wait_ge(w_ready, n + 1)
                into(psU, 2, ch, cl, u_done)
                pe.wait_ge(lo_ready, n * 2 + 2)
                pe.wait_ge(p_used, n + 1)
                into(psP, 0, xh, xl, p_done)

            def group_sums(n):
                pe.wait_ge(q_ready, n + 1)
                nc.tensor.matmul(psS[:, 0:3 * NB], C["gsum"][:], q[:].rearrange("p a b -> p (a b)"), start=True, stop=True).then_inc(s_ready, 1)

            def back(n, p, h, ahead):
                group_sums(n)
                if ahead:
                    products(*ahead)
                pe.wait_ge(xn2_ready, n + 1)
                for r in range(KD):
                    pe.wait_ge(t_used, n * 2 + (r + 1))
                    for j in range(NB):
                        last = nc.tensor.transpose(psT[:, j * P:(j + 1) * P], xn[:, p, j * D + r * P:j * D + (r + 1) * P], C["ident"][:])
                    last.then_inc(t_done, 1)
                pe.wait_ge(t_used, n * 2 + 3)
                for j in range(NB):
                    for r in range(KD):
                        last = nc.tensor.matmul(psS[:, 64 + j * E0:64 + (j + 1) * E0], xt[:, r * NB + j, :], wr[:, r, :],
                                                start=(r == 0), stop=(r == KD - 1))
                last.then_inc(l_done, 1)

            pair, last_back = over_steps(products, back)
            with pe.Fori(1, STEPS // 2) as h:
                pair(h)
            last_back()


def first_of(nc, link, values, best, rank, work, top, mask):
    n = values.shape[-1]
    link(nc.vector.tensor_tensor(work, values, best.unsqueeze(2).to_broadcast(values.shape), ALU.is_equal))
    link(nc.vector.tensor_tensor(work, work, rank.unsqueeze(1).to_broadcast(values.shape), ALU.mult))
    link(nc.vector.tensor_reduce(top, work, AX.X, ALU.max))
    return nc.vector.tensor_tensor(mask, work, top.unsqueeze(2).to_broadcast(values.shape), ALU.is_equal)


def route(nc, C, held):
    NI = HALVES * 2 * TILES
    MK = HALVES * E0 * 2 * TILES
    V = 5
    with ExitStack() as ctx:
        m = Space(nc, ctx, "route")
        sb, ps, sem = m.sb, m.ps, m.sem
        lg = C["logits0"]
        mx = sb("mx", [P, B])
        pr = sb("pr", [P, B, E0])
        sm = sb("sm", [P, B])
        best = sb("best", [P, 2, B])
        work = sb("work", [P, B, E0])
        top = sb("top", [P, B])
        mask = sb("mask", [P, 2, B, E0])
        p2 = sb("p2", [P, B, E0])
        rank = sb("rank", [P, E0])
        mk = sb("mk", [P, HALVES, E0, 2, TILES])
        reset = sb("reset", [P, HALVES * E0, 2 * TILES])
        tot = sb("tot", [P, MK])
        upto = sb("upto", [P, MK])
        pos = sb("pos", [P, HALVES, E0, 2, TILES])
        posk = sb("posk", [P, HALVES, 2, TILES])
        parts = sb("parts", [P, 3, NI], BF16)
        rest = sb("rest", [P, 2, NI])
        gk = sb("gk", [P, HALVES, 2, TILES])
        tileno = sb("tileno", [P, HALVES, 2, TILES])
        rowno = sb("rowno", [P, 1])
        val = sb("val", [P, V, NI], BF16)
        rhs = sb("rhs", [P, NI, E0, V], BF16)
        place = sb("place", [P, CAP])
        onehot = sb("onehot", [P, NI, CAP], BF16)
        tab = sb("tab", [SLOTS, PARTS, E0, V])
        free = sb("free", [SLOTS, 1])
        nfree = sb("nfree", [SLOTS, 1])
        f = sb("f", [SLOTS, PARTS, E0])
        ix = sb("ix", [SLOTS, PARTS, E0])
        psC, psN = ps("psC", [P, MK]), ps("psN", [P, MK])
        psTab = ps("psTab", [SLOTS, PARTS, E0 * V])
        iotas, l_sub, e_up, mk_up, counted, hot, tabled, step = (sem(n) for n in ("iotas", "l_sub", "e_up", "mk_up", "counted", "hot", "tabled", "step"))
        held.stage(ctx)
        block = ctx.enter_context(nc.Block())

        @block.gpsimd
        def _(pool):
            small = dict(allow_small_or_imprecise_dtypes=True)
            nc.gpsimd.iota(rank[:], [[-1, E0]], base=E0, channel_multiplier=0, **small)
            nc.gpsimd.iota(place[:], [[1, CAP]], base=0, channel_multiplier=0, **small)
            nc.gpsimd.iota(tileno[:], [[TILES, HALVES], [0, 2], [1, TILES]], base=1, channel_multiplier=0, **small)
            nc.gpsimd.iota(rowno[:], [[0, 1]], base=0, channel_multiplier=1, **small)
            nc.gpsimd.iota(free[:], [[0, 1]], base=DUMMY, channel_multiplier=1, **small)
            nc.gpsimd.iota(nfree[:], [[0, 1]], base=-DUMMY - P, channel_multiplier=-1, **small)
            nc.gpsimd.memset(reset[:], 1.0).then_inc(iotas, 1)
            pool.wait_ge(iotas, 1)
            nc.gpsimd.memset(reset[:, :, 0:1], 0.0).then_inc(iotas, 1)
            pool.wait_ge(iotas, 2)
            held.gpsimd(pool)

        @block.sync
        def _(sp):
            held.sync(sp)

        @block.scalar
        def _(act):
            act.wait_ge(l_sub, 1)
            nc.scalar.activation(pr[:], pr[:], ACT.Exp).then_inc(e_up, 1)
            held.scalar(act)

        @block.tensor
        def _(pe):
            held.tensor(pe)
            pe.wait_ge(mk_up, 1)
            flat = mk[:].rearrange("p h e k t -> p (h e k t)")
            nc.tensor.matmul(psC[:], C["tri"][:], flat, start=True, stop=True)
            nc.tensor.matmul(psN[:], C["ones"][:], flat, start=True, stop=True).then_inc(counted, 1)
            pe.wait_ge(hot, 4)
            for h in range(HALVES):
                for part in range(CAP // SLOTS):
                    for i in range(2 * TILES):
                        n = h * 2 * TILES + i
                        last = nc.tensor.matmul(psTab[:, h * (CAP // SLOTS) + part, :], onehot[:, n, part * SLOTS:(part + 1) * SLOTS],
                                                rhs[:, n].rearrange("p e v -> p (e v)"), start=(i == 0), stop=(i == 2 * TILES - 1))
            last.then_inc(tabled, 1)

        @block.vector
        def _(dve):
            link = Chain(dve, step, 0)
            bc = lambda a: a.unsqueeze(2).to_broadcast([P, B, E0])
            v = nc.vector
            dve.wait_ge(iotas, 2)
            link(v.tensor_reduce(mx[:], lg[:], AX.X, ALU.max))
            v.tensor_tensor(pr[:], lg[:], bc(mx[:]), ALU.subtract).then_inc(l_sub, 1)
            dve.wait_ge(e_up, 1)
            link(v.tensor_reduce(sm[:], pr[:], AX.X, ALU.add))
            link(v.reciprocal(sm[:], sm[:]))
            link(v.tensor_tensor(pr[:], pr[:], bc(sm[:]), ALU.mult))
            link(v.tensor_reduce(best[:, 0, :], pr[:], AX.X, ALU.max))
            link(first_of(nc, link, pr[:], best[:, 0, :], rank[:], work[:], top[:], mask[:, 0]))
            link(v.scalar_tensor_tensor(rows(p2), rows(mask[:, 0]), -2.0, rows(pr), ALU.mult, ALU.add))
            link(v.tensor_reduce(best[:, 1, :], p2[:], AX.X, ALU.max))
            link(first_of(nc, link, p2[:], best[:, 1, :], rank[:], work[:], top[:], mask[:, 1]))
            for k in range(2):
                for h in range(HALVES):
                    last = v.tensor_copy(mk[:, h, :, k, :], mask[:, k, h * TILES:(h + 1) * TILES, :].rearrange("p t e -> p e t"))
            last.then_inc(mk_up, 1)
            for k in range(2):
                last = v.tensor_copy(gk[:, :, k, :], best[:, k, :].rearrange("p (h t) -> p h t", h=HALVES))
            link(last)
            g = gk[:].rearrange("p h k t -> p (h k t)")
            link(v.tensor_copy(parts[:, 0], g))
            link(v.tensor_tensor(rest[:, 0], g, parts[:, 0], ALU.subtract))
            link(v.tensor_copy(parts[:, 1], rest[:, 0]))
            link(v.tensor_tensor(rest[:, 1], rest[:, 0], parts[:, 1], ALU.subtract))
            v.tensor_copy(val[:, 0], tileno[:].rearrange("p h k t -> p (h k t)"))
            v.tensor_copy(val[:, 1], rowno[:].to_broadcast([P, NI]))
            v.tensor_copy(val[:, 2:4], parts[:, 0:2])
            link(v.tensor_copy(val[:, 4], rest[:, 1]))
            for h in range(HALVES):
                r = slice(h * 2 * TILES, (h + 1) * 2 * TILES)
                for n in range(V):
                    last = v.tensor_tensor(rhs[:, r, :, n], mk[:, h].rearrange("p e k t -> p (k t) e"),
                                           val[:, n, r].unsqueeze(2).to_broadcast([P, 2 * TILES, E0]), ALU.mult)
            link(last)
            dve.wait_ge(counted, 1)
            link(v.tensor_copy(tot[:], psN[:]))
            link(v.tensor_tensor_scan(upto[:], reset[:].rearrange("p a b -> p (a b)"), tot[:], 0.0, ALU.mult, ALU.add))
            link(v.tensor_tensor(upto[:], upto[:], tot[:], ALU.subtract))
            flat = pos[:].rearrange("p h e k t -> p (h e k t)")
            link(v.scalar_tensor_tensor(flat, psC[:], -1.0, upto[:], ALU.add, ALU.add))
            link(v.tensor_tensor(flat, flat, mk[:].rearrange("p h e k t -> p (h e k t)"), ALU.mult))
            for h in range(HALVES):
                last = v.tensor_reduce(posk[:, h].rearrange("p k t -> p (k t)"), pos[:, h].rearrange("p e k t -> p (k t) e"), AX.X, ALU.add)
            link(last)
            pk = posk[:].rearrange("p h k t -> p (h k t)")
            for c in range(4):
                r = slice(c * NI // 4, (c + 1) * NI // 4)
                v.tensor_tensor(onehot[:, r], place[:].unsqueeze(1).to_broadcast([P, NI // 4, CAP]),
                                pk[:, r].unsqueeze(2).to_broadcast([P, NI // 4, CAP]), ALU.is_equal).then_inc(hot, 1)
            dve.wait_ge(tabled, 1)
            link(v.tensor_copy(tab[:].rearrange("p a e v -> p a (e v)"), psTab[:]))
            v.tensor_scalar(f[:], tab[:, :, :, 0], 0.0, None, ALU.is_gt)
            link(v.scalar_tensor_tensor(ix[:], tab[:, :, :, 0], float(P), tab[:, :, :, 1], ALU.mult, ALU.add))
            link(v.tensor_scalar(f[:], f[:], nfree[:], free[:], ALU.mult, ALU.add))
            link(v.tensor_tensor(ix[:], ix[:], f[:], ALU.add))
            link(v.tensor_copy(C["slot_row"][:].rearrange("p e a -> p a e"), ix[:]))
            link(v.tensor_tensor(f[:], tab[:, :, :, 4], tab[:, :, :, 3], ALU.add))
            link(v.tensor_tensor(f[:], f[:], tab[:, :, :, 2], ALU.add))
            link(v.tensor_scalar(C["slot_weight"][:].rearrange("p e a -> p a e"), f[:], C["gate"][0:SLOTS, 2:3], None, ALU.mult))


def experts(nc, A, C, X2, XN):
    N = PARTS * SLOTS
    NF = F0 // P
    with ExitStack() as ctx:
        m = Space(nc, ctx, "experts")
        sb, ps, sem = m.sb, m.ps, m.sem
        raw = sb("raw", [P, 2, 2048])
        wih = sb("wih", [P, 2, KD, F0], F32R)
        wil = sb("wil", [P, 2, KD, F0], F32R)
        woh = sb("woh", [P, 2, NF, D], F32R)
        wol = sb("wol", [P, 2, NF, D], F32R)
        row_in, row_out = (sb(n, [SLOTS, 2, PARTS], I32) for n in ("row_in", "row_out"))
        xg = sb("xg", [SLOTS, 2, PARTS, D])
        xth = sb("xth", [P, KD, N], F32R)
        xtl = sb("xtl", [P, KD, N], F32R)
        hh = sb("hh", [P, NF, N], F32R)
        hl = sb("hl", [P, NF, N], F32R)
        yg = sb("yg", [SLOTS, 2, PARTS, D])
        psX = [ps(f"psX{k}", [P, 512]) for k in range(KD)]
        psH = [ps(f"psH{k}", [P, 512]) for k in range(4)]
        psY = ps("psY", [SLOTS, PARTS, D])
        w_in = [sem("wi_in"), sem("wo_in")]
        w_hi, w_lo, row_in_up, row_out_up, stood = (sem(n) for n in ("w_hi", "w_lo", "row_in_up", "row_out_up", "stood"))
        gathered = [sem(f"gathered{p}") for p in range(2)]
        added = [sem(f"added{p}") for p in range(2)]
        xt_done, x_hi, x_lo, h_done, h_hi, h_lo, y_done, y_up = (sem(n) for n in ("xt_done", "x_hi", "x_lo", "h_done", "h_hi", "h_lo", "y_done", "y_up"))
        block = ctx.enter_context(nc.Block())
        PAIRS_OF = E0 // 2

        def over(eng, body):
            body(0, 0, 0)
            body(1, 1, 0)
            with eng.Fori(1, PAIRS_OF - 1) as h:
                body(h * 2, 0, h)
                body(h * 2 + 1, 1, h)
            body(E0 - 2, 0, PAIRS_OF - 1)

        def later(e, first):
            return not isinstance(e, int) or e >= first

        @block.sync
        def _(sp):
            def load(e, p, h):
                sp.wait_ge(w_lo, e * 2 + 1)
                sp.dma_start(raw[:, 0].rearrange("p (k f) -> p k f", k=KD), A["wi"][bass.ds(e, 1)].rearrange("a (k p) f -> p (a k) f", p=P)).then_inc(w_in[0], 16)
                sp.wait_ge(w_lo, e * 2 + 2)
                sp.dma_start(raw[:, 1].rearrange("p (k f) -> p k f", k=NF), A["wo"][bass.ds(e, 1)].rearrange("a (k p) f -> p (a k) f", p=P)).then_inc(w_in[1], 16)
            over(sp, load)
            load(E0 - 1, 1, PAIRS_OF - 1)

        @block.gpsimd
        def _(pool):
            def rows_of(e, to, up):
                nc.gpsimd.tensor_copy(to, C["slot_row"][:, bass.ds(e, 1), :].rearrange("p e a -> p (e a)")).then_inc(up, 1)
                pool.wait_ge(up, e + 1)

            def gather(e, p):
                pool.wait_ge(xt_done, e + 1)
                rows_of(e, row_in[:, p], row_in_up)
                stand(pool, stood)
                for a in range(PARTS):
                    nc.gpsimd.indirect_dma_start(out=xg[:, p, a, :], out_offset=None, in_=XN,
                                                 in_offset=bass.IndirectOffsetOnAxis(ap=row_in[:, p, a:a + 1], axis=0)).then_inc(gathered[p], 16)

            def add(e, p, h):
                if later(e, 1):
                    pool.wait_ge(added[1 - p], (h + p) * 16 * PARTS)
                rows_of(e, row_out[:, p], row_out_up)
                pool.wait_ge(y_up, e + 2)
                stand(pool, stood)
                for a in range(PARTS):
                    nc.gpsimd.indirect_dma_start(out=X2, out_offset=bass.IndirectOffsetOnAxis(ap=row_out[:, p, a:a + 1], axis=0),
                                                 in_=yg[:, p, a, :], in_offset=None, compute_op=ALU.add).then_inc(added[p], 16)

            gather(0, 0)
            gather(1, 1)

            def body(e, p, h):
                if not isinstance(e, int) or e + 2 < E0:
                    gather(e + 2, p)
                add(e, p, h)

            over(pool, body)
            add(E0 - 1, 1, PAIRS_OF - 1)
            for p in range(2):
                pool.wait_ge(added[p], PAIRS_OF * 16 * PARTS)

        @block.scalar
        def _(act):
            act.sem_inc(y_up, 1)

            def weights(e, p, h):
                act.wait_ge(y_done, e + 1)
                act.wait_ge(w_in[0], e * 16 + 16)
                nc.scalar.activation(wih[:, p].rearrange("p a b -> p (a b)"), raw[:, 0], ACT.Copy).then_inc(w_hi, 1)
                act.wait_ge(w_in[1], e * 16 + 16)
                nc.scalar.activation(woh[:, p].rearrange("p a b -> p (a b)"), raw[:, 1], ACT.Copy).then_inc(w_hi, 1)

            def x_high(e, p, h):
                act.wait_ge(xt_done, e + 3)
                for k in range(KD):
                    last = nc.scalar.activation(xth[:, k, :], psX[k][:, 0:N], ACT.Copy)
                last.then_inc(x_hi, 1)

            def relu(e, p, h):
                for n in range(NF):
                    act.wait_ge(h_done, e * NF + (n + 1))
                    nc.scalar.activation(hh[:, n, :], psH[n % 4][:, 0:N], ACT.Relu).then_inc(h_hi, 1)

            def weigh(e, p, h):
                act.wait_ge(y_done, e + 3)
                if later(e, 2):
                    act.wait_ge(added[p], h * 16 * PARTS)
                for a in range(PARTS):
                    last = nc.scalar.activation(yg[:, p, a, :], psY[:, a, :], ACT.Copy,
                                                scale=C["slot_weight"][:, bass.ds(e, 1), a:a + 1].rearrange("p e a -> p (e a)"))
                last.then_inc(y_up, 1)

            weights(0, 0, 0)
            x_high(0, 0, 0)

            def body(e, p, h):
                relu(e, p, h)
                x_high(e + 1, 1 - p, h + p)
                weights(e + 1, 1 - p, h + p)
                weigh(e, p, h)

            over(act, body)
            relu(E0 - 1, 1, PAIRS_OF - 1)
            weigh(E0 - 1, 1, PAIRS_OF - 1)

        @block.vector
        def _(dve):
            dve.sem_inc(w_lo, 2)
            dve.sem_inc(h_lo, 4)

            def weights(e, p, h):
                dve.wait_ge(w_hi, e * 2 + 1)
                nc.vector.tensor_tensor(wil[:, p].rearrange("p a b -> p (a b)"), raw[:, 0], wih[:, p].rearrange("p a b -> p (a b)"), ALU.subtract).then_inc(w_lo, 1)
                dve.wait_ge(w_hi, e * 2 + 2)
                nc.vector.tensor_tensor(wol[:, p].rearrange("p a b -> p (a b)"), raw[:, 1], woh[:, p].rearrange("p a b -> p (a b)"), ALU.subtract).then_inc(w_lo, 1)

            def x_low(e, p, h):
                dve.wait_ge(x_hi, e + 1)
                for k in range(KD):
                    last = nc.vector.tensor_tensor(xtl[:, k, :], psX[k][:, 0:N], xth[:, k, :], ALU.subtract)
                last.then_inc(x_lo, 1)

            def relu(e, p, h):
                for n in range(NF):
                    dve.wait_ge(h_hi, e * NF + (n + 1))
                    nc.vector.scalar_tensor_tensor(hl[:, n, :], psH[n % 4][:, 0:N], 0.0, hh[:, n, :], ALU.max, ALU.subtract).then_inc(h_lo, 1)

            weights(0, 0, 0)
            x_low(0, 0, 0)

            def body(e, p, h):
                relu(e, p, h)
                x_low(e + 1, 1 - p, h + p)
                weights(e + 1, 1 - p, h + p)

            over(dve, body)
            relu(E0 - 1, 1, PAIRS_OF - 1)

        @block.tensor
        def _(pe):
            pe.sem_inc(y_done, 2)
            pe.sem_inc(xt_done, 2)

            def turn(e, p, h):
                pe.wait_ge(gathered[p], (h + 1) * 16 * PARTS)
                for k in range(KD):
                    for a in range(PARTS):
                        last = nc.tensor.transpose(psX[k][:, a * SLOTS:(a + 1) * SLOTS], xg[:, p, a, k * P:(k + 1) * P], C["ident"][0:SLOTS, 0:SLOTS])
                last.then_inc(xt_done, 1)

            def up(e, p, h):
                pe.wait_ge(w_lo, e * 2 + 4)
                pe.wait_ge(x_lo, e + 1)
                for n in range(NF):
                    f = slice(n * P, (n + 1) * P)
                    pe.wait_ge(h_lo, e * NF + (n + 1))
                    for k in range(KD):
                        last = product(pe, psH[n % 4][:, 0:N], (wih[:, p, k, f], wil[:, p, k, f]), (xth[:, k, :], xtl[:, k, :]), k == 0, k == KD - 1)
                    last.then_inc(h_done, 1)

            def down(e, p, h):
                pe.wait_ge(h_lo, e * NF + (NF + 4))
                pe.wait_ge(y_up, e + 1)
                for a in range(PARTS):
                    s = slice(a * SLOTS, (a + 1) * SLOTS)
                    for n in range(NF):
                        last = product(pe, psY[:, a, :], (hh[:, n, s], hl[:, n, s]), (woh[:, p, n, :], wol[:, p, n, :]), n == 0, n == NF - 1)
                last.then_inc(y_done, 1)

            turn(0, 0, 0)

            def body(e, p, h):
                up(e, p, h)
                turn(e + 1, 1 - p, h + p)
                down(e, p, h)

            over(pe, body)
            up(E0 - 1, 1, PAIRS_OF - 1)
            down(E0 - 1, 1, PAIRS_OF - 1)


BUCKETS, MAX_DISTANCE = 32, 128


def bucket_onehot():
    exact = BUCKETS // 2
    d = np.maximum(S - 1 - np.arange(2 * S), 0)
    large = exact + (np.log(np.maximum(d, 1) / exact) / np.log(MAX_DISTANCE / exact) * (BUCKETS - exact)).astype(np.int32)
    bucket = np.where(d < exact, d, np.minimum(large, BUCKETS - 1))
    return (np.arange(BUCKETS)[:, None] == bucket[None, :]).astype(np.float32)


UNITS = 2
UB, UH = PAIRS // UNITS, HEADS // UNITS
UW = UH * P


class AttendHeld:

    def __init__(self, nc, ctx, A, VB):
        m = Space(nc, ctx, "held")
        self.nc, self.A, self.VB = nc, A, VB
        self.high = [m.sb(n, [P, 2 * HEADS * DH], F32R) for n in ("wqh", "wkh", "wvh", "woh")]
        self.low = [m.sb(n, [P, 2 * HEADS * DH], F32R) for n in ("wql", "wkl", "wvl", "wol")]
        self.bias = m.sb("bias", [P, UNITS, UW])

    def stage(self, ctx):
        m = Space(self.nc, ctx, "making")
        self.raw = [m.sb(f"raw{k}", [P, 2 * HEADS * DH]) for k in range(2)]
        self.rel = m.sb("rel", [BUCKETS, HEADS])
        self.hot = m.sb("hot", [BUCKETS, 2 * P])
        self.vb = m.sb("vb", [HEADS, 2 * P])
        self.mask8 = m.sb("mask8", [P, P], mybir.dt.uint8)
        self.mask = m.sb("mask", [P, P])
        self.psV = m.ps("psV", [P, 512])
        self.raw_in = [m.sem(f"raw_in{k}") for k in range(2)]
        self.w_hi, self.w_lo, self.rel_in, self.vb_done, self.vb_up, self.vb_out, self.bias_in, self.mask_in, self.bias_up = (
            m.sem(n) for n in ("w_hi", "w_lo", "rel_in", "vb_done", "vb_up", "vb_out", "bias_in", "mask_in", "bias_up"))

    def sync(self, sp):
        A, VB = self.A, self.VB
        sp.dma_start(self.rel[:], A["relT"]).then_inc(self.rel_in, 16)
        sp.dma_start(self.hot[:], A["hot"]).then_inc(self.rel_in, 16)
        sp.dma_start(self.mask8[:], A["mask"]).then_inc(self.mask_in, 16)
        for k, name in enumerate(("Wq", "Wk", "Wv", "Wo")):
            if k >= 2:
                sp.wait_ge(self.w_lo, k - 1)
            blocks = PAIRS if name == "Wo" else KD
            sp.dma_start(self.raw[k % 2][:].rearrange("p (k n) -> p k n", k=blocks), A[name].rearrange("(k p) n -> p k n", p=P)).then_inc(self.raw_in[k % 2], 16)
            if k == 1:
                sp.wait_ge(self.vb_up, 1)
                sp.dma_start(VB, self.vb[:].unsqueeze(1).to_broadcast([HEADS, P, 2 * P])).then_inc(self.vb_out, 16)
                sp.wait_ge(self.vb_out, 16)
                for g in range(UNITS):
                    for r in range(2):
                        sp.dma_start(self.bias[:, g, r * UW // 2:(r + 1) * UW // 2].rearrange("p (m k) -> p m k", m=UB),
                                     bass.AP(VB.tensor, VB.offset + (2 * UB * g + r) * P * 2 * P + P - 1, [[2 * P - 1, P], [2 * P * 2 * P, UB], [1, P]])).then_inc(self.bias_in, 16)

    def tensor(self, pe):
        pe.wait_ge(self.rel_in, 32)
        self.nc.tensor.matmul(self.psV[0:HEADS, 0:2 * P], self.rel[:], self.hot[:], start=True, stop=True).then_inc(self.vb_done, 1)

    def scalar(self, act):
        act.wait_ge(self.vb_done, 1)
        self.nc.scalar.activation(self.vb[:], self.psV[0:HEADS, 0:2 * P], ACT.Copy).then_inc(self.vb_up, 1)
        for k in range(4):
            act.wait_ge(self.raw_in[k % 2], 16 * (k // 2 + 1))
            self.nc.scalar.activation(self.high[k][:], self.raw[k % 2][:], ACT.Copy).then_inc(self.w_hi, 1)

    def gpsimd(self, pool):
        nc = self.nc
        for k in range(4):
            pool.wait_ge(self.w_hi, k + 1)
            nc.gpsimd.tensor_tensor(self.low[k][:], self.raw[k % 2][:], self.high[k][:], ALU.subtract).then_inc(self.w_lo, 1)
        pool.wait_ge(self.mask_in, 16)
        nc.gpsimd.tensor_copy(self.mask[:], self.mask8[:]).then_inc(self.bias_up, 1)
        pool.wait_ge(self.bias_up, 1)
        nc.gpsimd.tensor_scalar(self.mask[:], self.mask[:], -1.0, -LOWEST, ALU.add, ALU.mult).then_inc(self.bias_up, 1)
        pool.wait_ge(self.bias_up, 2)
        pool.wait_ge(self.bias_in, 16 * 2 * UNITS)
        flat = self.bias[:].rearrange("p g (a k) -> p (g a) k", k=P)
        nc.gpsimd.tensor_tensor(flat, flat, self.mask[:].unsqueeze(1).to_broadcast([P, HEADS, P]), ALU.add).then_inc(self.bias_up, 1)
        pool.wait_ge(self.bias_up, 3)
        pool.wait_ge(self.w_lo, 4)


def attend(nc, A, C, held, X2, X3):
    STEPS, NB = B // 2, 2
    N = NB * P
    W = HEADS * P
    SCALE = DH ** -0.5
    CHUNK = 8
    with ExitStack() as ctx:
        m_ = Space(nc, ctx, "attend")
        sb, ps, sem = m_.sb, m_.ps, m_.sem
        wqh, wkh, wvh, woh, wql, wkl, wvl, wol = (
            w[:].rearrange("p (k n) -> p k n", k=blocks) for half in (held.high, held.low) for w, blocks in zip(half, (KD, KD, KD, PAIRS)))
        bias = held.bias
        q_t, k_t = (sb(n, [P, 2, PAIRS, N]) for n in ("q_t", "k_t"))
        v_n = sb("v_n", [P, 2, NB, HEADS * DH])
        s, pr, pt = (sb(n, [P, UNITS, UH, P]) for n in ("s", "pr", "pt"))
        oh, ol = (sb(n, [P, PAIRS, P], F32R) for n in ("oh", "ol"))
        xin, cin = (sb(n, [P, 2, NB, D]) for n in ("xin", "cin"))
        xn = sb("xn", [P, NB, D])
        xh, xl, ch, cl = (sb(n, [P, KD, N], F32R) for n in ("xh", "xl", "ch", "cl"))
        res = sb("res", [P, 2, D])
        x3 = sb("x3", [P, 2, D])
        stat = sb("stat", [P, CHUNK, 6])
        mv = sb("mv", [P, B, 2])
        sd = sb("sd", [P, B])
        rs = sb("rs", [P, B])
        mx, less, sm, rc = (sb(n, [P, UNITS, UH]) for n in ("mx", "less", "sm", "rc"))
        psS = [ps(f"psS{g}", [P, UW]) for g in range(UNITS)]
        psO = [ps(f"psO{g}", [P, UB * P]) for g in range(UNITS)]
        psJ = [ps(f"psJ{k}", [P, 512]) for k in range(2)]

        x_in = [sem(f"x_in{k}") for k in range(2)]
        c_in = [sem(f"c_in{k}") for k in range(2)]
        res_in = [sem(f"res_in{k}") for k in range(2)]
        stored = [sem(f"stored{k}") for k in range(2)]
        j_done = [sem(f"j_done{k}") for k in range(2)]
        j_free = [sem(f"j_free{k}") for k in range(2)]
        xn_up, var, sd_up, rs_up = (sem(n) for n in ("xn_up", "var", "sd_up", "rs_up"))
        x_all = [sem(f"x_all{k}") for k in range(2)]
        x_hi, c_hi = sem("x_hi"), sem("c_hi")
        s_done, s_less, e_up, p_up, pt_done, pt_up, o_done, o_hi, o_lo = (
            sem(n) for n in ("s_done", "s_less", "e_up", "p_up", "pt_done", "pt_up", "o_done", "o_hi", "o_lo"))
        s_ln, s_soft, stood = (sem(n) for n in ("s_ln", "s_soft", "stood"))
        block = ctx.enter_context(nc.Block())

        x2_d = X2[0:B * S, :].rearrange("(b p) d -> p b d", p=P)
        x3_d = X3.rearrange("(b p) d -> p b d", p=P)
        c_d = A["ctx_1024"].rearrange("b p d -> p b d")

        Q, WO_OLD, K, V0, WO_NEW, V1, TURN = [0, 1, 2, 3], [4], [5, 6, 7, 8], [9, 10], [11], [12, 13], [14, 15]
        ALL = Q + WO_OLD + K + V0 + WO_NEW + V1 + TURN

        def uses(n):
            if n == -1:
                return [u for u in ALL if u not in WO_OLD + WO_NEW]
            if n == 0:
                return [u for u in ALL if u not in WO_OLD]
            if n == STEPS - 2:
                return [u for u in ALL if u not in TURN]
            if n == STEPS - 1:
                return WO_OLD + WO_NEW
            return WO_OLD if n == STEPS else ALL

        def uses_before(bank, n):
            return 1 + sum(u % 2 == bank for k in range(-1, n) for u in uses(k))

        def turn_of(n, u):
            bank = u % 2
            if isinstance(n, int) and n == -2:
                return 1
            at = sum(v % 2 == bank and v <= u for v in (uses(n) if isinstance(n, int) else ALL))
            if isinstance(n, int):
                return uses_before(bank, n) + at
            return (n - 1) * (len(ALL) // 2) + (uses_before(bank, 1) + at)

        def used(eng, n, u):
            eng.wait_ge(j_done[u % 2], turn_of(n, u))

        def read(eng, n, u):
            eng.wait_ge(j_free[u % 2], turn_of(n, u))

        def over(eng, body, last):
            body(0, 0, 0)
            with eng.Fori(0, (STEPS - 4) // 2) as h:
                body(h * 2 + 1, 1, h)
                body(h * 2 + 2, 0, h + 1)
            for n in range(STEPS - 3, STEPS):
                body(n, n % 2, n // 2)
            last()

        def projects(n):
            return not isinstance(n, int) or n <= STEPS - 2

        def turns(n):
            return not isinstance(n, int) or n <= STEPS - 3

        def later(n):
            return not isinstance(n, int) or n >= 1

        def staged(c):
            return (pr, s)[c % 2][:].rearrange("p g a b -> p (g a b)").rearrange("p (b d) -> p b d", b=CHUNK)

        def unit(u):
            return u[0] * UNITS + (u[1] + 1)

        @block.sync
        def _(sp):
            def load(n, p, h):
                sp.wait_ge(xn_up, n + 1)
                sp.dma_start(xin[:, p], x2_d[:, bass.ds(n * NB, NB), :]).then_inc(x_in[p], 16)
                if not isinstance(n, int) or n >= 2:
                    used(sp, n - 4, TURN[1])
                sp.dma_start(cin[:, p], c_d[:, bass.ds(n * NB, NB), :]).then_inc(c_in[p], 16)

            def residual(n, i):
                if later(n):
                    read(sp, *((n - 1, WO_NEW[0]) if i == 0 else (n, WO_OLD[0])))
                sp.dma_start(res[:, i], x2_d[:, bass.ds(n * NB + i, 1), :].rearrange("p a d -> p (a d)")).then_inc(res_in[i], 16)

            load(0, 0, 0)
            load(1, 1, 0)
            for c in range(B // CHUNK):
                if c >= 2:
                    sp.wait_ge(var, c - 1)
                sp.dma_start(staged(c), x2_d[:, c * CHUNK:(c + 1) * CHUNK, :]).then_inc(x_all[c % 2], 16)

            def body(n, p, h):
                residual(n, 0)
                if turns(n):
                    load(n + 2, p, h + 1)
                residual(n, 1)

            over(sp, body, lambda: None)

        @block.scalar
        def _(act):
            for p in range(2):
                act.sem_inc(stored[p], 16)

            def x_high(n):
                for u, to, done in ((TURN[0], xh, x_hi), (TURN[1], ch, c_hi)):
                    used(act, n, u)
                    nc.scalar.activation(to[:].rearrange("p a b -> p (a b)"), psJ[u % 2][:], ACT.Copy).then_inc(done, 1)

            def deviation(c):
                act.wait_ge(var, c + 1)
                r = slice(c * CHUNK, (c + 1) * CHUNK)
                nc.scalar.activation(sd[:, r], mv[:, r, 1], ACT.Sqrt, bias=C["eps"][:]).then_inc(sd_up, 1)

            def exps(b, g, part):
                act.wait_ge(s_less, unit((b, g)))
                for j in range(part * UH // 2, (part + 1) * UH // 2):
                    last = nc.scalar.activation(s[:, g, j, :], s[:, g, j, :], ACT.Exp, bias=less[:, g, j:j + 1], accum_out=sm[:, g, j:j + 1])
                if part == 1:
                    last.then_inc(e_up, 1)

            def evacuate(n, u, to):
                used(act, n, u)
                nc.scalar.activation(to, psJ[u % 2][:].rearrange("p (a b) -> p a b", a=to.shape[1]), ACT.Copy).then_inc(j_free[u % 2], 1)

            def qk(n, us, to, p):
                for k, u in enumerate(us):
                    evacuate(n, u, to[:, p, k * 2:k * 2 + 2, :])

            def vs(n, us, i, p):
                for k, u in enumerate(us):
                    evacuate(n, u, v_n[:, p, i:i + 1, k * 512:(k + 1) * 512])

            def p_out(b, g):
                act.wait_ge(pt_done, unit((b, g)))
                nc.scalar.activation(pt[:, g].rearrange("p a b -> p (a b)"), psS[g][:], ACT.Copy).then_inc(pt_up, 1)

            def o_high(b, g):
                act.wait_ge(o_done, unit((b, g)))
                nc.scalar.activation(oh[:, g * UB:(g + 1) * UB].rearrange("p a b -> p (a b)"), psO[g][:], ACT.Copy).then_inc(o_hi, 1)

            def store(b, n, u, i):
                read(act, n, u)
                act.dma_start(x3_d[:, bass.ds(b, 1), :].rearrange("p a d -> p (a d)"), x3[:, i]).then_inc(stored[i], 16)

            deviation(0)
            x_high(-2)
            qk(-1, Q, q_t, 0)
            qk(-1, K, k_t, 0)
            vs(-1, V0, 0, 0)
            vs(-1, V1, 1, 0)
            x_high(-1)
            for c in range(1, B // CHUNK):
                deviation(c)

            def batch(b, n, fill, outs, late):
                exps(b, 0, 0)
                exps(b, 0, 1)
                if later(b):
                    o_high(b - 1, 0)
                    o_high(b - 1, 1)
                exps(b, 1, 0)
                for do in fill[2:3]:
                    do()
                exps(b, 1, 1)
                for do in fill[3:]:
                    do()
                p_out(b, 0)
                outs()
                p_out(b, 1)
                for do in late:
                    do()

            def copies(n, us, to, p):
                return [lambda k=k, u=u: evacuate(n, u, to(k)) for k, u in enumerate(us)] if projects(n) else []

            def body(n, p, h):
                b = n * 2
                to_q = lambda k: q_t[:, 1 - p, k * 2:k * 2 + 2, :]
                to_k = lambda k: k_t[:, 1 - p, k * 2:k * 2 + 2, :]
                to_k2 = lambda k: k_t[:, 1 - p, 4 + k * 2:6 + k * 2, :]
                to_v0, to_v1 = (lambda k, i=i: v_n[:, 1 - p, i:i + 1, k * 512:(k + 1) * 512] for i in range(2))
                batch(b, n, copies(n, Q, to_q, p), lambda: store(b - 1, n, WO_OLD[0], 1) if later(n) else None, copies(n, K[0:2], to_k, p))
                batch(b + 1, n, copies(n, K[2:4], to_k2, p) + copies(n, V0, to_v0, p), lambda: store(b, n, WO_NEW[0], 0),
                      copies(n, V1, to_v1, p) + ([lambda: x_high(n)] if turns(n) else []))

            def last():
                o_high(B - 1, 0)
                o_high(B - 1, 1)
                store(B - 1, STEPS, WO_OLD[0], 1)
                for p in range(2):
                    act.wait_ge(stored[p], 16 * (B // 2) + 16)

            over(act, body, last)

        @block.vector
        def _(dve):
            dve.sem_inc(xn_up, 2)
            v = nc.vector
            stats, soft = Chain(dve, s_ln, B // CHUNK), Chain(dve, s_soft, 3 * UNITS)

            def statistics(c):
                dve.wait_ge(x_all[c % 2], c // 2 * 16 + 16)
                for i in range(CHUNK):
                    last = v.bn_stats(stat[:, i, :], staged(c)[:, i, :])
                stats(last)
                for i in range(CHUNK):
                    last = v.bn_aggr(mv[:, c * CHUNK + i, :], stat[:, i, :])
                last.then_inc(var, 1)
                dve.wait_ge(sd_up, c + 1)
                r = slice(c * CHUNK, (c + 1) * CHUNK)
                v.reciprocal(rs[:, r], sd[:, r]).then_inc(rs_up, 1)

            def norm(n, p, h):
                dve.wait_ge(x_in[p], h * 16 + 16)
                if not isinstance(n, int) or n >= 1:
                    used(dve, n - 3, TURN[0])
                for i in range(NB):
                    at = bass.ds(n * NB + i, 1)
                    last = v.tensor_scalar(xn[:, i, :], xin[:, p, i, :], mv[:, at, 0:1].rearrange("p a c -> p (a c)"), rs[:, at], ALU.subtract, ALU.mult)
                last.then_inc(xn_up, 1)

            def x_low(n, m):
                for u, high, low, done in ((TURN[0], xh, xl, x_hi), (TURN[1], ch, cl, c_hi)):
                    dve.wait_ge(done, m + 1)
                    v.tensor_tensor(low[:].rearrange("p a b -> p (a b)"), psJ[u % 2][:], high[:].rearrange("p a b -> p (a b)"), ALU.subtract).then_inc(j_free[u % 2], 1)

            def biased(b, g):
                dve.wait_ge(s_done, unit((b, g)))
                soft(v.scalar_tensor_tensor(s[:, g].rearrange("p a b -> p (a b)"), psS[g][:], SCALE, bias[:, g], ALU.mult, ALU.add))
                soft(v.tensor_reduce(mx[:, g], s[:, g], AX.X, ALU.max))
                v.tensor_scalar(less[:, g], mx[:, g], -1.0, None, ALU.mult).then_inc(s_less, 1)

            def normed(b, g):
                dve.wait_ge(e_up, unit((b, g)))
                soft(v.reciprocal(rc[:, g], sm[:, g]))
                if later(b):
                    dve.wait_ge(pt_done, b * UNITS + (g - 1))
                v.tensor_tensor(pr[:, g], s[:, g], rc[:, g].unsqueeze(2).to_broadcast([P, UH, P]), ALU.mult).then_inc(p_up, 1)

            def o_low(b, g):
                dve.wait_ge(o_hi, unit((b, g)))
                r = slice(g * UB, (g + 1) * UB)
                v.tensor_tensor(ol[:, r].rearrange("p a b -> p (a b)"), psO[g][:], oh[:, r].rearrange("p a b -> p (a b)"), ALU.subtract).then_inc(o_lo, 1)

            def add(n, u, i, nb):
                used(dve, n, u)
                dve.wait_ge(res_in[i], nb * 16 + 16)
                dve.wait_ge(stored[i], nb * 16 + 16)
                v.scalar_tensor_tensor(x3[:, i], psJ[u % 2][:, 0:D], C["gate"][:, 1:2], res[:, i], ALU.mult, ALU.add).then_inc(j_free[u % 2], 1)

            statistics(0)
            dve.wait_ge(rs_up, 1)
            norm(0, 0, 0)
            x_low(-2, 0)
            norm(1, 1, 0)
            for c in range(1, B // CHUNK):
                statistics(c)
            dve.wait_ge(rs_up, B // CHUNK)
            x_low(-1, 1)

            def evacuate(n, u, to):
                if projects(n):
                    used(dve, n, u)
                    v.tensor_copy(to, psJ[u % 2][:].rearrange("p (a b) -> p a b", a=to.shape[1])).then_inc(j_free[u % 2], 1)

            def batch(b, n, us, to):
                soft.start(b)
                biased(b, 0)
                biased(b, 1)
                evacuate(n, us[0], to(0))
                if later(b):
                    o_low(b - 1, 0)
                    o_low(b - 1, 1)
                evacuate(n, us[1], to(1))
                normed(b, 0)
                normed(b, 1)

            def body(n, p, h):
                b = n * 2
                batch(b, n, Q[0:2], lambda k: q_t[:, 1 - p, k * 2:k * 2 + 2, :])
                if turns(n):
                    norm(n + 2, p, h + 1)
                if later(n):
                    add(n, WO_OLD[0], 1, n - 1)
                batch(b + 1, n, K[2:4], lambda k: k_t[:, 1 - p, 4 + k * 2:6 + k * 2, :])
                add(n, WO_NEW[0], 0, n)
                if turns(n):
                    x_low(n, n + 2)

            def last():
                o_low(B - 1, 0)
                o_low(B - 1, 1)
                add(STEPS, WO_OLD[0], 1, STEPS - 1)

            over(dve, body, last)

        @block.tensor
        def _(pe):
            def bank(n, u):
                before = turn_of(n, u) - 1
                if not (isinstance(before, int) and before == 0):
                    pe.wait_ge(j_free[u % 2], before)
                return psJ[u % 2]

            def turn(n, m, p, h):
                for u, src, ready in ((TURN[0], xn, lambda: pe.wait_ge(xn_up, m + 3)),
                                      (TURN[1], cin[:, p], lambda: pe.wait_ge(c_in[p], h * 16 + 16))):
                    to = bank(n, u)
                    ready()
                    for k in range(KD):
                        for i in range(NB):
                            last = nc.tensor.transpose(to[:, k * N + i * P:k * N + (i + 1) * P], src[:, i, k * P:(k + 1) * P], C["ident"][:])
                    last.then_inc(j_done[u % 2], 1)

            def qk(n, us, weights, moving, at=0):
                for c, u in enumerate(us):
                    to = bank(n, u)
                    for j in range(2):
                        r = slice((at + c * 2 + j) * P, (at + c * 2 + j + 1) * P)
                        for k in range(KD):
                            last = product(pe, to[:, j * N:(j + 1) * N], [w[:, k, r] for w in weights], [x[:, k, :] for x in moving], k == 0, k == KD - 1)
                    last.then_inc(j_done[u % 2], 1)

            def vs(n, us, i):
                for c, u in enumerate(us):
                    to = bank(n, u)
                    for k in range(KD):
                        last = product(pe, to[:], [x[:, k, i * P:(i + 1) * P] for x in (ch, cl)],
                                       [w[:, k, c * 512:(c + 1) * 512] for w in (wvh, wvl)], k == 0, k == KD - 1)
                    last.then_inc(j_done[u % 2], 1)

            def scores(b, n, p, i, g):
                if i == 0 and g == 0:
                    for u in V1:
                        read(pe, n - 1, u)
                if later(b):
                    pe.wait_ge(pt_up, b * UNITS + (g - 1))
                q = slice(i * P, (i + 1) * P)
                for j in range(UB):
                    for r in range(2):
                        half = slice(r * DH, (r + 1) * DH)
                        m = g * UB + j
                        last = nc.tensor.matmul(psS[g][:, (r * UB + j) * P:(r * UB + j + 1) * P], q_t[half, p, m, q], k_t[half, p, m, q],
                                                start=True, stop=True)
                last.then_inc(s_done, 1)

            def turn_p(b, g):
                pe.wait_ge(p_up, unit((b, g)))
                for j in range(UH):
                    last = nc.tensor.transpose(psS[g][:, j * P:(j + 1) * P], pr[:, g, j, :], C["ident"][:])
                last.then_inc(pt_done, 1)

            def values(b, p, i, g):
                pe.wait_ge(pt_up, unit((b, g)))
                if later(b):
                    pe.wait_ge(o_lo, b * UNITS + (g - 1))
                for j in range(UB):
                    for r in range(2):
                        head = 2 * (g * UB + j) + r
                        last = nc.tensor.matmul(psO[g][r * DH:(r + 1) * DH, j * P:(j + 1) * P], v_n[:, p, i, head * DH:(head + 1) * DH],
                                                pt[:, g, r * UB + j, :], start=True, stop=True)
                last.then_inc(o_done, 1)

            def out(b, n, u):
                to = bank(n, u)
                pe.wait_ge(o_lo, unit((b, 1)))
                for m in range(PAIRS):
                    last = product(pe, to[:, 0:D], (oh[:, m, :], ol[:, m, :]), (woh[:, m, :], wol[:, m, :]), m == 0, m == PAIRS - 1)
                last.then_inc(j_done[u % 2], 1)

            turn(-2, 0, 0, 0)
            qk(-1, Q, (wqh, wql), (xh, xl))
            qk(-1, K, (wkh, wkl), (ch, cl))
            vs(-1, V0, 0)
            vs(-1, V1, 1)
            turn(-1, 1, 1, 0)

            def body(n, p, h):
                b = n * 2
                scores(b, n, p, 0, 0)
                scores(b, n, p, 0, 1)
                if later(n):
                    values(b - 1, 1 - p, 1, 0)
                    values(b - 1, 1 - p, 1, 1)
                if projects(n):
                    qk(n, Q, (wqh, wql), (xh, xl))
                turn_p(b, 0)
                if later(n):
                    out(b - 1, n, WO_OLD[0])
                turn_p(b, 1)
                if projects(n):
                    qk(n, K[0:2], (wkh, wkl), (ch, cl))
                scores(b + 1, n, p, 1, 0)
                scores(b + 1, n, p, 1, 1)
                values(b, p, 0, 0)
                values(b, p, 0, 1)
                if projects(n):
                    qk(n, K[2:4], (wkh, wkl), (ch, cl), 4)
                    vs(n, V0, 0)
                turn_p(b + 1, 0)
                out(b, n, WO_NEW[0])
                turn_p(b + 1, 1)
                if projects(n):
                    vs(n, V1, 1)
                if turns(n):
                    turn(n, n + 2, p, h + 1)

            def last():
                values(B - 1, 1, 1, 0)
                values(B - 1, 1, 1, 1)
                out(B - 1, STEPS, WO_OLD[0])

            over(pe, body, last)


def gated_in(nc, A, C, X3, acc, xth, xtl):
    STEPS, NB = B // 4, 4
    N = NB * P
    with ExitStack() as ctx:
        m = Space(nc, ctx, "gin")
        sb, ps, sem = m.sb, m.ps, m.sem
        gw = sb("gw", [P, KD, E1])
        stat = sb("stat", [P, NB, 6])
        mv = sb("mv", [P, 2, NB, 2])
        sd = sb("sd", [P, 2, NB])
        rs = sb("rs", [P, NB])
        xn = sb("xn", [P, 2, NB, D])
        xt = sb("xt", [P, 2, KD, N])
        psT = [ps(f"psT{p}", [P, KD, N]) for p in range(2)]
        psL = [ps(f"psL{p}", [P, 512]) for p in range(2)]
        x_in = [sem(f"x_in{p}") for p in range(2)]
        gw_in, var, sd_up, xn_up, t_done, t_up, hi, lo, l_done, l_up = (sem(n) for n in ("gw_in", "var", "sd_up", "xn_up", "t_done", "t_up", "hi", "lo", "l_done", "l_up"))
        s_ln, stood = sem("s_ln"), sem("stood")
        block = ctx.enter_context(nc.Block())
        x3_d = X3.rearrange("(b p) d -> p b d", p=P)

        def over(eng, body):
            with eng.Fori(0, STEPS // 2) as h:
                body(h * 2, 0, h)
                body(h * 2 + 1, 1, h)

        @block.sync
        def _(sp):
            sp.dma_start(gw[:], A["gwT"].rearrange("(k p) e -> p k e", p=P)).then_inc(gw_in, 16)

            def load(n, p, h):
                sp.wait_ge(var, n + 1)
                sp.dma_start(acc[:, bass.ds(n * NB, NB), :], x3_d[:, bass.ds(n * NB, NB), :]).then_inc(x_in[p], 16)
            over(sp, load)

        @block.scalar
        def _(act):
            act.sem_inc(l_up, 2)
            act.sem_inc(t_up, 2)

            def body(n, p, h):
                act.wait_ge(var, n + 3)
                nc.scalar.activation(sd[:, p], mv[:, p, :, 1], ACT.Sqrt, bias=C["eps"][:]).then_inc(sd_up, 1)
                act.wait_ge(t_done, n + 3)
                act.wait_ge(lo, n + 1)
                nc.scalar.activation(xt[:, p].rearrange("p k t -> p (k t)"), psT[p][:].rearrange("p k t -> p (k t)"), ACT.Copy).then_inc(t_up, 1)
                act.wait_ge(t_up, n + 3)
                nc.scalar.activation(xth[:, :, bass.ds(n * N, N)], xt[:, p], ACT.Copy).then_inc(hi, 1)
                act.wait_ge(l_done, n + 1)
                nc.scalar.activation(C["logits1"][:, bass.ds(n * NB, NB), :], psL[p][:, 0:NB * E1].rearrange("p (i e) -> p i e", e=E1), ACT.Copy).then_inc(l_up, 1)
            over(act, body)

        @block.gpsimd
        def _(pool):
            pool.sem_inc(lo, 2)

            def body(n, p, h):
                pool.wait_ge(hi, n + 1)
                nc.gpsimd.tensor_tensor(xtl[:, :, bass.ds(n * N, N)], xt[:, p], xth[:, :, bass.ds(n * N, N)], ALU.subtract).then_inc(lo, 1)
            over(pool, body)

        @block.tensor
        def _(pe):
            pe.wait_ge(gw_in, 16)
            pe.sem_inc(t_done, 2)

            def body(n, p, h):
                pe.wait_ge(xn_up, n + 3)
                pe.wait_ge(t_up, n + 1)
                for k in range(KD):
                    for i in range(NB):
                        last = nc.tensor.transpose(psT[p][:, k, i * P:(i + 1) * P], xn[:, p, i, k * P:(k + 1) * P], C["ident"][:])
                last.then_inc(t_done, 1)
                pe.wait_ge(t_up, n + 3)
                pe.wait_ge(l_up, n + 1)
                for i in range(NB):
                    for k in range(KD):
                        last = nc.tensor.matmul(psL[p][:, i * E1:(i + 1) * E1], xt[:, p, k, i * P:(i + 1) * P], gw[:, k, :], start=(k == 0), stop=(k == KD - 1))
                last.then_inc(l_done, 1)
            over(pe, body)

        @block.vector
        def _(dve):
            v = nc.vector
            dve.sem_inc(var, 2)
            dve.sem_inc(xn_up, 2)
            ln = Chain(dve, s_ln, 2)

            def body(n, p, h):
                ln.start(n)
                dve.wait_ge(x_in[p], h * 16 + 16)
                for i in range(NB):
                    last = v.bn_stats(stat[:, i, :], acc[:, bass.ds(n * NB + i, 1), :].rearrange("p a d -> p (a d)"))
                ln(last)
                stand(dve, stood)
                for i in range(NB):
                    last = v.bn_aggr(mv[:, p, i, :], stat[:, i, :])
                last.then_inc(var, 1)
                dve.wait_ge(sd_up, n + 1)
                ln(v.reciprocal(rs[:], sd[:, p]))
                dve.wait_ge(t_done, n + 1)
                for i in range(NB):
                    last = v.tensor_scalar(xn[:, p, i, :], acc[:, bass.ds(n * NB + i, 1), :].rearrange("p a d -> p (a d)"), mv[:, p, i, 0:1], rs[:, i:i + 1],
                                           ALU.subtract, ALU.mult)
                last.then_inc(xn_up, 1)
                ln.end()
            over(dve, body)


def gated_route(nc, A, C):
    NG = E1 // 4
    with ExitStack() as ctx:
        m = Space(nc, ctx, "groute")
        sb, sem = m.sb, m.sem
        score, tmp, work, pick, sel = (sb(n, [P, B, E1]) for n in ("score", "tmp", "work", "pick", "sel"))
        eb = sb("eb", [P, E1])
        rank = sb("rank", [P, E1])
        hi2, lo2 = sb("hi2", [P, B, NG, 2]), sb("lo2", [P, B, NG, 2])
        gs, gwork, g1, g2 = (sb(n, [P, B, NG]) for n in ("gs", "gwork", "g1", "g2"))
        top, best = sb("top", [P, B]), sb("best", [P, B])
        eb_in, ranked, s_up, step = sem("eb_in"), sem("ranked"), sem("s_up"), sem("step")
        block = ctx.enter_context(nc.Block())

        @block.sync
        def _(sp):
            sp.dma_start(eb[:], A["ebias"].rearrange("(a n) -> a n", a=1).to_broadcast((P, E1))).then_inc(eb_in, 16)

        @block.gpsimd
        def _(pool):
            nc.gpsimd.iota(rank[:], [[-1, E1]], base=E1, channel_multiplier=0, allow_small_or_imprecise_dtypes=True).then_inc(ranked, 1)

        @block.scalar
        def _(act):
            nc.scalar.activation(score[:], C["logits1"][:], ACT.Sigmoid).then_inc(s_up, 1)

        @block.vector
        def _(dve):
            v = nc.vector
            link = Chain(dve, step, 0)
            dve.wait_ge(eb_in, 16)
            dve.wait_ge(ranked, 1)
            dve.wait_ge(s_up, 1)
            link(v.tensor_tensor(tmp[:], score[:], eb[:].unsqueeze(1).to_broadcast([P, B, E1]), ALU.add))
            four = tmp[:].rearrange("p t (g a b) -> p (t g) a b", g=NG, a=2)
            flat = lambda x: x[:].rearrange("p t g a -> p (t g) a")
            v.tensor_tensor(flat(hi2), four[:, :, :, 0], four[:, :, :, 1], ALU.max)
            link(v.tensor_tensor(flat(lo2), four[:, :, :, 0], four[:, :, :, 1], ALU.min))
            v.tensor_tensor(gs[:], hi2[:, :, :, 0], hi2[:, :, :, 1], ALU.max)
            v.tensor_tensor(g1[:], hi2[:, :, :, 0], hi2[:, :, :, 1], ALU.min)
            link(v.tensor_tensor(g2[:], lo2[:, :, :, 0], lo2[:, :, :, 1], ALU.max))
            link(v.tensor_tensor(g1[:], g1[:], g2[:], ALU.max))
            link(v.tensor_tensor(gs[:], gs[:], g1[:], ALU.add))
            link(v.tensor_reduce(best[:], gs[:], AX.X, ALU.max))
            link(first_of(nc, link, gs[:], best[:], rank[:, 0:NG], gwork[:], top[:], g1[:]))
            link(v.scalar_tensor_tensor(rows(gs), rows(g1), -1e30, rows(gs), ALU.mult, ALU.add))
            link(v.tensor_reduce(best[:], gs[:], AX.X, ALU.max))
            link(first_of(nc, link, gs[:], best[:], rank[:, 0:NG], gwork[:], top[:], g2[:]))
            link(v.tensor_tensor(g1[:], g1[:], g2[:], ALU.add))
            link(v.tensor_tensor(tmp[:].rearrange("p t (g a) -> p (t g) a", g=NG), tmp[:].rearrange("p t (g a) -> p (t g) a", g=NG),
                                 g1[:].rearrange("p t g -> p (t g)").unsqueeze(2).to_broadcast([P, B * NG, E1 // NG]), ALU.mult))
            for k in range(TOP):
                link(v.tensor_reduce(best[:], tmp[:], AX.X, ALU.max))
                link(first_of(nc, link, tmp[:], best[:], rank[:], work[:], top[:], pick[:]))
                if k == 0:
                    link(v.tensor_copy(sel[:], pick[:]))
                else:
                    link(v.tensor_tensor(sel[:], sel[:], pick[:], ALU.add))
                if k < TOP - 1:
                    link(v.scalar_tensor_tensor(rows(tmp), rows(pick), -1e30, rows(tmp), ALU.mult, ALU.add))
            link(v.tensor_tensor(sel[:], sel[:], score[:], ALU.mult))
            link(v.tensor_reduce(top[:], sel[:], AX.X, ALU.add))
            link(v.tensor_scalar(top[:], top[:], 1e-20, None, ALU.add))
            link(v.reciprocal(top[:], top[:]))
            link(v.tensor_tensor(sel[:], sel[:], top[:].unsqueeze(2).to_broadcast([P, B, E1]), ALU.mult))
            link(v.tensor_scalar(C["weight1"][:, :, 0:E1], sel[:], 2.5, C["gate"][:, 3:4], ALU.mult, ALU.mult))
            link(v.tensor_copy(C["weight1"][:, :, E1:E1 + 1].rearrange("p t a -> p (t a)"), C["gate"][:, 3:4].to_broadcast([P, B])))


def gated(nc, A, C, acc, xth, xtl, out):
    EX, NB = E1 + 1, 4
    N = NB * P
    BLOCKS = B // NB
    with ExitStack() as ctx:
        m = Space(nc, ctx, "gated")
        sb, ps, sem = m.sb, m.ps, m.sem
        raw = sb("raw", [P, 2, 3, KD, I1])
        wh = sb("wh", [P, 2, 3, KD, I1], F32R)
        wl = sb("wl", [P, 2, 3, KD, I1], F32R)
        sg = sb("sg", [P, 2, N])
        it = sb("it", [P, 2, N])
        ih = sb("ih", [P, 2, N], F32R)
        il = sb("il", [P, 2, N], F32R)
        psG = [ps(f"psG{p}", [P, N]) for p in range(2)]
        psU = [ps(f"psU{p}", [P, N]) for p in range(2)]
        psY = [ps(f"psY{p}", [P, NB, D]) for p in range(2)]
        w_in = [sem(f"w_in{p}") for p in range(2)]
        w_hi, w_lo, g_done, u_done, s_up, i_up, i_hi, i_lo, y_done, y_up, stored = (
            sem(n) for n in ("w_hi", "w_lo", "g_done", "u_done", "s_up", "i_up", "i_hi", "i_lo", "y_done", "y_up", "stored"))
        block = ctx.enter_context(nc.Block())
        out_d = out.rearrange("b p d -> p b d")

        def over(eng, body):
            with eng.Fori(0, EX // 2) as h:
                body(h * 2, 0, h)
                body(h * 2 + 1, 1, h)
            body(EX - 1, 0, EX // 2)

        @block.sync
        def _(sp):
            def load(e, p, h):
                sp.wait_ge(w_lo, e + 1)
                sp.dma_start(raw[:, p].rearrange("p a k i -> p (a k i)"), A["gex"][bass.ds(e, 1)].rearrange("a p n -> p (a n)")).then_inc(w_in[p], 16)
            over(sp, load)
            sp.wait_ge(y_up, EX * BLOCKS)
            sp.wait_ge(stored, 16 * BLOCKS)

        @block.gpsimd
        def _(pool):
            pool.sem_inc(w_lo, 2)

            def weights(e, p, h):
                pool.wait_ge(w_hi, e + 1)
                nc.gpsimd.tensor_tensor(wl[:, p].rearrange("p a k i -> p (a k i)"), raw[:, p].rearrange("p a k i -> p (a k i)"),
                                        wh[:, p].rearrange("p a k i -> p (a k i)"), ALU.subtract).then_inc(w_lo, 1)

            def low(e, j):
                n = e * BLOCKS + j
                pool.wait_ge(i_hi, n + 1)
                nc.gpsimd.tensor_tensor(il[:, j % 2], it[:, j % 2], ih[:, j % 2], ALU.subtract).then_inc(i_lo, 1)

            weights(0, 0, 0)

            def body(e, p, h):
                for j in range(BLOCKS):
                    low(e, j)
                    if j == 3 and not (isinstance(e, int) and e == EX - 1):
                        weights(e + 1, 1 - p, h + p)
            over(pool, body)

        @block.scalar
        def _(act):
            def weights(e, p, h):
                act.wait_ge(w_in[p], h * 16 + 16)
                if not (isinstance(e, int) and e < 1):
                    act.wait_ge(y_done, e * BLOCKS - BLOCKS + 1)
                nc.scalar.activation(wh[:, p].rearrange("p a k i -> p (a k i)"), raw[:, p].rearrange("p a k i -> p (a k i)"), ACT.Copy).then_inc(w_hi, 1)

            def body(e, p, h):
                for j in range(BLOCKS):
                    n = e * BLOCKS + j
                    act.wait_ge(g_done, n + 1)
                    nc.scalar.activation(sg[:, j % 2], psG[j % 2][:], ACT.Silu).then_inc(s_up, 1)
                    act.wait_ge(i_up, n + 1)
                    nc.scalar.activation(ih[:, j % 2], it[:, j % 2], ACT.Copy).then_inc(i_hi, 1)
                    if j == 3 and not (isinstance(e, int) and e == EX - 1):
                        weights(e + 1, 1 - p, h + p)
                    if isinstance(e, int) and e == EX - 1 and j >= 1:
                        store(j - 1)

            def store(j):
                act.wait_ge(y_up, (EX - 1) * BLOCKS + j + 1)
                act.dma_start(out_d[:, j * NB:(j + 1) * NB, :], acc[:, j * NB:(j + 1) * NB, :]).then_inc(stored, 16)

            weights(0, 0, 0)
            over(act, body)
            store(BLOCKS - 1)

        @block.vector
        def _(dve):
            v = nc.vector

            def mul(e, j):
                n = e * BLOCKS + j
                dve.wait_ge(s_up, n + 1)
                dve.wait_ge(u_done, n + 1)
                v.tensor_tensor(it[:, j % 2], sg[:, j % 2], psU[j % 2][:], ALU.mult).then_inc(i_up, 1)

            def add(e, j):
                n = e * BLOCKS + j
                dve.wait_ge(y_done, n + 2)
                for i in range(NB):
                    a = acc[:, j * NB + i, :]
                    last = v.scalar_tensor_tensor(a, psY[j % 2][:, i, :], C["weight1"][:, j * NB + i, bass.ds(e, 1)], a, ALU.mult, ALU.add)
                last.then_inc(y_up, 1)

            def body(e, p, h):
                for j in range(BLOCKS):
                    mul(e, j)
                    if j:
                        add(e, j - 1)
                    elif not (isinstance(e, int) and e == 0):
                        add(e - 1, BLOCKS - 1)

            mul(0, 0)
            for j in range(1, BLOCKS):
                mul(0, j)
                add(0, j - 1)
            with dve.Fori(0, (EX - 1) // 2) as h:
                body(h * 2 + 1, 1, h)
                body(h * 2 + 2, 0, h + 1)
            add(EX - 1, BLOCKS - 1)

        @block.tensor
        def _(pe):
            def up(e, p, j):
                n = e * BLOCKS + j
                t = slice(j * N, (j + 1) * N)
                if isinstance(n, int) and n < 2:
                    pass
                else:
                    pe.wait_ge(i_up, n - 1)
                if j == 0:
                    pe.wait_ge(w_lo, e + 3)
                for a, to, done in ((0, psG, g_done), (1, psU, u_done)):
                    for k in range(KD):
                        last = product(pe, to[j % 2][:], (wh[:, p, a, k, :], wl[:, p, a, k, :]), (xth[:, k, t], xtl[:, k, t]), k == 0, k == KD - 1)
                    last.then_inc(done, 1)

            def down(e, p, j):
                n = e * BLOCKS + j
                pe.wait_ge(i_lo, n + 1)
                if not (isinstance(n, int) and n < 2):
                    pe.wait_ge(y_up, n - 1)
                w = [x[:, p, 2].rearrange("p k i -> p (k i)") for x in (wh, wl)]
                for i in range(NB):
                    r = slice(i * P, (i + 1) * P)
                    last = product(pe, psY[j % 2][:, i, :], (ih[:, j % 2, r], il[:, j % 2, r]), w, True, True)
                last.then_inc(y_done, 1)

            def body(e, p):
                for j in range(BLOCKS):
                    up(e, p, j)
                    if j:
                        down(e, p, j - 1)
                    elif not (isinstance(e, int) and e == 0):
                        down(e - 1, 1 - p, BLOCKS - 1)

            pe.sem_inc(y_done, 1)
            body(0, 0)
            with pe.Fori(0, (EX - 1) // 2) as h:
                body(h * 2 + 1, 1)
                body(h * 2 + 2, 0)
            down(EX - 1, 0, BLOCKS - 1)


def gated_mix__experts__attend__gated_experts(nc, A, out):
    X2, XN = (nc.dram_tensor(n, (ROWS, D), F32, kind="Internal").ap() for n in ("x2_rows", "xn_rows"))
    X3 = nc.dram_tensor("x3_rows", (B * S, D), F32, kind="Internal").ap()
    VB = nc.dram_tensor("bias_by_distance", (HEADS, P, 2 * P), F32, kind="Internal").ap()
    with ExitStack() as ctx:
        m = Space(nc, ctx, "const")
        C = {n: m.sb(n, [P, P]) for n in ("ident", "ones", "tri", "gsum")}
        C["gate"] = m.sb("gate", [P, 4])
        C["eps"] = m.sb("eps", [P, 1])
        setup(nc, A, C)
        with ExitStack() as until_attend:
            held = AttendHeld(nc, until_attend, A, VB)
            with ExitStack() as layer:
                m0 = Space(nc, layer, "layer0")
                C["logits0"] = m0.sb("logits0", [P, B, E0])
                C["slot_row"] = m0.sb("slot_row", [SLOTS, E0, PARTS], I32)
                C["slot_weight"] = m0.sb("slot_weight", [SLOTS, E0, PARTS])
                mix(nc, A, C, X2, XN)
                route(nc, C, held)
                experts(nc, A, C, X2, XN)
            attend(nc, A, C, held, X2, X3)
        C["logits1"] = m.sb("logits1", [P, B, E1])
        C["weight1"] = m.sb("weight1", [P, B, E1 + 1])
        acc = m.sb("acc", [P, B, D])
        xth, xtl = (m.sb(n, [P, KD, B * P], F32R) for n in ("xth", "xtl"))
        gated_in(nc, A, C, X3, acc, xth, xtl)
        gated_route(nc, A, C)
        gated(nc, A, C, acc, xth, xtl, out)


def layouts(i):
    def blocks(w):
        return w.transpose(0, 2, 1).reshape(E1 + 1, KD, P, I1).transpose(0, 2, 1, 3)

    def with_shared(name, shared):
        return np.concatenate([np.asarray(i[name]), np.asarray(i[shared])[None]])

    gate = with_shared("L1_ffn_gate_proj", "L1_ffn_shared_gate_w")
    up = with_shared("L1_ffn_up_proj", "L1_ffn_shared_up_w")
    down = with_shared("L1_ffn_down_proj", "L1_ffn_shared_down_w")
    down = down.transpose(0, 2, 1).reshape(E1 + 1, I1, KD, P)
    arrays = {
        "x": i["x"], "ctx_1024": i["ctx_1024"], "g_xattn": i["g_xattn"], "g_ffn": i["g_ffn"],
        "Wt": i["L0_xattn_Wt"], "WpT": np.asarray(i["L0_xattn_Wp"]).T, "WgT": np.asarray(i["L0_xattn_Wg"]).T,
        "WzT": np.asarray(i["L0_xattn_Wz"]).transpose(0, 2, 1).reshape(GROUPS * GROUP, GROUP),
        "gamma": i["L0_xattn_gamma"], "beta": i["L0_xattn_beta"],
        "wr": i["L0_ffn_w_router"], "wi": i["L0_ffn_wi"], "wo": i["L0_ffn_wo"],
        "Wq": i["L1_xattn_Wq"], "Wk": i["L1_xattn_Wk"], "Wv": i["L1_xattn_Wv"], "Wo": i["L1_xattn_Wo"],
        "relT": np.asarray(i["L1_xattn_rel_bias"]).T, "hot": bucket_onehot(),
        "mask": np.asarray(i["mask_1x1xSxS2_bk0"]).reshape(S, S),
        "gwT": np.asarray(i["L1_ffn_gate_w"]).T, "ebias": i["L1_ffn_e_bias"],
        "gex": np.stack([blocks(gate), blocks(up), down], 2).reshape(E1 + 1, P, 3 * KD * I1),
    }
    return {n: np.ascontiguousarray(a) for n, a in arrays.items()}


def kernel(**inputs):
    import concourse.bacc as bacc
    from concourse.bass_utils import run_bass_kernel_spmd

    nc = bacc.Bacc("TRN2", target_bir_lowering=False, num_devices=1)
    laid = layouts(inputs)
    A = {n: nc.dram_tensor(f"in_{n}_dram", a.shape, mybir.dt.from_np(a.dtype), kind="ExternalInput").ap() for n, a in laid.items()}
    out = nc.dram_tensor("out_0_dram", (B, S, D), F32, kind="ExternalOutput").ap()
    gated_mix__experts__attend__gated_experts(nc, A, out)
    r = run_bass_kernel_spmd(nc, [{f"in_{n}_dram": a for n, a in laid.items()}], core_ids=[0])
    return r.results[0]["out_0_dram"]
```

```python
from contextlib import ExitStack

import numpy as np
import concourse.bass as bass
from concourse import mybir

F32 = mybir.dt.float32
F32R = mybir.dt.float32r
BF16 = mybir.dt.bfloat16
I32 = mybir.dt.int32
ALU = mybir.AluOpType
ACT = mybir.ActivationFunctionType
AX = mybir.AxisListType

P = 128
B, S, D = 32, 128, 256
KD = D // P
EPS = 1e-5
LOWEST = -3.4028234663852886e38

GROUPS, GROUP = 8, 16
E0, F0, CAP = 8, 1024, 160
HALVES = 2
TILES = B // HALVES
SLOTS = 80
PARTS = HALVES * (CAP // SLOTS)
DUMMY = B * S
ROWS = B * S + P
HEADS, DH = 16, 64
PAIRS = HEADS // 2
E1, I1, TOP = 16, 128, 4


class Chain:

    def __init__(self, eng, sem, length):
        self.eng, self.sem, self.length, self.count, self.base = eng, sem, length, 0, 0

    def start(self, step):
        self.base, self.count = step * self.length, 0

    def __call__(self, ins):
        self.count += 1
        ins.then_inc(self.sem, 1)
        self.eng.wait_ge(self.sem, self.base + self.count)

    def end(self):
        assert self.count == self.length, (self.count, self.length)


def rows(t):
    return t.rearrange("p a b -> p (a b)")


def stand(eng, C):
    eng.sem_inc(C["stood"], 1)


def product(pe, out, weights, moving, first, last):
    (wh, wl), (mh, ml) = weights, moving
    pe.matmul(out, wl, mh, start=first, stop=False)
    pe.matmul(out, wh, ml, start=False, stop=False)
    return pe.matmul(out, wh, mh, start=False, stop=last)


class Space:

    def __init__(self, nc, ctx, tag):
        self.nc, self.ctx, self.tag = nc, ctx, tag

    def sb(self, name, shape, dt=F32):
        return self.ctx.enter_context(self.nc.sbuf_tensor(f"{self.tag}_{name}", shape, dt))

    def ps(self, name, shape, dt=F32):
        return self.ctx.enter_context(self.nc.psum_tensor(f"{self.tag}_{name}", shape, dt))

    def sem(self, name):
        return self.ctx.enter_context(self.nc.semaphore(f"{self.tag}_{name}"))


def setup(nc, A, C):
    with ExitStack() as ctx:
        m = Space(nc, ctx, "setup")
        made, gates_in, gates_up = (m.sem(n) for n in ("made", "gates_in", "gates_up"))
        graw = m.sb("graw", [P, 4])
        block = ctx.enter_context(nc.Block())

        @block.sync
        def _(sp):
            sp.dma_start(graw[:, 0:2], A["g_xattn"].rearrange("(a n) -> a n", a=1).to_broadcast((P, 2))).then_inc(gates_in, 16)
            sp.dma_start(graw[:, 2:4], A["g_ffn"].rearrange("(a n) -> a n", a=1).to_broadcast((P, 2))).then_inc(gates_in, 16)
            sp.wait_ge(gates_in, 32)

        @block.scalar
        def _(act):
            act.wait_ge(gates_in, 32)
            nc.scalar.activation(C["gate"][:], graw[:], ACT.Tanh).then_inc(gates_up, 1)
            act.wait_ge(gates_up, 1)

        @block.gpsimd
        def _(pool):
            nc.gpsimd.memset(C["eps"][:], EPS)
            nc.gpsimd.memset(C["ident"][:], 0.0)
            nc.gpsimd.memset(C["ones"][:], 1.0)
            nc.gpsimd.memset(C["tri"][:], 1.0)
            nc.gpsimd.memset(C["gsum"][:], 1.0 / GROUP).then_inc(made, 1)
            pool.wait_ge(made, 1)
            nc.gpsimd.affine_select(out=C["ident"][:], in_=C["ident"][:], compare_op=ALU.not_equal, fill=1.0,
                                    base=0, pattern=[[-1, P]], channel_multiplier=1)
            nc.gpsimd.affine_select(out=C["tri"][:], in_=C["tri"][:], compare_op=ALU.is_ge, fill=0.0,
                                    base=0, pattern=[[1, P]], channel_multiplier=-1)
            g = C["gsum"].rearrange("p (a b) -> p a b", b=GROUP)
            nc.gpsimd.affine_select(out=g, in_=g, compare_op=ALU.is_ge, fill=0.0,
                                    base=0, pattern=[[-GROUP, GROUPS], [0, GROUP]], channel_multiplier=1).then_inc(made, 1)
            pool.wait_ge(made, 2)
            nc.gpsimd.affine_select(out=g, in_=g, compare_op=ALU.is_ge, fill=0.0,
                                    base=GROUP - 1, pattern=[[GROUP, GROUPS], [0, GROUP]], channel_multiplier=-1).then_inc(made, 1)
            pool.wait_ge(made, 3)


def mix(nc, A, C, X2, XN):
    STEPS, NB = B // 4, 4
    W = NB * D
    with ExitStack() as ctx:
        m = Space(nc, ctx, "mix")
        sb, ps, sem = m.sb, m.ps, m.sem
        wz = sb("wz", [P, GROUP])
        bdz = sb("bdz", [P, P])
        wt = sb("wt", [P, P])
        wraw = sb("wraw", [P, 3, P])
        wh = sb("wh", [P, 3, P], F32R)
        wl = sb("wl", [P, 3, P], F32R)
        wr = sb("wr", [P, KD, E0])
        gb = sb("gb", [P, 2])
        gbt = sb("gbt", [P, 2])
        xin = sb("xin", [P, 2, NB, D])
        cin = sb("cin", [P, 2, NB, D])
        xnf = sb("xnf", [P, 2, W])
        xh = sb("xh", [P, 2, W], F32R)
        xl = sb("xl", [P, 2, W], F32R)
        ch = sb("ch", [P, 2, W], F32R)
        cl = sb("cl", [P, 2, W], F32R)
        stat = sb("stat", [P, NB, 6])
        mv = sb("mv", [P, 2, NB, 2])
        sd = sb("sd", [P, 2, NB])
        rs = sb("rs", [P, NB])
        gs = sb("gs", [P, W])
        junk = sb("junk", [P, W])
        ustat = sb("ustat", [P, NB, 6])
        umv = sb("umv", [P, NB, 2])
        q = sb("q", [P, 3, NB])
        s3 = sb("s3", [P, 3, NB])
        t1 = sb("t1", [P, NB])
        t2 = sb("t2", [P, NB])
        va = sb("va", [P, NB])
        sdu = sb("sdu", [P, NB])
        ab = sb("ab", [P, 2, NB])
        w = sb("w", [P, W])
        zc, z = sb("zc", [P, 2, W]), sb("z", [P, W])
        x1 = sb("x1", [P, 2, W])
        stat2 = sb("stat2", [P, NB, 6])
        mv2 = sb("mv2", [P, NB, 2])
        sd2 = sb("sd2", [P, NB])
        rs2, mr2 = sb("rs2", [P, NB]), sb("mr2", [P, NB])
        xn = sb("xn", [P, 2, W])
        xt = sb("xt", [P, NB * KD, P])
        zero = sb("zero", [P, D])
        psP, psG, psU = (ps(n, [P, W]) for n in ("psP", "psG", "psU"))
        psS = ps("psS", [P, 512])
        psT = ps("psT", [P, 512])

        w_in, wz_in, bdz_up, w_up, w2_made, w_split, gbt_up = (sem(n) for n in ("w_in", "wz_in", "bdz_up", "w_up", "w2_made", "w_split", "gbt_up"))
        in_ready = [sem(f"in_ready{p}") for p in range(2)]
        in_free, var1, sd1_ready, xn_ready, hi_ready, lo_ready = (sem(n) for n in ("in_free", "var1", "sd1_ready", "xn_ready", "hi_ready", "lo_ready"))
        g_done, p_done, u_done, gs_ready, p_used = (sem(n) for n in ("g_done", "p_done", "u_done", "gs_ready", "p_used"))
        q_ready, s_ready, va_ready, sdu_ready, ab_ready, w_ready = (sem(n) for n in ("q_ready", "s_ready", "va_ready", "sdu_ready", "ab_ready", "w_ready"))
        x1_ready, var2, sd2_ready, rs2_ready, xn2_ready = (sem(n) for n in ("x1_ready", "var2", "sd2_ready", "rs2_ready", "xn2_ready"))
        lg_copied = sem("lg_copied")
        t_done, t_used, l_done = (sem(n) for n in ("t_done", "t_used", "l_done"))
        stored = [sem(f"stored{p}") for p in range(2)]
        zeros_up, dummies = sem("zeros_up"), sem("dummies")
        s_front, s_back, c_high = (sem(n) for n in ("s_front", "s_back", "c_high"))
        zc_ready, z_ready = sem("zc_ready"), sem("z_ready")
        block = ctx.enter_context(nc.Block())

        x_d = A["x"].rearrange("b p d -> p b d")
        c_d = A["ctx_1024"].rearrange("b p d -> p b d")
        x2_d = X2[0:B * S, :].rearrange("(b p) d -> p b d", p=P)
        xn_d = XN[0:B * S, :].rearrange("(b p) d -> p b d", p=P)

        def over_steps(front, back):
            front(0, 0, 0)
            back(0, 0, 0, (1, 1, 0))

            def pair(h):
                back(h * 2 - 1, 1, h - 1, (h * 2, 0, h))
                back(h * 2, 0, h, (h * 2 + 1, 1, h))
            return pair, lambda: back(STEPS - 1, 1, STEPS // 2 - 1, None)

        @block.sync
        def _(sp):
            def front(n, p, h):
                sp.wait_ge(in_free, n + 1)
                sp.dma_start(xin[:, p], x_d[:, bass.ds(n * NB, NB), :]).then_inc(in_ready[p], 16)
                sp.dma_start(cin[:, p], c_d[:, bass.ds(n * NB, NB), :]).then_inc(in_ready[p], 16)

            with sp.Fori(0, STEPS // 2) as h:
                front(h * 2, 0, h)
                front(h * 2 + 1, 1, h)
            sp.wait_ge(zeros_up, 1)
            sp.dma_start(X2[DUMMY:ROWS, :], zero[:]).then_inc(dummies, 16)
            sp.dma_start(XN[DUMMY:ROWS, :], zero[:]).then_inc(dummies, 16)
            sp.wait_ge(dummies, 32)

        @block.gpsimd
        def _(pool):
            pool.sem_inc(in_free, 2)
            pool.sem_inc(z_ready, 2)
            nc.gpsimd.memset(zero[:], 0.0).then_inc(zeros_up, 1)
            pool.wait_ge(w_up, 1)
            nc.gpsimd.tensor_tensor(wl[:], wraw[:], wh[:], ALU.subtract).then_inc(w_split, 1)

            def split(n, p, h):
                pool.wait_ge(c_high, n + 1)
                nc.gpsimd.tensor_tensor(cl[:, p], rows(cin[:, p]), ch[:, p], ALU.subtract).then_inc(lo_ready, 1)
                pool.wait_ge(hi_ready, n + 1)
                nc.gpsimd.tensor_tensor(xl[:, p], xnf[:, p], xh[:, p], ALU.subtract).then_inc(lo_ready, 1)
                pool.wait_ge(zc_ready, n + 1)
                pool.wait_ge(x1_ready, n + 1)
                nc.gpsimd.tensor_tensor(z[:], zc[:, p], rows(xin[:, p]), ALU.add).then_inc(z_ready, 1)
                pool.wait_ge(z_ready, n + 3)
                pool.sem_inc(in_free, 1)

            with pool.Fori(0, STEPS // 2) as h:
                split(h * 2, 0, h)
                split(h * 2 + 1, 1, h)

        @block.scalar
        def _(act):
            act.dma_start(wt[:], A["Wt"]).then_inc(wz_in, 16)
            act.dma_start(wz[:], A["WzT"]).then_inc(wz_in, 16)
            act.dma_start(wraw[:, 0, :], A["WpT"]).then_inc(w_in, 16)
            act.dma_start(wraw[:, 1, :], A["WgT"]).then_inc(w_in, 16)
            act.dma_start(wr[:], A["wr"].rearrange("(k p) e -> p k e", p=P)).then_inc(w_in, 16)
            act.dma_start(gb[:, 0:1], A["gamma"].rearrange("(p a) -> p a", a=1)).then_inc(w_in, 16)
            act.dma_start(gb[:, 1:2], A["beta"].rearrange("(p a) -> p a", a=1)).then_inc(w_in, 16)

            def weights():
                act.wait_ge(w2_made, 1)
                act.wait_ge(w_in, 16 * 5)
                nc.scalar.activation(wraw[:, 2, :], psS[:, 0:P], ACT.Copy).then_inc(gbt_up, 1)
                act.wait_ge(gbt_up, 1)
                nc.scalar.activation(wh[:], wraw[:], ACT.Copy).then_inc(w_up, 1)
                nc.scalar.activation(gbt[:], gb[:], ACT.Copy, scale=C["gate"][:, 0:1]).then_inc(gbt_up, 1)

            act.sem_inc(gs_ready, 1)
            act.sem_inc(w_ready, 1)
            act.sem_inc(t_used, 1)

            def ctx_high(n, p, h):
                act.wait_ge(in_ready[p], h * 32 + 32)
                act.wait_ge(p_done, n + 1)
                nc.scalar.activation(ch[:, p], rows(cin[:, p]), ACT.Copy).then_inc(c_high, 1)

            def ctx_gated(n, p, h):
                act.wait_ge(z_ready, n + 1)
                nc.scalar.activation(zc[:, p], rows(cin[:, p]), ACT.Copy, scale=C["gate"][:, 0:1]).then_inc(zc_ready, 1)

            def deviation(n, p, h):
                act.wait_ge(var1, n + 1)
                nc.scalar.activation(sd[:, p], mv[:, p, :, 1], ACT.Sqrt, bias=C["eps"][:]).then_inc(sd1_ready, 1)

            def x_high(n, p, h):
                act.wait_ge(xn_ready, n + 1)
                act.wait_ge(p_done, n + 1)
                nc.scalar.activation(xh[:, p], xnf[:, p], ACT.Copy).then_inc(hi_ready, 1)

            def g_out(n, p, h):
                act.wait_ge(g_done, n + 1)
                act.wait_ge(p_used, n + 1)
                nc.scalar.activation(gs[:], psG[:], ACT.Copy).then_inc(gs_ready, 1)

            def front(n, p, h):
                ctx_high(n, p, h)
                weights()
                deviation(n, p, h)
                x_high(n, p, h)
                ctx_gated(n, p, h)
                g_out(n, p, h)

            def back(n, p, h, ahead):
                if ahead:
                    ctx_high(*ahead)
                    deviation(*ahead)
                act.wait_ge(va_ready, n + 1)
                nc.scalar.activation(sdu[:], va[:], ACT.Sqrt, bias=C["eps"][:]).then_inc(sdu_ready, 1)
                act.wait_ge(ab_ready, n + 1)
                for j in range(NB):
                    last = nc.scalar.activation(w[:, j * D:(j + 1) * D], psU[:, j * D:(j + 1) * D], ACT.Identity,
                                                bias=ab[:, 1, j:j + 1], scale=ab[:, 0, j:j + 1])
                last.then_inc(w_ready, 1)
                if ahead:
                    x_high(*ahead)
                    ctx_gated(*ahead)
                act.wait_ge(var2, n + 1)
                nc.scalar.activation(sd2[:], mv2[:, :, 1], ACT.Sqrt, bias=C["eps"][:]).then_inc(sd2_ready, 1)
                act.wait_ge(x1_ready, n + 2)
                act.dma_start(x2_d[:, bass.ds(n * NB, NB), :], x1[:, p].rearrange("p (a b) -> p a b", b=D)).then_inc(stored[p], 16)
                if ahead:
                    g_out(*ahead)
                act.wait_ge(rs2_ready, n + 1)
                for j in range(NB):
                    r = slice(j * D, (j + 1) * D)
                    last = nc.scalar.activation(xn[:, p, r], x1[:, p, r], ACT.Identity, bias=mr2[:, j:j + 1], scale=rs2[:, j:j + 1])
                last.then_inc(xn2_ready, 1)
                for r in range(KD):
                    act.wait_ge(t_done, n * 2 + (r + 1))
                    if r == 0:
                        act.wait_ge(l_done, n + 1)
                    nc.scalar.activation(rows(xt[:, r * NB:(r + 1) * NB, :]), psT[:], ACT.Copy).then_inc(t_used, 1)
                act.wait_ge(xn2_ready, n + 1)
                act.dma_start(xn_d[:, bass.ds(n * NB, NB), :], xn[:, p].rearrange("p (a b) -> p a b", b=D)).then_inc(stored[p], 16)

            pair, last_back = over_steps(front, back)
            with act.Fori(1, STEPS // 2) as h:
                pair(h)
            last_back()
            for p in range(2):
                act.wait_ge(stored[p], 32 * (STEPS // 2) + 16)

        @block.vector
        def _(dve):
            dve.wait_ge(wz_in, 32)
            nc.vector.scalar_tensor_tensor(bdz[:].rearrange("p (g o) -> p g o", g=GROUPS), C["gsum"][:].rearrange("p (g o) -> p g o", g=GROUPS), float(GROUP),
                                           wz[:].unsqueeze(1).to_broadcast([P, GROUPS, GROUP]), ALU.mult, ALU.mult).then_inc(bdz_up, 1)
            dve.sem_inc(x1_ready, 1)
            dve.sem_inc(p_used, 1)
            for p in range(2):
                dve.sem_inc(stored[p], 16)
            fchain, bchain = Chain(dve, s_front, 2), Chain(dve, s_back, 12)

            def x_stats(n, p, h):
                fchain.start(n)
                dve.wait_ge(in_ready[p], h * 32 + 32)
                for j in range(NB):
                    last = nc.vector.bn_stats(stat[:, j, :], xin[:, p, j, :])
                fchain(last)
                stand(dve, C)
                for j in range(NB):
                    last = nc.vector.bn_aggr(mv[:, p, j, :], stat[:, j, :])
                last.then_inc(var1, 1)

            def x_norm(n, p, h):
                dve.wait_ge(sd1_ready, n + 1)
                fchain(nc.vector.reciprocal(rs[:], sd[:, p]))
                for j in range(NB):
                    last = nc.vector.tensor_scalar(xnf[:, p, j * D:(j + 1) * D], xin[:, p, j, :], mv[:, p, j, 0:1],
                                                   rs[:, j:j + 1], ALU.subtract, ALU.mult)
                last.then_inc(xn_ready, 1)
                fchain.end()

            def front(n, p, h):
                x_stats(n, p, h)
                x_norm(n, p, h)

            def logits(n):
                dve.wait_ge(l_done, n + 2)
                nc.vector.tensor_copy(C["logits0"][:, bass.ds(n * NB, NB), :],
                                      psT[:, 0:NB * E0].rearrange("p (a b) -> p a b", b=E0)).then_inc(lg_copied, 1)

            def back(n, p, h, ahead):
                c = bchain
                c.start(n)
                dve.wait_ge(u_done, n + 1)
                for j in range(NB):
                    last = nc.vector.bn_stats(ustat[:, j, :], psU[:, j * D:(j + 1) * D])
                c(last)
                stand(dve, C)
                for j in range(NB):
                    last = nc.vector.bn_aggr(umv[:, j, :], ustat[:, j, :])
                c(last)
                dve.wait_ge(p_done, n + 3)
                dve.wait_ge(gs_ready, n + 2)
                for j in range(NB):
                    last = nc.vector.tensor_tensor_reduce(junk[:, j * D:(j + 1) * D], psP[:, j * D:(j + 1) * D], gs[:, j * D:(j + 1) * D], 1.0, 0.0,
                                                          ALU.mult, ALU.add, q[:, 0, j:j + 1])
                last.then_inc(p_used, 1)
                nc.vector.tensor_copy(q[:, 1, :], umv[:, :, 0])
                c(nc.vector.tensor_tensor(t1[:], umv[:, :, 0], umv[:, :, 0], ALU.mult))
                nc.vector.tensor_tensor(q[:, 2, :], umv[:, :, 1], t1[:], ALU.add).then_inc(q_ready, 1)
                if ahead:
                    x_stats(*ahead)
                dve.wait_ge(s_ready, n + 1)
                c(nc.vector.tensor_copy(s3[:], psS[:, 0:3 * NB].rearrange("p (a b) -> p a b", b=NB)))
                nc.vector.scalar_tensor_tensor(t1[:], s3[:, 0, :], 4.0, s3[:, 0, :], ALU.mult, ALU.mult)
                c(nc.vector.tensor_tensor(t2[:], s3[:, 1, :], s3[:, 1, :], ALU.mult))
                c(nc.vector.tensor_tensor(t2[:], s3[:, 2, :], t2[:], ALU.subtract))
                nc.vector.tensor_tensor(va[:], t1[:], t2[:], ALU.mult).then_inc(va_ready, 1)
                dve.wait_ge(sdu_ready, n + 1)
                c(nc.vector.reciprocal(t1[:], sdu[:]))
                c(nc.vector.scalar_tensor_tensor(t2[:], s3[:, 0, :], 2.0, t1[:], ALU.mult, ALU.mult))
                if isinstance(n, int) and n == 0:
                    dve.wait_ge(gbt_up, 2)
                c(nc.vector.tensor_scalar(ab[:, 0, :], t2[:], gbt[:, 0:1], None, ALU.mult))
                c(nc.vector.tensor_tensor(t1[:], ab[:, 0, :], s3[:, 1, :], ALU.mult))
                nc.vector.tensor_scalar(ab[:, 1, :], t1[:], -1.0, gbt[:, 1:2], ALU.mult, ALU.add).then_inc(ab_ready, 1)
                if not isinstance(n, int) or n >= 1:
                    logits(n - 1)
                if ahead:
                    x_norm(*ahead)
                dve.wait_ge(w_ready, n + 2)
                dve.wait_ge(z_ready, n + 3)
                dve.wait_ge(stored[p], h * 32 + 16)
                nc.vector.tensor_tensor(x1[:, p], z[:], w[:], ALU.add).then_inc(x1_ready, 1)
                dve.wait_ge(x1_ready, n + 2)
                for j in range(NB):
                    last = nc.vector.bn_stats(stat2[:, j, :], x1[:, p, j * D:(j + 1) * D])
                c(last)
                stand(dve, C)
                for j in range(NB):
                    last = nc.vector.bn_aggr(mv2[:, j, :], stat2[:, j, :])
                last.then_inc(var2, 1)
                dve.wait_ge(sd2_ready, n + 1)
                c(nc.vector.reciprocal(rs2[:], sd2[:]))
                nc.vector.scalar_tensor_tensor(mr2[:], mv2[:, :, 0], -1.0, rs2[:], ALU.mult, ALU.mult).then_inc(rs2_ready, 1)
                c.end()

            pair, last_back = over_steps(front, back)
            with dve.Fori(1, STEPS // 2) as h:
                pair(h)
            last_back()
            logits(STEPS - 1)
            dve.wait_ge(lg_copied, STEPS)

        @block.tensor
        def _(pe):
            pe.sem_inc(p_done, 2)
            pe.sem_inc(l_done, 1)
            pe.wait_ge(bdz_up, 1)
            nc.tensor.matmul(psS[:, 0:P], wt[:], bdz[:], start=True, stop=True).then_inc(w2_made, 1)
            pe.wait_ge(w_split, 1)

            def products(n, p, h):
                def into(out, k, high, low, done):
                    for half in range(W // 512):
                        r = slice(half * 512, half * 512 + 512)
                        last = product(pe, out[:, r], (wh[:, k, :], wl[:, k, :]), (high[:, p, r], low[:, p, r]), True, True)
                    last.then_inc(done, 1)

                pe.wait_ge(lo_ready, n * 2 + 1)
                pe.wait_ge(gs_ready, n + 1)
                into(psG, 1, ch, cl, g_done)
                pe.wait_ge(w_ready, n + 1)
                into(psU, 2, ch, cl, u_done)
                pe.wait_ge(lo_ready, n * 2 + 2)
                pe.wait_ge(p_used, n + 1)
                into(psP, 0, xh, xl, p_done)

            def group_sums(n):
                pe.wait_ge(q_ready, n + 1)
                nc.tensor.matmul(psS[:, 0:3 * NB], C["gsum"][:], q[:].rearrange("p a b -> p (a b)"), start=True, stop=True).then_inc(s_ready, 1)

            def back(n, p, h, ahead):
                group_sums(n)
                if not isinstance(n, int) or n >= 1:
                    logits(n - 1)
                if ahead:
                    products(*ahead)
                pe.wait_ge(xn2_ready, n + 1)
                if not isinstance(n, int) or n >= 1:
                    pe.wait_ge(lg_copied, n)
                for r in range(KD):
                    pe.wait_ge(t_used, n * 2 + (r + 1))
                    for j in range(NB):
                        last = nc.tensor.transpose(psT[:, j * P:(j + 1) * P], xn[:, p, j * D + r * P:j * D + (r + 1) * P], C["ident"][:])
                    last.then_inc(t_done, 1)

            def logits(n):
                pe.wait_ge(t_used, n * 2 + 3)
                for j in range(NB):
                    for r in range(KD):
                        last = nc.tensor.matmul(psT[:, j * E0:(j + 1) * E0], xt[:, r * NB + j, :], wr[:, r, :],
                                                start=(r == 0), stop=(r == KD - 1))
                last.then_inc(l_done, 1)

            pair, last_back = over_steps(products, back)
            with pe.Fori(1, STEPS // 2) as h:
                pair(h)
            last_back()
            logits(STEPS - 1)


def first_of(v, link, values, best, rank, work, top, mask):
    link(v.tensor_tensor(work, values, best.unsqueeze(2).to_broadcast(values.shape), ALU.is_equal))
    link(v.tensor_tensor(work, work, rank.unsqueeze(1).to_broadcast(values.shape), ALU.mult))
    link(v.tensor_reduce(top, work, AX.X, ALU.max))
    return v.tensor_tensor(mask, work, top.unsqueeze(2).to_broadcast(values.shape), ALU.is_equal)


def load_expert(eng, A, raw, e, k):
    blocks = (KD, F0 // P)[k]
    return eng.dma_start(raw[:, k].rearrange("p (k f) -> p k f", k=blocks), A[("wi", "wo")[k]][bass.ds(e, 1)].rearrange("a (k p) f -> p (a k) f", p=P))


def route(nc, A, C, held, raw):
    NI = HALVES * 2 * TILES
    MK = HALVES * E0 * 2 * TILES
    V = 5
    with ExitStack() as ctx:
        m = Space(nc, ctx, "route")
        sb, ps, sem = m.sb, m.ps, m.sem
        lg = C["logits0"]
        mx = sb("mx", [P, B])
        pr = sb("pr", [P, B, E0])
        sm = sb("sm", [P, B])
        best = sb("best", [P, 2, B])
        work = sb("work", [P, B, E0])
        top = sb("top", [P, B])
        mask = sb("mask", [P, 2, B, E0])
        p2 = sb("p2", [P, B, E0])
        rank = sb("rank", [P, E0])
        mk = sb("mk", [P, HALVES, E0, 2, TILES])
        reset = sb("reset", [P, HALVES * E0, 2 * TILES])
        tot = sb("tot", [P, MK])
        upto = sb("upto", [P, MK])
        pos = sb("pos", [P, HALVES, E0, 2, TILES])
        posk = sb("posk", [P, HALVES, 2, TILES])
        parts = sb("parts", [P, 3, NI], BF16)
        rest = sb("rest", [P, 2, NI])
        gk = sb("gk", [P, HALVES, 2, TILES])
        tileno = sb("tileno", [P, HALVES, 2, TILES])
        rowno = sb("rowno", [P, 1])
        val = sb("val", [P, V, NI], BF16)
        rhs = sb("rhs", [P, NI, E0, V], BF16)
        place = sb("place", [P, CAP])
        onehot = sb("onehot", [P, NI, CAP], BF16)
        tab = sb("tab", [SLOTS, PARTS, E0, V])
        free = sb("free", [SLOTS, 1])
        nfree = sb("nfree", [SLOTS, 1])
        f = sb("f", [SLOTS, PARTS, E0])
        ix = sb("ix", [SLOTS, PARTS, E0])
        psC, psN = ps("psC", [P, MK]), ps("psN", [P, MK])
        psTab = ps("psTab", [SLOTS, PARTS, E0 * V])
        iotas, l_sub, e_up, mk_up, counted, hot, tabled, step = (sem(n) for n in ("iotas", "l_sub", "e_up", "mk_up", "counted", "hot", "tabled", "step"))
        raw_in = sem("raw_in")
        held.stage(ctx)
        block = ctx.enter_context(nc.Block())

        @block.gpsimd
        def _(pool):
            small = dict(allow_small_or_imprecise_dtypes=True)
            nc.gpsimd.iota(rank[:], [[-1, E0]], base=E0, channel_multiplier=0, **small)
            nc.gpsimd.iota(place[:], [[1, CAP]], base=0, channel_multiplier=0, **small)
            nc.gpsimd.iota(tileno[:], [[TILES, HALVES], [0, 2], [1, TILES]], base=1, channel_multiplier=0, **small)
            nc.gpsimd.iota(rowno[:], [[0, 1]], base=0, channel_multiplier=1, **small)
            nc.gpsimd.iota(free[:], [[0, 1]], base=DUMMY, channel_multiplier=1, **small)
            nc.gpsimd.iota(nfree[:], [[0, 1]], base=-DUMMY - P, channel_multiplier=-1, **small)
            nc.gpsimd.memset(reset[:], 1.0).then_inc(iotas, 1)
            pool.wait_ge(iotas, 1)
            nc.gpsimd.memset(reset[:, :, 0:1], 0.0).then_inc(iotas, 1)
            pool.wait_ge(iotas, 2)
            held.gpsimd(pool)

        @block.sync
        def _(sp):
            for k in range(2):
                load_expert(sp, A, raw, 0, k).then_inc(raw_in, 16)
            held.sync(sp)
            sp.wait_ge(raw_in, 32)

        @block.scalar
        def _(act):
            act.wait_ge(l_sub, 1)
            nc.scalar.activation(pr[:], pr[:], ACT.Exp).then_inc(e_up, 1)
            held.scalar(act)

        @block.tensor
        def _(pe):
            held.tensor(pe)
            pe.wait_ge(mk_up, 1)
            flat = mk[:].rearrange("p h e k t -> p (h e k t)")
            nc.tensor.matmul(psC[:], C["tri"][:], flat, start=True, stop=True)
            nc.tensor.matmul(psN[:], C["ones"][:], flat, start=True, stop=True).then_inc(counted, 1)
            for h in range(HALVES):
                for part in range(CAP // SLOTS):
                    for i in range(2 * TILES):
                        if part == 0 and i % TILES == 0:
                            pe.wait_ge(hot, h * 2 + i // TILES + 1)
                        n = h * 2 * TILES + i
                        last = nc.tensor.matmul(psTab[:, h * (CAP // SLOTS) + part, :], onehot[:, n, part * SLOTS:(part + 1) * SLOTS],
                                                rhs[:, n].rearrange("p e v -> p (e v)"), start=(i == 0), stop=(i == 2 * TILES - 1))
            last.then_inc(tabled, 1)

        @block.vector
        def _(dve):
            link = Chain(dve, step, 0)
            bc = lambda a: a.unsqueeze(2).to_broadcast([P, B, E0])
            v = nc.vector
            dve.wait_ge(iotas, 2)
            link(v.tensor_reduce(mx[:], lg[:], AX.X, ALU.max))
            v.tensor_tensor(pr[:], lg[:], bc(mx[:]), ALU.subtract).then_inc(l_sub, 1)
            dve.wait_ge(e_up, 1)
            link(v.tensor_reduce(sm[:], pr[:], AX.X, ALU.add))
            link(v.reciprocal(sm[:], sm[:]))
            link(v.tensor_tensor(pr[:], pr[:], bc(sm[:]), ALU.mult))
            link(v.tensor_reduce(best[:, 0, :], pr[:], AX.X, ALU.max))
            link(first_of(v, link, pr[:], best[:, 0, :], rank[:], work[:], top[:], mask[:, 0]))
            link(v.scalar_tensor_tensor(rows(p2), rows(mask[:, 0]), -2.0, rows(pr), ALU.mult, ALU.add))
            link(v.tensor_reduce(best[:, 1, :], p2[:], AX.X, ALU.max))
            link(first_of(v, link, p2[:], best[:, 1, :], rank[:], work[:], top[:], mask[:, 1]))
            for k in range(2):
                for h in range(HALVES):
                    last = v.tensor_copy(mk[:, h, :, k, :], mask[:, k, h * TILES:(h + 1) * TILES, :].rearrange("p t e -> p e t"))
            last.then_inc(mk_up, 1)
            for k in range(2):
                last = v.tensor_copy(gk[:, :, k, :], best[:, k, :].rearrange("p (h t) -> p h t", h=HALVES))
            link(last)
            g = gk[:].rearrange("p h k t -> p (h k t)")
            link(v.tensor_copy(parts[:, 0], g))
            link(v.tensor_tensor(rest[:, 0], g, parts[:, 0], ALU.subtract))
            link(v.tensor_copy(parts[:, 1], rest[:, 0]))
            link(v.tensor_tensor(rest[:, 1], rest[:, 0], parts[:, 1], ALU.subtract))
            v.tensor_copy(val[:, 0], tileno[:].rearrange("p h k t -> p (h k t)"))
            v.tensor_copy(val[:, 1], rowno[:].to_broadcast([P, NI]))
            v.tensor_copy(val[:, 2:4], parts[:, 0:2])
            link(v.tensor_copy(val[:, 4], rest[:, 1]))
            for h in range(HALVES):
                r = slice(h * 2 * TILES, (h + 1) * 2 * TILES)
                for n in range(V):
                    last = v.tensor_tensor(rhs[:, r, :, n], mk[:, h].rearrange("p e k t -> p (k t) e"),
                                           val[:, n, r].unsqueeze(2).to_broadcast([P, 2 * TILES, E0]), ALU.mult)
            link(last)
            dve.wait_ge(counted, 1)
            link(v.tensor_copy(tot[:], psN[:]))
            link(v.tensor_tensor_scan(upto[:], reset[:].rearrange("p a b -> p (a b)"), tot[:], 0.0, ALU.mult, ALU.add))
            link(v.tensor_tensor(upto[:], upto[:], tot[:], ALU.subtract))
            flat = pos[:].rearrange("p h e k t -> p (h e k t)")
            link(v.scalar_tensor_tensor(flat, psC[:], -1.0, upto[:], ALU.add, ALU.add))
            link(v.tensor_tensor(flat, flat, mk[:].rearrange("p h e k t -> p (h e k t)"), ALU.mult))
            for h in range(HALVES):
                last = v.tensor_reduce(posk[:, h].rearrange("p k t -> p (k t)"), pos[:, h].rearrange("p e k t -> p (k t) e"), AX.X, ALU.add)
            link(last)
            pk = posk[:].rearrange("p h k t -> p (h k t)")
            for c in range(4):
                r = slice(c * NI // 4, (c + 1) * NI // 4)
                v.tensor_tensor(onehot[:, r], place[:].unsqueeze(1).to_broadcast([P, NI // 4, CAP]),
                                pk[:, r].unsqueeze(2).to_broadcast([P, NI // 4, CAP]), ALU.is_equal).then_inc(hot, 1)
            dve.wait_ge(tabled, 1)
            link(v.tensor_copy(tab[:].rearrange("p a e v -> p a (e v)"), psTab[:]))
            v.tensor_scalar(f[:], tab[:, :, :, 0], 0.0, None, ALU.is_gt)
            link(v.scalar_tensor_tensor(ix[:], tab[:, :, :, 0], float(P), tab[:, :, :, 1], ALU.mult, ALU.add))
            link(v.tensor_scalar(f[:], f[:], nfree[:], free[:], ALU.mult, ALU.add))
            link(v.tensor_tensor(ix[:], ix[:], f[:], ALU.add))
            link(v.tensor_copy(C["slot_row"][:].rearrange("p e a -> p a e"), ix[:]))
            link(v.tensor_tensor(f[:], tab[:, :, :, 4], tab[:, :, :, 3], ALU.add))
            link(v.tensor_tensor(f[:], f[:], tab[:, :, :, 2], ALU.add))
            link(v.tensor_scalar(C["slot_weight"][:].rearrange("p e a -> p a e"), f[:], C["gate"][0:SLOTS, 2:3], None, ALU.mult))


def experts(nc, A, C, X2, XN, raw):
    N = PARTS * SLOTS
    NF = F0 // P
    with ExitStack() as ctx:
        m = Space(nc, ctx, "experts")
        sb, ps, sem = m.sb, m.ps, m.sem
        wih = sb("wih", [P, 2, KD, F0], F32R)
        wil = sb("wil", [P, 2, KD, F0], F32R)
        woh = sb("woh", [P, 2, NF, D], F32R)
        wol = sb("wol", [P, 2, NF, D], F32R)
        row_in, row_out = (sb(n, [SLOTS, 2, PARTS], I32) for n in ("row_in", "row_out"))
        xg = sb("xg", [SLOTS, 2, PARTS, D])
        xth = sb("xth", [P, 2, KD, N], F32R)
        xtl = sb("xtl", [P, 2, KD, N], F32R)
        hh = sb("hh", [P, NF, N], F32R)
        hl = sb("hl", [P, NF, N], F32R)
        yt = sb("yt", [P, KD, N])
        yg = sb("yg", [SLOTS, 2, PARTS, D])
        psX = [ps(f"psX{k}", [P, 512]) for k in range(KD)]
        psH = [ps(f"psH{k}", [P, 512]) for k in range(4)]
        psY = ps("psY", [SLOTS, PARTS, D])
        w_in = [sem("wi_in"), sem("wo_in")]
        w_hi, w_lo, row_in_up, row_out_up = (sem(n) for n in ("w_hi", "w_lo", "row_in_up", "row_out_up"))
        gathered = [sem(f"gathered{p}") for p in range(2)]
        added = [sem(f"added{p}") for p in range(2)]
        xt_done, x_hi, x_lo, h_done, h_hi, h_lo, y_done, yt_up, y_turned, y_up = (
            sem(n) for n in ("xt_done", "x_hi", "x_lo", "h_done", "h_hi", "h_lo", "y_done", "yt_up", "y_turned", "y_up"))
        block = ctx.enter_context(nc.Block())
        PAIRS_OF = E0 // 2

        def over(eng, body):
            body(0, 0, 0)
            body(1, 1, 0)
            with eng.Fori(1, PAIRS_OF - 1) as h:
                body(h * 2, 0, h)
                body(h * 2 + 1, 1, h)
            body(E0 - 2, 0, PAIRS_OF - 1)

        def later(e, first):
            return not isinstance(e, int) or e >= first

        @block.sync
        def _(sp):
            def load(e, p, h):
                for k in range(2):
                    sp.wait_ge(w_lo, e * 2 + (k + 1))
                    load_expert(sp, A, raw, e, k).then_inc(w_in[k], 16)

            for k in range(2):
                sp.sem_inc(w_in[k], 16)
            load(1, 1, 0)
            with sp.Fori(1, PAIRS_OF - 1) as h:
                load(h * 2, 0, h)
                load(h * 2 + 1, 1, h)
            load(E0 - 2, 0, PAIRS_OF - 1)
            load(E0 - 1, 1, PAIRS_OF - 1)

        @block.gpsimd
        def _(pool):
            def rows_of(e, to, up):
                nc.gpsimd.tensor_copy(to, C["slot_row"][:, bass.ds(e, 1), :].rearrange("p e a -> p (e a)")).then_inc(up, 1)
                pool.wait_ge(up, e + 1)

            def gather(e, p):
                pool.wait_ge(xt_done, e + 1)
                rows_of(e, row_in[:, p], row_in_up)
                stand(pool, C)
                for a in range(PARTS):
                    nc.gpsimd.indirect_dma_start(out=xg[:, p, a, :], out_offset=None, in_=XN,
                                                 in_offset=bass.IndirectOffsetOnAxis(ap=row_in[:, p, a:a + 1], axis=0)).then_inc(gathered[p], 16)

            def add(e, p, h):
                if later(e, 1):
                    pool.wait_ge(added[1 - p], (h + p) * 16 * PARTS)
                rows_of(e, row_out[:, p], row_out_up)
                pool.wait_ge(y_up, e + 2)
                stand(pool, C)
                for a in range(PARTS):
                    nc.gpsimd.indirect_dma_start(out=X2, out_offset=bass.IndirectOffsetOnAxis(ap=row_out[:, p, a:a + 1], axis=0),
                                                 in_=yg[:, p, a, :], in_offset=None, compute_op=ALU.add).then_inc(added[p], 16)

            gather(0, 0)
            gather(1, 1)

            def body(e, p, h):
                if not isinstance(e, int) or e + 2 < E0:
                    gather(e + 2, p)
                add(e, p, h)

            over(pool, body)
            add(E0 - 1, 1, PAIRS_OF - 1)
            for p in range(2):
                pool.wait_ge(added[p], PAIRS_OF * 16 * PARTS)

        @block.scalar
        def _(act):
            act.sem_inc(y_up, 1)

            def weights(e, p, h):
                act.wait_ge(y_done, e + 1)
                act.wait_ge(w_in[0], e * 16 + 16)
                nc.scalar.activation(wih[:, p].rearrange("p a b -> p (a b)"), raw[:, 0], ACT.Copy).then_inc(w_hi, 1)
                act.wait_ge(w_in[1], e * 16 + 16)
                nc.scalar.activation(woh[:, p].rearrange("p a b -> p (a b)"), raw[:, 1], ACT.Copy).then_inc(w_hi, 1)

            def x_high(e, p, h):
                act.wait_ge(xt_done, e + 3)
                for k in range(KD):
                    last = nc.scalar.activation(xth[:, p, k, :], psX[k][:, 0:N], ACT.Copy)
                last.then_inc(x_hi, 1)

            def relu(e, start, end):
                for n in range(start, end):
                    act.wait_ge(h_done, e * NF + (n + 1))
                    nc.scalar.activation(hh[:, n, :], psH[n % 4][:, 0:N], ACT.Relu).then_inc(h_hi, 1)

            def y_copy(e):
                act.wait_ge(y_done, e + 3)
                for k in range(KD):
                    last = nc.scalar.activation(yt[:, k, :], psX[k][:, 0:N], ACT.Copy)
                last.then_inc(yt_up, 1)

            def weigh(e, p, h):
                act.wait_ge(y_turned, e + 1)
                if later(e, 2):
                    act.wait_ge(added[p], h * 16 * PARTS)
                for a in range(PARTS):
                    last = nc.scalar.activation(yg[:, p, a, :], psY[:, a, :], ACT.Copy,
                                                scale=C["slot_weight"][:, bass.ds(e, 1), a:a + 1].rearrange("p e a -> p (e a)"))
                last.then_inc(y_up, 1)

            weights(0, 0, 0)
            x_high(0, 0, 0)

            def body(e, p, h):
                relu(e, 0, 4)
                if later(e, 1):
                    weigh(e - 1, 1 - p, h + (p - 1))
                relu(e, 4, NF - 2)
                x_high(e + 1, 1 - p, h + p)
                relu(e, NF - 2, NF)
                weights(e + 1, 1 - p, h + p)
                y_copy(e)

            over(act, body)
            relu(E0 - 1, 0, 4)
            weigh(E0 - 2, 0, PAIRS_OF - 1)
            relu(E0 - 1, 4, NF)
            y_copy(E0 - 1)
            weigh(E0 - 1, 1, PAIRS_OF - 1)

        @block.vector
        def _(dve):
            dve.sem_inc(w_lo, 2)
            dve.sem_inc(h_lo, 4)

            def weights(e, p, h):
                dve.wait_ge(w_hi, e * 2 + 1)
                nc.vector.tensor_tensor(wil[:, p].rearrange("p a b -> p (a b)"), raw[:, 0], wih[:, p].rearrange("p a b -> p (a b)"), ALU.subtract).then_inc(w_lo, 1)
                dve.wait_ge(w_hi, e * 2 + 2)
                nc.vector.tensor_tensor(wol[:, p].rearrange("p a b -> p (a b)"), raw[:, 1], woh[:, p].rearrange("p a b -> p (a b)"), ALU.subtract).then_inc(w_lo, 1)

            def x_low(e, p, h):
                dve.wait_ge(x_hi, e + 1)
                for k in range(KD):
                    last = nc.vector.tensor_tensor(xtl[:, p, k, :], psX[k][:, 0:N], xth[:, p, k, :], ALU.subtract)
                last.then_inc(x_lo, 1)

            def relu(e, start, end):
                for n in range(start, end):
                    dve.wait_ge(h_hi, e * NF + (n + 1))
                    nc.vector.scalar_tensor_tensor(hl[:, n, :], psH[n % 4][:, 0:N], 0.0, hh[:, n, :], ALU.max, ALU.subtract).then_inc(h_lo, 1)

            weights(0, 0, 0)
            x_low(0, 0, 0)

            def body(e, p, h):
                relu(e, 0, NF - 2)
                x_low(e + 1, 1 - p, h + p)
                relu(e, NF - 2, NF)
                weights(e + 1, 1 - p, h + p)

            over(dve, body)
            relu(E0 - 1, 0, NF)

        @block.tensor
        def _(pe):
            pe.sem_inc(y_done, 2)
            pe.sem_inc(xt_done, 2)

            def turn(e, p, h):
                pe.wait_ge(gathered[p], (h + 1) * 16 * PARTS)
                if later(e, 2):
                    pe.wait_ge(yt_up, e - 1)
                for k in range(KD):
                    for a in range(PARTS):
                        last = nc.tensor.transpose(psX[k][:, a * SLOTS:(a + 1) * SLOTS], xg[:, p, a, k * P:(k + 1) * P], C["ident"][0:SLOTS, 0:SLOTS])
                last.then_inc(xt_done, 1)

            def up(e, p, start, end):
                if start == 0:
                    pe.wait_ge(w_lo, e * 2 + 4)
                    pe.wait_ge(x_lo, e + 1)
                for n in range(start, end):
                    f = slice(n * P, (n + 1) * P)
                    pe.wait_ge(h_lo, e * NF + (n + 1))
                    for k in range(KD):
                        last = product(pe, psH[n % 4][:, 0:N], (wih[:, p, k, f], wil[:, p, k, f]), (xth[:, p, k, :], xtl[:, p, k, :]), k == 0, k == KD - 1)
                    last.then_inc(h_done, 1)

            def down(e, p, ahead):
                if ahead:
                    pe.wait_ge(x_lo, e + 2)
                for k in range(KD):
                    for n in range(NF):
                        if k == 0:
                            pe.wait_ge(h_lo, e * NF + (n + 5))
                        r = slice(k * P, (k + 1) * P)
                        last = product(pe, psX[k][:, 0:N], (woh[:, p, n, r], wol[:, p, n, r]), (hh[:, n, :], hl[:, n, :]), n == 0, n == NF - 1)
                last.then_inc(y_done, 1)

            def turn_back(e):
                pe.wait_ge(yt_up, e + 1)
                pe.wait_ge(y_up, e + 1)
                for a in range(PARTS):
                    for k in range(KD):
                        last = nc.tensor.transpose(psY[:, a, k * P:(k + 1) * P], yt[:, k, a * SLOTS:(a + 1) * SLOTS], C["ident"][:])
                last.then_inc(y_turned, 1)

            turn(0, 0, 0)

            def body(e, p, h):
                up(e, p, 0, 2)
                if later(e, 1):
                    turn_back(e - 1)
                up(e, p, 2, 5)
                turn(e + 1, 1 - p, h + p)
                up(e, p, 5, NF)
                down(e, p, True)

            over(pe, body)
            up(E0 - 1, 1, 0, 2)
            turn_back(E0 - 2)
            up(E0 - 1, 1, 2, NF)
            down(E0 - 1, 1, False)
            turn_back(E0 - 1)


BUCKETS, MAX_DISTANCE = 32, 128


def bucket_onehot():
    exact = BUCKETS // 2
    d = np.maximum(S - 1 - np.arange(2 * S), 0)
    large = exact + (np.log(np.maximum(d, 1) / exact) / np.log(MAX_DISTANCE / exact) * (BUCKETS - exact)).astype(np.int32)
    bucket = np.where(d < exact, d, np.minimum(large, BUCKETS - 1))
    return (np.arange(BUCKETS)[:, None] == bucket[None, :]).astype(np.float32)


UNITS = 2
UB, UH = PAIRS // UNITS, HEADS // UNITS
UW = UH * P


class AttendHeld:

    def __init__(self, nc, ctx, A, VB):
        m = Space(nc, ctx, "held")
        self.nc, self.A, self.VB = nc, A, VB
        size = 2 * HEADS * DH
        self.all_high, self.all_low = (m.sb(n, [P, 4 * size], F32R) for n in ("high", "low"))
        self.high = [self.all_high[:, k * size:(k + 1) * size] for k in range(4)]
        self.low = [self.all_low[:, k * size:(k + 1) * size] for k in range(4)]
        self.bias = m.sb("bias", [P, UNITS, UW])

    def stage(self, ctx):
        m = Space(self.nc, ctx, "making")
        self.raw = [m.sb(f"raw{k}", [P, 2 * HEADS * DH]) for k in range(2)]
        self.rel = m.sb("rel", [BUCKETS, HEADS])
        self.hot = m.sb("hot", [BUCKETS, 2 * P])
        self.vb = m.sb("vb", [HEADS, 2 * P])
        self.mask8 = m.sb("mask8", [P, P], mybir.dt.uint8)
        self.mask = m.sb("mask", [P, P])
        self.psV = m.ps("psV", [P, 512])
        self.raw_in = [m.sem(f"raw_in{k}") for k in range(2)]
        self.w_hi, self.w_lo, self.rel_in, self.vb_done, self.vb_up, self.vb_out, self.bias_in, self.mask_in, self.bias_up = (
            m.sem(n) for n in ("w_hi", "w_lo", "rel_in", "vb_done", "vb_up", "vb_out", "bias_in", "mask_in", "bias_up"))

    def sync(self, sp):
        A, VB = self.A, self.VB
        sp.dma_start(self.rel[:], A["relT"]).then_inc(self.rel_in, 16)
        sp.dma_start(self.hot[:], A["hot"]).then_inc(self.rel_in, 16)
        sp.dma_start(self.mask8[:], A["mask"]).then_inc(self.mask_in, 16)
        for k, name in enumerate(("Wq", "Wk", "Wv", "Wo")):
            if k >= 2:
                sp.wait_ge(self.w_lo, k - 1)
            blocks = PAIRS if name == "Wo" else KD
            sp.dma_start(self.raw[k % 2][:].rearrange("p (k n) -> p k n", k=blocks), A[name].rearrange("(k p) n -> p k n", p=P)).then_inc(self.raw_in[k % 2], 16)
            if k == 1:
                sp.wait_ge(self.vb_up, 1)
                sp.dma_start(VB, self.vb[:].unsqueeze(1).to_broadcast([HEADS, P, 2 * P])).then_inc(self.vb_out, 16)
                sp.wait_ge(self.vb_out, 16)
                for g in range(UNITS):
                    for r in range(2):
                        sp.dma_start(self.bias[:, g, r * UW // 2:(r + 1) * UW // 2].rearrange("p (m k) -> p m k", m=UB),
                                     bass.AP(VB.tensor, VB.offset + (2 * UB * g + r) * P * 2 * P + P - 1, [[2 * P - 1, P], [2 * P * 2 * P, UB], [1, P]])).then_inc(self.bias_in, 16)

    def tensor(self, pe):
        pe.wait_ge(self.rel_in, 32)
        self.nc.tensor.matmul(self.psV[0:HEADS, 0:2 * P], self.rel[:], self.hot[:], start=True, stop=True).then_inc(self.vb_done, 1)

    def scalar(self, act):
        act.wait_ge(self.vb_done, 1)
        self.nc.scalar.activation(self.vb[:], self.psV[0:HEADS, 0:2 * P], ACT.Copy).then_inc(self.vb_up, 1)
        for k in range(4):
            act.wait_ge(self.raw_in[k % 2], 16 * (k // 2 + 1))
            self.nc.scalar.activation(self.high[k], self.raw[k % 2][:], ACT.Copy).then_inc(self.w_hi, 1)

    def gpsimd(self, pool):
        nc = self.nc
        for k in range(4):
            pool.wait_ge(self.w_hi, k + 1)
            nc.gpsimd.tensor_tensor(self.low[k], self.raw[k % 2][:], self.high[k], ALU.subtract).then_inc(self.w_lo, 1)
        pool.wait_ge(self.mask_in, 16)
        nc.gpsimd.tensor_copy(self.mask[:], self.mask8[:]).then_inc(self.bias_up, 1)
        pool.wait_ge(self.bias_up, 1)
        nc.gpsimd.tensor_scalar(self.mask[:], self.mask[:], -1.0, -LOWEST, ALU.add, ALU.mult).then_inc(self.bias_up, 1)
        pool.wait_ge(self.bias_up, 2)
        pool.wait_ge(self.bias_in, 16 * 2 * UNITS)
        flat = self.bias[:].rearrange("p g (a k) -> p (g a) k", k=P)
        nc.gpsimd.tensor_tensor(flat, flat, self.mask[:].unsqueeze(1).to_broadcast([P, HEADS, P]), ALU.add).then_inc(self.bias_up, 1)
        pool.wait_ge(self.bias_up, 3)
        pool.wait_ge(self.w_lo, 4)


def attend(nc, A, C, held, X2, acc, stat3):
    STEPS, NB = B // 2, 2
    N = NB * P
    SCALE = DH ** -0.5
    CHUNK = 8
    with ExitStack() as ctx:
        m_ = Space(nc, ctx, "attend")
        sb, ps, sem = m_.sb, m_.ps, m_.sem
        wqh, wkh, wvh, woh, wql, wkl, wvl, wol = (
            w.rearrange("p (k n) -> p k n", k=blocks) for half in (held.high, held.low) for w, blocks in zip(half, (KD, KD, KD, PAIRS)))
        bias = held.bias
        q_t, k_t = (sb(n, [P, 2, PAIRS, N]) for n in ("q_t", "k_t"))
        v_n = sb("v_n", [P, 2, NB, HEADS * DH])
        s, pr, pt = (sb(n, [P, UNITS, UH, P]) for n in ("s", "pr", "pt"))
        oh, ol = (sb(n, [P, PAIRS, P], F32R) for n in ("oh", "ol"))
        cin = sb("cin", [P, 2, NB, D])
        xn = sb("xn", [P, NB, D])
        xh, xl, ch, cl = (sb(n, [P, KD, N], F32R) for n in ("xh", "xl", "ch", "cl"))
        stat = sb("stat", [P, B, 6])
        mv = sb("mv", [P, B, 2])
        sd = sb("sd", [P, B])
        rs = sb("rs", [P, B])
        mx, less, sm, rc = (sb(n, [P, UNITS, UH]) for n in ("mx", "less", "sm", "rc"))
        psS = [ps(f"psS{g}", [P, UW]) for g in range(UNITS)]
        psO = [ps(f"psO{g}", [P, UB * P]) for g in range(UNITS)]
        psJ = [ps(f"psJ{k}", [P, 512]) for k in range(2)]

        c_in = [sem(f"c_in{k}") for k in range(2)]
        j_done = [sem(f"j_done{k}") for k in range(2)]
        j_free = [sem(f"j_free{k}") for k in range(2)]
        xn_up, var, sd_up, rs_up = (sem(n) for n in ("xn_up", "var", "sd_up", "rs_up"))
        x_in = [sem(f"x_in{c}") for c in range(B // CHUNK)]
        x_hi, c_hi = sem("x_hi"), sem("c_hi")
        s_done, s_less, e_up, p_up, pt_done, pt_up, o_done, o_hi, o_lo = (
            sem(n) for n in ("s_done", "s_less", "e_up", "p_up", "pt_done", "pt_up", "o_done", "o_hi", "o_lo"))
        s_ln, s_soft = (sem(n) for n in ("s_ln", "s_soft"))
        block = ctx.enter_context(nc.Block())

        x2_d = X2[0:B * S, :].rearrange("(b p) d -> p b d", p=P)
        c_d = A["ctx_1024"].rearrange("b p d -> p b d")

        Q, WO_OLD, K, V0, WO_NEW, V1, TURN = [0, 1, 2, 3], [4], [5, 6, 7, 8], [9, 10], [11], [12, 13], [14, 15]
        ALL = Q + WO_OLD + K + V0 + WO_NEW + V1 + TURN

        BEFORE = [(-2, TURN[1])] + [(-1, u) for u in K + V0 + V1] + [(-2, TURN[0])] + [(-1, u) for u in Q + TURN]

        def uses(n):
            if n == -1:
                return [u for u in ALL if u not in WO_OLD + WO_NEW]
            if n == 0:
                return [u for u in ALL if u not in WO_OLD]
            if n == STEPS - 2:
                return [u for u in ALL if u not in TURN]
            if n == STEPS - 1:
                return WO_OLD + WO_NEW
            return WO_OLD if n == STEPS else ALL

        def uses_before(bank, n):
            return 1 + sum(u % 2 == bank for k in range(-1, n) for u in uses(k))

        def turn_of(n, u):
            bank = u % 2
            if isinstance(n, int) and n < 0:
                return sum(v % 2 == bank for _, v in BEFORE[:BEFORE.index((n, u)) + 1])
            at = sum(v % 2 == bank and v <= u for v in (uses(n) if isinstance(n, int) else ALL))
            if isinstance(n, int):
                return uses_before(bank, n) + at
            return (n - 1) * (len(ALL) // 2) + (uses_before(bank, 1) + at)

        def used(eng, n, u):
            eng.wait_ge(j_done[u % 2], turn_of(n, u))

        def read(eng, n, u):
            eng.wait_ge(j_free[u % 2], turn_of(n, u))

        def over(eng, body, last):
            body(0, 0, 0)
            with eng.Fori(0, (STEPS - 4) // 2) as h:
                body(h * 2 + 1, 1, h)
                body(h * 2 + 2, 0, h + 1)
            for n in range(STEPS - 3, STEPS):
                body(n, n % 2, n // 2)
            last()

        def projects(n):
            return not isinstance(n, int) or n <= STEPS - 2

        def turns(n):
            return not isinstance(n, int) or n <= STEPS - 3

        def later(n):
            return not isinstance(n, int) or n >= 1

        def unit(u):
            return u[0] * UNITS + (u[1] + 1)

        @block.sync
        def _(sp):
            def load(n, p, h):
                if not isinstance(n, int) or n >= 2:
                    used(sp, n - 4, TURN[1])
                sp.dma_start(cin[:, p], c_d[:, bass.ds(n * NB, NB), :]).then_inc(c_in[p], 16)

            load(0, 0, 0)
            for c in range(B // CHUNK):
                r = slice(c * CHUNK, (c + 1) * CHUNK)
                sp.dma_start(acc[:, r, :], x2_d[:, r, :]).then_inc(x_in[c], 16)
            load(1, 1, 0)

            def body(n, p, h):
                if turns(n):
                    load(n + 2, p, h + 1)

            over(sp, body, lambda: None)

        @block.scalar
        def _(act):
            def x_high(n, which=(0, 1)):
                for u, to, done in [((TURN[0], xh, x_hi), (TURN[1], ch, c_hi))[k] for k in which]:
                    used(act, n, u)
                    nc.scalar.activation(to[:].rearrange("p a b -> p (a b)"), psJ[u % 2][:], ACT.Copy).then_inc(done, 1)

            def deviation(chunks, r):
                act.wait_ge(var, chunks)
                nc.scalar.activation(sd[:, r], mv[:, r, 1], ACT.Sqrt, bias=C["eps"][:]).then_inc(sd_up, 1)

            def exps(b, g, part):
                act.wait_ge(s_less, unit((b, g)))
                for j in range(part * UH // 2, (part + 1) * UH // 2):
                    last = nc.scalar.activation(s[:, g, j, :], s[:, g, j, :], ACT.Exp, bias=less[:, g, j:j + 1], accum_out=sm[:, g, j:j + 1])
                if part == 1:
                    last.then_inc(e_up, 1)

            def evacuate(n, u, to):
                used(act, n, u)
                nc.scalar.activation(to, psJ[u % 2][:].rearrange("p (a b) -> p a b", a=to.shape[1]), ACT.Copy).then_inc(j_free[u % 2], 1)

            def qk(n, us, to, p):
                for k, u in enumerate(us):
                    evacuate(n, u, to[:, p, k * 2:k * 2 + 2, :])

            def vs(n, us, i, p):
                for k, u in enumerate(us):
                    evacuate(n, u, v_n[:, p, i:i + 1, k * 512:(k + 1) * 512])

            def p_out(b, g):
                act.wait_ge(pt_done, unit((b, g)))
                nc.scalar.activation(pt[:, g].rearrange("p a b -> p (a b)"), psS[g][:], ACT.Copy).then_inc(pt_up, 1)

            def o_high(b, g):
                act.wait_ge(o_done, unit((b, g)))
                nc.scalar.activation(oh[:, g * UB:(g + 1) * UB].rearrange("p a b -> p (a b)"), psO[g][:], ACT.Copy).then_inc(o_hi, 1)

            x_high(-2, (1,))
            qk(-1, K, k_t, 0)
            deviation(1, slice(0, CHUNK))
            vs(-1, V0, 0, 0)
            vs(-1, V1, 1, 0)
            x_high(-2, (0,))
            qk(-1, Q, q_t, 0)
            x_high(-1)
            deviation(B // CHUNK, slice(CHUNK, B))

            def batch(b, n, fill, outs, late):
                exps(b, 0, 0)
                exps(b, 0, 1)
                if later(b):
                    o_high(b - 1, 0)
                    o_high(b - 1, 1)
                exps(b, 1, 0)
                for do in fill[2:3]:
                    do()
                exps(b, 1, 1)
                for do in fill[3:]:
                    do()
                p_out(b, 0)
                outs()
                p_out(b, 1)
                for do in late:
                    do()

            def copies(n, us, to, p):
                return [lambda k=k, u=u: evacuate(n, u, to(k)) for k, u in enumerate(us)] if projects(n) else []

            def body(n, p, h):
                b = n * 2
                to_q = lambda k: q_t[:, 1 - p, k * 2:k * 2 + 2, :]
                to_k = lambda k: k_t[:, 1 - p, k * 2:k * 2 + 2, :]
                to_k2 = lambda k: k_t[:, 1 - p, 4 + k * 2:6 + k * 2, :]
                to_v0, to_v1 = (lambda k, i=i: v_n[:, 1 - p, i:i + 1, k * 512:(k + 1) * 512] for i in range(2))
                batch(b, n, copies(n, Q, to_q, p), lambda: used(act, n, WO_OLD[0]) if later(n) else None, copies(n, K[0:2], to_k, p))
                batch(b + 1, n, copies(n, K[2:4], to_k2, p) + copies(n, V0, to_v0, p), lambda: used(act, n, WO_NEW[0]),
                      copies(n, V1, to_v1, p) + ([lambda: x_high(n)] if turns(n) else []))

            def last():
                o_high(B - 1, 0)
                o_high(B - 1, 1)

            over(act, body, last)

        @block.vector
        def _(dve):
            dve.sem_inc(xn_up, 2)
            v = nc.vector
            stats, soft = Chain(dve, s_ln, B // CHUNK), Chain(dve, s_soft, 3 * UNITS)

            def statistics(c):
                dve.wait_ge(x_in[c], 16)
                for i in range(CHUNK):
                    last = v.bn_stats(stat[:, c * CHUNK + i, :], acc[:, c * CHUNK + i, :])
                stats(last)
                for i in range(CHUNK):
                    last = v.bn_aggr(mv[:, c * CHUNK + i, :], stat[:, c * CHUNK + i, :])
                last.then_inc(var, 1)

            def scale(k, r):
                dve.wait_ge(sd_up, k)
                v.reciprocal(rs[:, r], sd[:, r]).then_inc(rs_up, 1)
                dve.wait_ge(rs_up, k)

            def norm(n, p, h):
                if not isinstance(n, int) or n >= 1:
                    used(dve, n - 3, TURN[0])
                for i in range(NB):
                    at = bass.ds(n * NB + i, 1)
                    last = v.tensor_scalar(xn[:, i, :], acc[:, at, :].rearrange("p a d -> p (a d)"), mv[:, at, 0:1].rearrange("p a c -> p (a c)"), rs[:, at], ALU.subtract, ALU.mult)
                last.then_inc(xn_up, 1)

            def x_low(n, m, which=(0, 1)):
                for u, high, low, done in [((TURN[0], xh, xl, x_hi), (TURN[1], ch, cl, c_hi))[k] for k in which]:
                    dve.wait_ge(done, m + 1)
                    v.tensor_tensor(low[:].rearrange("p a b -> p (a b)"), psJ[u % 2][:], high[:].rearrange("p a b -> p (a b)"), ALU.subtract).then_inc(j_free[u % 2], 1)

            def biased(b, g):
                dve.wait_ge(s_done, unit((b, g)))
                soft(v.scalar_tensor_tensor(s[:, g].rearrange("p a b -> p (a b)"), psS[g][:], SCALE, bias[:, g], ALU.mult, ALU.add))
                soft(v.tensor_reduce(mx[:, g], s[:, g], AX.X, ALU.max))
                v.tensor_scalar(less[:, g], mx[:, g], -1.0, None, ALU.mult).then_inc(s_less, 1)

            def normed(b, g):
                dve.wait_ge(e_up, unit((b, g)))
                soft(v.reciprocal(rc[:, g], sm[:, g]))
                if later(b):
                    dve.wait_ge(pt_done, b * UNITS + (g - 1))
                v.tensor_tensor(pr[:, g], s[:, g], rc[:, g].unsqueeze(2).to_broadcast([P, UH, P]), ALU.mult).then_inc(p_up, 1)

            def o_low(b, g):
                dve.wait_ge(o_hi, unit((b, g)))
                r = slice(g * UB, (g + 1) * UB)
                v.tensor_tensor(ol[:, r].rearrange("p a b -> p (a b)"), psO[g][:], oh[:, r].rearrange("p a b -> p (a b)"), ALU.subtract).then_inc(o_lo, 1)

            def add(n, u, b):
                row = acc[:, bass.ds(b, 1), :].rearrange("p a d -> p (a d)")
                used(dve, n, u)
                v.scalar_tensor_tensor(row, psJ[u % 2][:, 0:D], C["gate"][:, 1:2], row, ALU.mult, ALU.add).then_inc(j_free[u % 2], 1)
                read(dve, n, u)
                stand(dve, C)
                v.bn_stats(stat3[:, bass.ds(b, 1), :].rearrange("p a s -> p (a s)"), row)

            x_low(-2, 0, (1,))
            statistics(0)
            scale(1, slice(0, CHUNK))
            norm(0, 0, 0)
            x_low(-2, 0, (0,))
            norm(1, 1, 0)
            for c in range(1, B // CHUNK):
                statistics(c)
            x_low(-1, 1)
            scale(2, slice(CHUNK, B))

            def evacuate(n, u, to):
                if projects(n):
                    used(dve, n, u)
                    v.tensor_copy(to, psJ[u % 2][:].rearrange("p (a b) -> p a b", a=to.shape[1])).then_inc(j_free[u % 2], 1)

            def batch(b, n, us, to):
                soft.start(b)
                biased(b, 0)
                biased(b, 1)
                evacuate(n, us[0], to(0))
                normed(b, 0)
                evacuate(n, us[1], to(1))
                if later(b):
                    o_low(b - 1, 0)
                    o_low(b - 1, 1)
                normed(b, 1)

            def body(n, p, h):
                b = n * 2
                batch(b, n, Q[0:2], lambda k: q_t[:, 1 - p, k * 2:k * 2 + 2, :])
                if turns(n):
                    norm(n + 2, p, h + 1)
                if later(n):
                    add(n, WO_OLD[0], b - 1)
                batch(b + 1, n, K[2:4], lambda k: k_t[:, 1 - p, 4 + k * 2:6 + k * 2, :])
                add(n, WO_NEW[0], b)
                if turns(n):
                    x_low(n, n + 2)

            def last():
                o_low(B - 1, 0)
                o_low(B - 1, 1)
                add(STEPS, WO_OLD[0], B - 1)

            over(dve, body, last)

        @block.tensor
        def _(pe):
            def bank(n, u):
                before = turn_of(n, u) - 1
                if not (isinstance(before, int) and before == 0):
                    pe.wait_ge(j_free[u % 2], before)
                return psJ[u % 2]

            def turn(n, m, p, h, which=(0, 1)):
                for u, src, ready in [((TURN[0], xn, lambda: pe.wait_ge(xn_up, m + 3)),
                                       (TURN[1], cin[:, p], lambda: pe.wait_ge(c_in[p], h * 16 + 16)))[k] for k in which]:
                    to = bank(n, u)
                    ready()
                    for k in range(KD):
                        for i in range(NB):
                            last = nc.tensor.transpose(to[:, k * N + i * P:k * N + (i + 1) * P], src[:, i, k * P:(k + 1) * P], C["ident"][:])
                    last.then_inc(j_done[u % 2], 1)

            def qk(n, us, weights, moving, at=0):
                for c, u in enumerate(us):
                    to = bank(n, u)
                    for j in range(2):
                        r = slice((at + c * 2 + j) * P, (at + c * 2 + j + 1) * P)
                        for k in range(KD):
                            last = product(pe, to[:, j * N:(j + 1) * N], [w[:, k, r] for w in weights], [x[:, k, :] for x in moving], k == 0, k == KD - 1)
                    last.then_inc(j_done[u % 2], 1)

            def vs(n, us, i):
                for c, u in enumerate(us):
                    to = bank(n, u)
                    for k in range(KD):
                        last = product(pe, to[:], [x[:, k, i * P:(i + 1) * P] for x in (ch, cl)],
                                       [w[:, k, c * 512:(c + 1) * 512] for w in (wvh, wvl)], k == 0, k == KD - 1)
                    last.then_inc(j_done[u % 2], 1)

            def scores(b, n, p, i, g):
                if i == 0 and g == 0:
                    for u in (Q[2:4] if isinstance(n, int) and n == 0 else V1):
                        read(pe, n - 1, u)
                if later(b):
                    pe.wait_ge(pt_up, b * UNITS + (g - 1))
                q = slice(i * P, (i + 1) * P)
                for j in range(UB):
                    for r in range(2):
                        half = slice(r * DH, (r + 1) * DH)
                        m = g * UB + j
                        last = nc.tensor.matmul(psS[g][:, (r * UB + j) * P:(r * UB + j + 1) * P], q_t[half, p, m, q], k_t[half, p, m, q],
                                                start=True, stop=True)
                last.then_inc(s_done, 1)

            def turn_p(b, g):
                pe.wait_ge(p_up, unit((b, g)))
                for j in range(UH):
                    last = nc.tensor.transpose(psS[g][:, j * P:(j + 1) * P], pr[:, g, j, :], C["ident"][:])
                last.then_inc(pt_done, 1)

            def values(b, p, i, g):
                pe.wait_ge(pt_up, unit((b, g)))
                if later(b):
                    pe.wait_ge(o_lo, b * UNITS + (g - 1))
                for j in range(UB):
                    for r in range(2):
                        head = 2 * (g * UB + j) + r
                        last = nc.tensor.matmul(psO[g][r * DH:(r + 1) * DH, j * P:(j + 1) * P], v_n[:, p, i, head * DH:(head + 1) * DH],
                                                pt[:, g, r * UB + j, :], start=True, stop=True)
                last.then_inc(o_done, 1)

            def out(b, n, u):
                to = bank(n, u)
                pe.wait_ge(o_lo, unit((b, 1)))
                for m in range(PAIRS):
                    last = product(pe, to[:, 0:D], (oh[:, m, :], ol[:, m, :]), (woh[:, m, :], wol[:, m, :]), m == 0, m == PAIRS - 1)
                last.then_inc(j_done[u % 2], 1)

            turn(-2, 0, 0, 0, (1,))
            qk(-1, K, (wkh, wkl), (ch, cl))
            vs(-1, V0, 0)
            vs(-1, V1, 1)
            turn(-2, 0, 0, 0, (0,))
            qk(-1, Q, (wqh, wql), (xh, xl))
            turn(-1, 1, 1, 0)

            def body(n, p, h):
                b = n * 2
                scores(b, n, p, 0, 0)
                scores(b, n, p, 0, 1)
                if later(n):
                    values(b - 1, 1 - p, 1, 0)
                    values(b - 1, 1 - p, 1, 1)
                if projects(n):
                    qk(n, Q, (wqh, wql), (xh, xl))
                turn_p(b, 0)
                if later(n):
                    out(b - 1, n, WO_OLD[0])
                turn_p(b, 1)
                if projects(n):
                    qk(n, K[0:2], (wkh, wkl), (ch, cl))
                scores(b + 1, n, p, 1, 0)
                scores(b + 1, n, p, 1, 1)
                values(b, p, 0, 0)
                values(b, p, 0, 1)
                if projects(n):
                    qk(n, K[2:4], (wkh, wkl), (ch, cl), 4)
                    vs(n, V0, 0)
                turn_p(b + 1, 0)
                out(b, n, WO_NEW[0])
                turn_p(b + 1, 1)
                if projects(n):
                    vs(n, V1, 1)
                if turns(n):
                    turn(n, n + 2, p, h + 1)

            def last():
                values(B - 1, 1, 1, 0)
                values(B - 1, 1, 1, 1)
                out(B - 1, STEPS, WO_OLD[0])

            over(pe, body, last)


BLOCK = 4
BLOCKS = B // BLOCK


class GatedHeld:

    def __init__(self, nc, ctx, A, held, acc, stat3):
        m = Space(nc, ctx, "gheld")
        self.nc, self.A, self.acc, self.stat3 = nc, A, acc, stat3
        self.xth, self.xtl = (t[:].rearrange("p (k n) -> p k n", k=KD) for t in (held.all_high, held.all_low))
        self.raw = m.sb("raw", [P, 2, 3, KD, I1])
        self.wh = m.sb("wh", [P, 2, 3, KD, I1], F32R)
        self.wl = m.sb("wl", [P, 2, 3, KD, I1], F32R)
        self.sg = m.sb("sg", [P, 2, BLOCK * P])
        self.it = m.sb("it", [P, 2, BLOCK * P])
        self.ih = m.sb("ih", [P, 2, BLOCK * P], F32R)
        self.il = m.sb("il", [P, 2, BLOCK * P], F32R)
        n = B // 2
        self.score = m.sb("score", [P, B, E1])
        self.eb, self.rank = m.sb("eb", [P, E1]), m.sb("rank", [P, E1])
        self.tmp, self.work, self.pick = (m.sb(t, [P, n, E1]) for t in ("tmp", "work", "pick"))
        self.hi2, self.lo2 = m.sb("hi2", [P, n, NG, 2]), m.sb("lo2", [P, n, NG, 2])
        self.gs, self.gwork, self.g1, self.g2 = (m.sb(t, [P, n, NG]) for t in ("gs", "gwork", "g1", "g2"))
        self.top, self.best = m.sb("top", [P, n]), m.sb("best", [P, n])

    def part(self, t, p):
        return t[:, p].rearrange("p a k i -> p (a k i)")

    def load(self, eng, e, p):
        return eng.dma_start(self.part(self.raw, p), self.A["gex"][bass.ds(e, 1)].rearrange("a p n -> p (a n)"))

    def high(self, p):
        return self.nc.scalar.activation(self.part(self.wh, p), self.part(self.raw, p), ACT.Copy)

    def low(self, p):
        return self.nc.gpsimd.tensor_tensor(self.part(self.wl, p), self.part(self.raw, p), self.part(self.wh, p), ALU.subtract)

    def up(self, pe, p, at, psG, psU, g_done, u_done):
        for a, to, done in ((0, psG, g_done), (1, psU, u_done)):
            for k in range(KD):
                last = product(pe, to[:], (self.wh[:, p, a, k, :], self.wl[:, p, a, k, :]), (self.xth[:, k, at], self.xtl[:, k, at]), k == 0, k == KD - 1)
            last.then_inc(done, 1)

    def down(self, pe, p, j, psY):
        w = [x[:, p, 2].rearrange("p k i -> p (k i)") for x in (self.wh, self.wl)]
        for i in range(BLOCK):
            r = slice(i * P, (i + 1) * P)
            last = product(pe, psY[:, i, :], (self.ih[:, j % 2, r], self.il[:, j % 2, r]), w, True, True)
        return last


NG = E1 // 4
TAKEN = -1e30


def weight_stages(v, link, C, G, half):
    n = B // 2
    part = slice(half * n, (half + 1) * n)
    score = G.score[:, part, :]
    tmp, work, pick, hi2, lo2, gs, gwork, g1, g2, top, best = (
        x[:] for x in (G.tmp, G.work, G.pick, G.hi2, G.lo2, G.gs, G.gwork, G.g1, G.g2, G.top, G.best))
    rank = G.rank[:]

    def group_scores():
        link(v.tensor_tensor(tmp, score, G.eb[:].unsqueeze(1).to_broadcast([P, n, E1]), ALU.add))
        four = tmp.rearrange("p t (g a b) -> p (t g) a b", g=NG, a=2)
        flat = lambda x: x.rearrange("p t g a -> p (t g) a")
        v.tensor_tensor(flat(hi2), four[:, :, :, 0], four[:, :, :, 1], ALU.max)
        link(v.tensor_tensor(flat(lo2), four[:, :, :, 0], four[:, :, :, 1], ALU.min))
        v.tensor_tensor(gs, hi2[:, :, :, 0], hi2[:, :, :, 1], ALU.max)
        v.tensor_tensor(g1, hi2[:, :, :, 0], hi2[:, :, :, 1], ALU.min)
        link(v.tensor_tensor(g2, lo2[:, :, :, 0], lo2[:, :, :, 1], ALU.max))
        link(v.tensor_tensor(g1, g1, g2, ALU.max))
        link(v.tensor_tensor(gs, gs, g1, ALU.add))

    def two_groups():
        link(v.tensor_reduce(best, gs, AX.X, ALU.max))
        link(first_of(v, link, gs, best, rank[:, 0:NG], gwork, top, g1))
        link(v.scalar_tensor_tensor(rows(gs), rows(g1), TAKEN, rows(gs), ALU.mult, ALU.add))
        link(v.tensor_reduce(best, gs, AX.X, ALU.max))
        link(first_of(v, link, gs, best, rank[:, 0:NG], gwork, top, g2))
        link(v.tensor_tensor(g1, g1, g2, ALU.add))
        grouped = tmp.rearrange("p t (g a) -> p (t g) a", g=NG)
        link(v.tensor_tensor(grouped, grouped, rows(g1).unsqueeze(2).to_broadcast([P, n * NG, E1 // NG]), ALU.mult))

    def take():
        link(v.tensor_reduce(best, tmp, AX.X, ALU.max))
        link(first_of(v, link, tmp, best, rank, work, top, pick))
        link(v.scalar_tensor_tensor(rows(tmp), rows(pick), TAKEN, rows(tmp), ALU.mult, ALU.add))

    def weights():
        link(v.scalar_tensor_tensor(rows(work), rows(tmp), TAKEN / 2, rows(score), ALU.is_lt, ALU.mult))
        link(v.tensor_reduce(top, work, AX.X, ALU.add))
        link(v.tensor_scalar(top, top, 1e-20, None, ALU.add))
        link(v.reciprocal(top, top))
        link(v.tensor_tensor(work, work, top.unsqueeze(2).to_broadcast([P, n, E1]), ALU.mult))
        link(v.tensor_scalar(C["weight1"][:, part, :], work, 2.5, C["gate"][:, 3:4], ALU.mult, ALU.mult))

    return [group_scores, two_groups] + [take] * TOP + [weights]


def gated_first(nc, A, C, G):
    N = BLOCK * P
    SHARED = 1
    with ExitStack() as ctx:
        m = Space(nc, ctx, "gfirst")
        sb, ps, sem = m.sb, m.ps, m.sem
        gw = sb("gw", [P, KD, E1])
        mv = sb("mv", [P, B, 2])
        sd, rs = sb("sd", [P, B]), sb("rs", [P, B])
        xn = sb("xn", [P, 2, BLOCK, D])
        xt = sb("xt", [P, KD, N])
        psG = [ps(f"psG{p}", [P, N]) for p in range(2)]
        psU = [ps(f"psU{p}", [P, N]) for p in range(2)]
        psY = ps("psY", [P, BLOCK, D])
        psT = ps("psT", [P, KD, N])
        ins, score_up, step, w_hi, w_lo, var, sd_up, rs_up, xn_up, t_done, t_up, hi, lo, l_done, l_up = (
            sem(n) for n in ("ins", "score_up", "step", "w_hi", "w_lo", "var", "sd_up", "rs_up", "xn_up", "t_done", "t_up", "hi", "lo", "l_done", "l_up"))
        g_done, u_done, s_up, i_up, i_hi, i_lo, y_done, y_up = (
            sem(n) for n in ("g_done", "u_done", "s_up", "i_up", "i_hi", "i_lo", "y_done", "y_up"))
        block = ctx.enter_context(nc.Block())

        @block.sync
        def _(sp):
            sp.dma_start(gw[:], A["gwT"].rearrange("(k p) e -> p k e", p=P)).then_inc(ins, 16)
            G.load(sp, E1, SHARED).then_inc(ins, 16)
            G.load(sp, 0, 1 - SHARED).then_inc(ins, 16)
            sp.dma_start(G.eb[:], A["ebias"].rearrange("(a n) -> a n", a=1).to_broadcast((P, E1))).then_inc(ins, 16)

        @block.gpsimd
        def _(pool):
            def x_low(j):
                pool.wait_ge(hi, j + 1)
                at = slice(j * N, (j + 1) * N)
                nc.gpsimd.tensor_tensor(G.xtl[:, :, at], xt[:], G.xth[:, :, at], ALU.subtract).then_inc(lo, 1)

            nc.gpsimd.iota(G.rank[:], [[-1, E1]], base=E1, channel_multiplier=0, allow_small_or_imprecise_dtypes=True)
            pool.wait_ge(w_hi, 1)
            G.low(SHARED).then_inc(w_lo, 1)
            x_low(0)
            for j in range(BLOCKS):
                if j + 1 < BLOCKS:
                    x_low(j + 1)
                pool.wait_ge(i_hi, j + 1)
                nc.gpsimd.tensor_tensor(G.il[:, j % 2], G.it[:, j % 2], G.ih[:, j % 2], ALU.subtract).then_inc(i_lo, 1)
            pool.wait_ge(w_hi, 2)
            G.low(1 - SHARED).then_inc(w_lo, 1)
            pool.wait_ge(w_lo, 2)

        @block.scalar
        def _(act):
            def x_high(j):
                act.wait_ge(t_done, j + 1)
                if j:
                    act.wait_ge(lo, j)
                    act.wait_ge(l_done, j)
                nc.scalar.activation(xt[:].rearrange("p k t -> p (k t)"), psT[:].rearrange("p k t -> p (k t)"), ACT.Copy).then_inc(t_up, 1)
                act.wait_ge(t_up, j + 1)
                nc.scalar.activation(G.xth[:, :, j * N:(j + 1) * N], xt[:], ACT.Copy).then_inc(hi, 1)

            def logits(j):
                act.wait_ge(l_done, j + 1)
                nc.scalar.activation(rows(C["logits1"][:, j * BLOCK:(j + 1) * BLOCK, :]), psT[:, 0, 0:BLOCK * E1], ACT.Copy).then_inc(l_up, 1)

            act.wait_ge(var, 1)
            nc.scalar.activation(sd[:], mv[:, :, 1], ACT.Sqrt, bias=C["eps"][:]).then_inc(sd_up, 1)
            act.wait_ge(ins, 64)
            G.high(SHARED).then_inc(w_hi, 1)
            x_high(0)
            logits(0)
            for j in range(BLOCKS):
                if j + 1 < BLOCKS:
                    x_high(j + 1)
                act.wait_ge(g_done, j + 1)
                nc.scalar.activation(G.sg[:, j % 2], psG[j % 2][:], ACT.Silu).then_inc(s_up, 1)
                act.wait_ge(i_up, j + 1)
                if j >= 2:
                    act.wait_ge(y_done, j - 1)
                nc.scalar.activation(G.ih[:, j % 2], G.it[:, j % 2], ACT.Copy).then_inc(i_hi, 1)
                if j + 1 < BLOCKS:
                    logits(j + 1)
                if j == BLOCKS // 2 - 1:
                    act.wait_ge(l_up, j + 1)
                    nc.scalar.activation(G.score[:, 0:B // 2, :], C["logits1"][:, 0:B // 2, :], ACT.Sigmoid).then_inc(score_up, 1)
            G.high(1 - SHARED).then_inc(w_hi, 1)

        @block.vector
        def _(dve):
            v = nc.vector
            for b in range(B):
                last = v.bn_aggr(mv[:, b, :], G.stat3[:, b, :])
            last.then_inc(var, 1)
            dve.wait_ge(sd_up, 1)
            v.reciprocal(rs[:], sd[:]).then_inc(rs_up, 1)
            dve.wait_ge(rs_up, 1)

            def norm(j):
                if j >= 2:
                    dve.wait_ge(t_done, j - 1)
                for i in range(BLOCK):
                    b = j * BLOCK + i
                    last = v.tensor_scalar(xn[:, j % 2, i, :], G.acc[:, b, :], mv[:, b, 0:1], rs[:, b:b + 1], ALU.subtract, ALU.mult)
                last.then_inc(xn_up, 1)

            def add(j):
                dve.wait_ge(y_done, j + 1)
                for i in range(BLOCK):
                    a = G.acc[:, j * BLOCK + i, :]
                    last = v.scalar_tensor_tensor(a, psY[:, i, :], C["gate"][:, 3:4], a, ALU.mult, ALU.add)
                last.then_inc(y_up, 1)

            stages = weight_stages(v, Chain(dve, step, 0), C, G, 0)
            norm(0)
            norm(1)
            for j in range(BLOCKS):
                dve.wait_ge(s_up, j + 1)
                dve.wait_ge(u_done, j + 1)
                v.tensor_tensor(G.it[:, j % 2], G.sg[:, j % 2], psU[j % 2][:], ALU.mult).then_inc(i_up, 1)
                if j + 2 < BLOCKS:
                    norm(j + 2)
                if j:
                    add(j - 1)
                if j >= BLOCKS // 2:
                    if j == BLOCKS // 2:
                        dve.wait_ge(score_up, 1)
                        dve.wait_ge(w_lo, 1)
                    for stage in stages[(j - BLOCKS // 2) * 2:(j - BLOCKS // 2) * 2 + 2]:
                        stage()
            add(BLOCKS - 1)

        @block.tensor
        def _(pe):
            pe.wait_ge(ins, 64)

            def turn(j):
                pe.wait_ge(xn_up, j + 1)
                if j:
                    pe.wait_ge(l_up, j)
                for k in range(KD):
                    for i in range(BLOCK):
                        last = nc.tensor.transpose(psT[:, k, i * P:(i + 1) * P], xn[:, j % 2, i, k * P:(k + 1) * P], C["ident"][:])
                last.then_inc(t_done, 1)

            def logits(j):
                pe.wait_ge(t_up, j + 1)
                for i in range(BLOCK):
                    for k in range(KD):
                        last = nc.tensor.matmul(psT[:, 0, i * E1:(i + 1) * E1], xt[:, k, i * P:(i + 1) * P], gw[:, k, :], start=(k == 0), stop=(k == KD - 1))
                last.then_inc(l_done, 1)

            def down(j):
                pe.wait_ge(i_lo, j + 1)
                if j:
                    pe.wait_ge(y_up, j)
                G.down(pe, SHARED, j, psY).then_inc(y_done, 1)

            turn(0)
            logits(0)
            pe.wait_ge(w_lo, 1)
            for j in range(BLOCKS):
                if j + 1 < BLOCKS:
                    turn(j + 1)
                pe.wait_ge(lo, j + 1)
                if j >= 2:
                    pe.wait_ge(i_up, j - 1)
                G.up(pe, SHARED, slice(j * N, (j + 1) * N), psG[j % 2], psU[j % 2], g_done, u_done)
                if j + 1 < BLOCKS:
                    logits(j + 1)
                if j:
                    down(j - 1)
            down(BLOCKS - 1)


def gated(nc, A, C, G, out):
    N = BLOCK * P
    acc = G.acc
    with ExitStack() as ctx:
        m = Space(nc, ctx, "gated")
        ps, sem = m.ps, m.sem
        psG = [ps(f"psG{p}", [P, N]) for p in range(2)]
        psU = [ps(f"psU{p}", [P, N]) for p in range(2)]
        psY = [ps(f"psY{p}", [P, BLOCK, D]) for p in range(2)]
        w_in = [sem(f"w_in{p}") for p in range(2)]
        w_hi, w_lo, g_done, u_done, s_up, i_up, i_hi, i_lo, y_done, y_up, stored = (
            sem(n) for n in ("w_hi", "w_lo", "g_done", "u_done", "s_up", "i_up", "i_hi", "i_lo", "y_done", "y_up", "stored"))
        score_up, step = sem("score_up"), sem("step")
        block = ctx.enter_context(nc.Block())
        out_d = out.rearrange("b p d -> p b d")

        def over(eng, body):
            body(0, 0, 0)
            with eng.Fori(0, E1 // 2 - 1) as h:
                body(h * 2 + 1, 1, h)
                body(h * 2 + 2, 0, h + 1)
            body(E1 - 1, 1, E1 // 2 - 1)

        def last_one(e):
            return isinstance(e, int) and e == E1 - 1

        @block.sync
        def _(sp):
            def load(e, p):
                sp.wait_ge(w_lo, e)
                G.load(sp, e, p).then_inc(w_in[p], 16)

            load(1, 1)
            with sp.Fori(1, E1 // 2) as h:
                load(h * 2, 0)
                load(h * 2 + 1, 1)
            sp.wait_ge(stored, 16 * BLOCKS)

        @block.gpsimd
        def _(pool):
            pool.sem_inc(w_lo, 2)

            def body(e, p, h):
                for j in range(BLOCKS):
                    pool.wait_ge(i_hi, e * BLOCKS + (j + 1))
                    nc.gpsimd.tensor_tensor(G.il[:, j % 2], G.it[:, j % 2], G.ih[:, j % 2], ALU.subtract).then_inc(i_lo, 1)
                    if j == 3 and not last_one(e):
                        pool.wait_ge(w_hi, e + 1)
                        G.low(1 - p).then_inc(w_lo, 1)
            over(pool, body)

        @block.scalar
        def _(act):
            def weights(e, p, h):
                act.wait_ge(w_in[p], h * 16 + 16 * p)
                if not isinstance(e, int) or e >= 2:
                    act.wait_ge(y_done, e * BLOCKS - BLOCKS + 1)
                G.high(p).then_inc(w_hi, 1)

            def body(e, p, h):
                for j in range(BLOCKS):
                    n = e * BLOCKS + j
                    act.wait_ge(g_done, n + 1)
                    nc.scalar.activation(G.sg[:, j % 2], psG[j % 2][:], ACT.Silu).then_inc(s_up, 1)
                    act.wait_ge(i_up, n + 1)
                    nc.scalar.activation(G.ih[:, j % 2], G.it[:, j % 2], ACT.Copy).then_inc(i_hi, 1)
                    if j == 3 and not last_one(e):
                        weights(e + 1, 1 - p, h + p)
                    if last_one(e) and j >= 1:
                        store(j - 1)

            half = slice(B // 2, B)
            nc.scalar.activation(G.score[:, half, :], C["logits1"][:, half, :], ACT.Sigmoid).then_inc(score_up, 1)

            def store(j):
                act.wait_ge(y_up, (E1 - 1) * BLOCKS + j + 1)
                act.dma_start(out_d[:, j * BLOCK:(j + 1) * BLOCK, :], acc[:, j * BLOCK:(j + 1) * BLOCK, :]).then_inc(stored, 16)

            over(act, body)
            store(BLOCKS - 1)

        @block.vector
        def _(dve):
            v = nc.vector
            stages = weight_stages(v, Chain(dve, step, 0), C, G, 1)

            def add(e, j):
                dve.wait_ge(y_done, e * BLOCKS + (j + 2))
                for i in range(BLOCK):
                    a = acc[:, j * BLOCK + i, :]
                    last = v.scalar_tensor_tensor(a, psY[j % 2][:, i, :], C["weight1"][:, j * BLOCK + i, bass.ds(e, 1)], a, ALU.mult, ALU.add)
                last.then_inc(y_up, 1)

            def body(e, p, h):
                for j in range(BLOCKS):
                    dve.wait_ge(s_up, e * BLOCKS + (j + 1))
                    dve.wait_ge(u_done, e * BLOCKS + (j + 1))
                    v.tensor_tensor(G.it[:, j % 2], G.sg[:, j % 2], psU[j % 2][:], ALU.mult).then_inc(i_up, 1)
                    if isinstance(e, int) and e == 0 and j < BLOCKS // 2:
                        if j == 0:
                            dve.wait_ge(score_up, 1)
                        for stage in stages[j * 2:j * 2 + 2]:
                            stage()
                    if j:
                        add(e, j - 1)
                    elif not isinstance(e, int) or e >= 1:
                        add(e - 1, BLOCKS - 1)
            over(dve, body)
            add(E1 - 1, BLOCKS - 1)

        @block.tensor
        def _(pe):
            pe.sem_inc(y_done, 1)

            def up(e, p, j):
                n = e * BLOCKS + j
                if not isinstance(n, int) or n >= 2:
                    pe.wait_ge(i_up, n - 1)
                if j == 0:
                    pe.wait_ge(w_lo, e + 2)
                G.up(pe, p, slice(j * N, (j + 1) * N), psG[j % 2], psU[j % 2], g_done, u_done)

            def down(e, p, j):
                n = e * BLOCKS + j
                pe.wait_ge(i_lo, n + 1)
                if not isinstance(n, int) or n >= 2:
                    pe.wait_ge(y_up, n - 1)
                G.down(pe, p, j, psY[j % 2]).then_inc(y_done, 1)

            def body(e, p, h):
                for j in range(BLOCKS):
                    up(e, p, j)
                    if j:
                        down(e, p, j - 1)
                    elif not isinstance(e, int) or e >= 1:
                        down(e - 1, 1 - p, BLOCKS - 1)
            over(pe, body)
            down(E1 - 1, 1, BLOCKS - 1)


def gated_mix__experts__attend__gated_experts(nc, A, out):
    X2, XN = (nc.dram_tensor(n, (ROWS, D), F32, kind="Internal").ap() for n in ("x2_rows", "xn_rows"))
    VB = nc.dram_tensor("bias_by_distance", (HEADS, P, 2 * P), F32, kind="Internal").ap()
    with ExitStack() as ctx:
        m = Space(nc, ctx, "const")
        C = {n: m.sb(n, [P, P]) for n in ("ident", "ones", "tri", "gsum")}
        C["gate"] = m.sb("gate", [P, 4])
        C["eps"] = m.sb("eps", [P, 1])
        C["stood"] = m.sem("stood")
        setup(nc, A, C)
        held = AttendHeld(nc, ctx, A, VB)
        with ExitStack() as layer:
            m0 = Space(nc, layer, "layer0")
            C["logits0"] = m0.sb("logits0", [P, B, E0])
            C["slot_row"] = m0.sb("slot_row", [SLOTS, E0, PARTS], I32)
            C["slot_weight"] = m0.sb("slot_weight", [SLOTS, E0, PARTS])
            mix(nc, A, C, X2, XN)
            raw = m0.sb("raw", [P, 2, KD * F0])
            route(nc, A, C, held, raw)
            experts(nc, A, C, X2, XN, raw)
        acc = m.sb("acc", [P, B, D])
        stat3 = m.sb("stat3", [P, B, 6])
        attend(nc, A, C, held, X2, acc, stat3)
        C["logits1"] = m.sb("logits1", [P, B, E1])
        C["weight1"] = m.sb("weight1", [P, B, E1])
        G = GatedHeld(nc, ctx, A, held, acc, stat3)
        gated_first(nc, A, C, G)
        gated(nc, A, C, G, out)


def layouts(i):
    def blocks(w):
        return w.transpose(0, 2, 1).reshape(E1 + 1, KD, P, I1).transpose(0, 2, 1, 3)

    def with_shared(name, shared):
        return np.concatenate([np.asarray(i[name]), np.asarray(i[shared])[None]])

    gate = with_shared("L1_ffn_gate_proj", "L1_ffn_shared_gate_w")
    up = with_shared("L1_ffn_up_proj", "L1_ffn_shared_up_w")
    down = with_shared("L1_ffn_down_proj", "L1_ffn_shared_down_w")
    down = down.transpose(0, 2, 1).reshape(E1 + 1, I1, KD, P)
    arrays = {
        "x": i["x"], "ctx_1024": i["ctx_1024"], "g_xattn": i["g_xattn"], "g_ffn": i["g_ffn"],
        "Wt": i["L0_xattn_Wt"], "WpT": np.asarray(i["L0_xattn_Wp"]).T, "WgT": np.asarray(i["L0_xattn_Wg"]).T,
        "WzT": np.asarray(i["L0_xattn_Wz"]).transpose(0, 2, 1).reshape(GROUPS * GROUP, GROUP),
        "gamma": i["L0_xattn_gamma"], "beta": i["L0_xattn_beta"],
        "wr": i["L0_ffn_w_router"], "wi": i["L0_ffn_wi"], "wo": i["L0_ffn_wo"],
        "Wq": i["L1_xattn_Wq"], "Wk": i["L1_xattn_Wk"], "Wv": i["L1_xattn_Wv"], "Wo": i["L1_xattn_Wo"],
        "relT": np.asarray(i["L1_xattn_rel_bias"]).T, "hot": bucket_onehot(),
        "mask": np.asarray(i["mask_1x1xSxS2_bk0"]).reshape(S, S),
        "gwT": np.asarray(i["L1_ffn_gate_w"]).T, "ebias": i["L1_ffn_e_bias"],
        "gex": np.stack([blocks(gate), blocks(up), down], 2).reshape(E1 + 1, P, 3 * KD * I1),
    }
    return {n: np.ascontiguousarray(a) for n, a in arrays.items()}


def kernel(**inputs):
    import concourse.bacc as bacc
    from concourse.bass_utils import run_bass_kernel_spmd

    nc = bacc.Bacc("TRN2", target_bir_lowering=False, num_devices=1)
    laid = layouts(inputs)
    A = {n: nc.dram_tensor(f"in_{n}_dram", a.shape, mybir.dt.from_np(a.dtype), kind="ExternalInput").ap() for n, a in laid.items()}
    out = nc.dram_tensor("out_0_dram", (B, S, D), F32, kind="ExternalOutput").ap()
    gated_mix__experts__attend__gated_experts(nc, A, out)
    r = run_bass_kernel_spmd(nc, [{f"in_{n}_dram": a for n, a in laid.items()}], core_ids=[0])
    return r.results[0]["out_0_dram"]
```
